# Optimizing a Trainium2 kernel written in Bass

```python
import numpy as np
import jax
import jax.numpy as jnp

def _softmax(x, axis=-1):
    return jax.nn.softmax(x, axis=axis)

def _gelu(x):
    return jax.nn.gelu(x, approximate=True)

def _silu(x):
    return jax.nn.silu(x)

def _sigmoid(x):
    return jax.nn.sigmoid(x)

def _layernorm(x, axis=-1, eps=1e-05):
    m = jnp.mean(x, axis=axis, keepdims=True)
    v = jnp.var(x, axis=axis, keepdims=True)
    return (x - m) / jnp.sqrt(v + eps)

def _scatter_add(tgt, idx, src, axis=0):
    return tgt.at[idx].add(src)

def _segment_sum(src, seg, n):
    return jax.ops.segment_sum(src, seg, n)
kernel_name = 'mk_perceiver_d1_seqx_r4_cbc874'

def setup_inputs(seed: int=0):
    np.random.seed(seed)
    _w = jnp.asarray

    def _rec_inputs():
        import jax
        import jax.numpy as jnp
        _rk = jax.random.key(seed)
        x = -0.0005146 + 1 * jax.random.normal(jax.random.fold_in(_rk, 1), (1, 256, 256), jnp.float32)
        _lenS = 256 - jax.random.randint(jax.random.fold_in(_rk, 7), (1,), 0, max(1, 256 // 4) + 1, jnp.int32)
        _lenS2 = 4096 - jax.random.randint(jax.random.fold_in(_rk, 8), (1,), 0, max(1, 4096 // 4) + 1, jnp.int32)
        _ctx_1024P = jax.random.normal(jax.random.fold_in(_rk, 11), (1, 16, 256), jnp.float32)
        _ctx_1024c = jax.random.dirichlet(jax.random.fold_in(_rk, 511), 0.3 * jnp.ones((16,), jnp.float32), (1, 4096))
        _ctx_1024t = jnp.einsum('bsk,bkd->bsd', _ctx_1024c, _ctx_1024P)
        _ctx_1024t = _ctx_1024t * jax.lax.rsqrt(jnp.mean(jnp.square(_ctx_1024t)) + 1e-12) * 0.953939
        ctx_1024 = -0.000392918 + 0.999932 * (_ctx_1024t + 0.3 * jax.random.normal(jax.random.fold_in(_rk, 611), (1, 4096, 256), jnp.float32))
        _validS = jnp.arange(256)[None, :] < _lenS[:, None]
        _validS2 = jnp.arange(4096)[None, :] < _lenS2[:, None]
        _causal = jnp.tril(jnp.ones((256, 256), dtype=bool))
        mask_BxS2_bf1 = jnp.ones((1, 4096), dtype=bool)
        return (x, ctx_1024, mask_BxS2_bf1)
    x, ctx_1024, mask_BxS2_bf1 = _rec_inputs()

    def _L0_xattn_setup():
        import jax, jax.numpy as jnp
        import numpy as np
        DIM = 256
        DIM_LATENT = 256
        DIM_HEAD = 64
        HEADS = 16
        INNER = HEADS * DIM_HEAD

        def layernorm(x, g, b, eps=1e-05):
            m = jnp.mean(x, axis=-1, keepdims=True)
            v = jnp.mean((x - m) ** 2, axis=-1, keepdims=True)
            return (x - m) / jnp.sqrt(v + eps) * g + b

        def rmsnorm(x, gamma, eps=1e-08):
            n = jnp.linalg.norm(x, axis=-1, keepdims=True) * x.shape[-1] ** (-0.5)
            return x / jnp.maximum(n, eps) * gamma
        key = jax.random.key(seed)
        ks = jax.random.split(key, 8)
        b, n, m = (4, 1024, 128)
        x = jax.random.normal(ks[0], (b, n, DIM), dtype=jnp.float32)
        latents = jax.random.normal(ks[1], (b, m, DIM_LATENT), dtype=jnp.float32)
        mask = jnp.ones((b, n), dtype=bool)
        s = 0.02
        return {'x': x, 'latents': latents, 'mask': mask, 'ln_x_g': jnp.ones((DIM,), jnp.float32), 'ln_x_b': jnp.zeros((DIM,), jnp.float32), 'ln_l_g': jnp.ones((DIM_LATENT,), jnp.float32), 'ln_l_b': jnp.zeros((DIM_LATENT,), jnp.float32), 'qn_g': jnp.ones((DIM_HEAD,), jnp.float32), 'kn_g': jnp.ones((DIM_HEAD,), jnp.float32), 'Wq': jax.random.normal(ks[2], (DIM_LATENT, INNER), jnp.float32) * s, 'Wkv': jax.random.normal(ks[3], (DIM, 2 * INNER), jnp.float32) * s, 'Wout': jax.random.normal(ks[4], (INNER, DIM_LATENT), jnp.float32) * s, 'bout': jnp.zeros((DIM_LATENT,), jnp.float32)}
    _L0_xattn_all = _L0_xattn_setup()
    _L0_xattn_in = {k: v for k, v in _L0_xattn_all.items() if k in ('ln_x_g', 'ln_x_b', 'ln_l_g', 'ln_l_b', 'qn_g', 'kn_g', 'Wq', 'Wkv', 'Wout', 'bout')}
    del _L0_xattn_all

    def _L0_attn_setup():
        import jax, jax.numpy as jnp
        import numpy as np
        B, N, D, H = (4, 1024, 256, 16)
        DH = D // H
        M = int(DH * np.log(DH))
        EPS = 0.0001

        def softmax_kernel(t, proj, is_query):
            dn = t.shape[-1] ** (-0.25)
            ratio = proj.shape[0] ** (-0.5)
            td = jnp.einsum('bhnd,md->bhnm', t * dn, proj)
            diag = 0.5 * dn ** 2 * jnp.sum(t * t, axis=-1, keepdims=True)
            if is_query:
                mx = jnp.max(td, axis=-1, keepdims=True)
            else:
                mx = jnp.max(td, axis=(-1, -2), keepdims=True)
            return ratio * (jnp.exp(td - diag - mx) + EPS)
        key = jax.random.key(seed)
        ks = jax.random.split(key, 12)
        s = 0.02
        inp = {'x': jax.random.normal(ks[0], (B, N, D), jnp.float32), 'Wq': jax.random.normal(ks[1], (D, D), jnp.float32) * s, 'bq': jnp.zeros((D,), jnp.float32), 'Wk': jax.random.normal(ks[2], (D, D), jnp.float32) * s, 'bk': jnp.zeros((D,), jnp.float32), 'Wv': jax.random.normal(ks[3], (D, D), jnp.float32) * s, 'bv': jnp.zeros((D,), jnp.float32), 'Wo': jax.random.normal(ks[4], (D, D), jnp.float32) * s, 'bo': jnp.zeros((D,), jnp.float32), 'Wfc': jax.random.normal(ks[5], (D, D), jnp.float32) * s, 'bfc': jnp.zeros((D,), jnp.float32), 'proj': jax.random.normal(ks[6], (M, DH), jnp.float32)}
        return inp
    _L0_attn_all = _L0_attn_setup()
    _L0_attn_in = {k: v for k, v in _L0_attn_all.items() if k in ('Wq', 'bq', 'Wk', 'bk', 'Wv', 'bv', 'Wo', 'bo', 'Wfc', 'bfc', 'proj')}
    del _L0_attn_all

    def _L0_ffn_setup():
        import jax, jax.numpy as jnp
        import numpy as np
        B, S, H = (2, 512, 256)
        F = 1024
        E = 8
        TOP_K = 2
        SHARED_SCALE = 0.1
        EPS = 1e-09

        def _moe_forward(x3, Wg, W1, b1, W2, b2, Ws1, bs1, Ws2, bs2):
            b, s, h = x3.shape
            x = x3.reshape(-1, h)
            T = x.shape[0]
            logits = x @ Wg
            probs = jax.nn.softmax(logits, axis=-1)
            vals, idx = jax.lax.top_k(probs, TOP_K)
            weights = vals / (jnp.sum(vals, axis=-1, keepdims=True) + EPS)
            cw = jnp.zeros((T, E), dtype=x.dtype).at[jnp.arange(T)[:, None], idx].set(weights)
            hpre = jnp.einsum('th,ehf->tef', x, W1) + b1
            act = jax.nn.silu(hpre)
            y = jnp.einsum('tef,efh->teh', act, W2) + b2
            out = jnp.einsum('te,teh->th', cw, y)
            shared = jax.nn.silu(x @ Ws1 + bs1) @ Ws2 + bs2
            out = out + SHARED_SCALE * shared
            return out.reshape(b, s, h)
        key = jax.random.key(seed)
        ks = jax.random.split(key, 10)
        sc = 0.02
        return {'hidden_states': jax.random.normal(ks[0], (B, S, H), dtype=jnp.float32), 'Wg': jax.random.normal(ks[1], (H, E), dtype=jnp.float32) * sc, 'W1': jax.random.normal(ks[2], (E, H, F), dtype=jnp.float32) * sc, 'b1': jnp.zeros((E, F), dtype=jnp.float32), 'W2': jax.random.normal(ks[3], (E, F, H), dtype=jnp.float32) * sc, 'b2': jnp.zeros((E, H), dtype=jnp.float32), 'Ws1': jax.random.normal(ks[4], (H, F), dtype=jnp.float32) * sc, 'bs1': jnp.zeros((F,), dtype=jnp.float32), 'Ws2': jax.random.normal(ks[5], (F, H), dtype=jnp.float32) * sc, 'bs2': jnp.zeros((H,), dtype=jnp.float32)}
    _L0_ffn_all = _L0_ffn_setup()
    _L0_ffn_in = {k: v for k, v in _L0_ffn_all.items() if k in ('Wg', 'W1', 'b1', 'W2', 'b2', 'Ws1', 'bs1', 'Ws2', 'bs2')}
    del _L0_ffn_all
    return {'x': x, 'ctx_1024': ctx_1024, 'mask_BxS2_bf1': mask_BxS2_bf1, 'L0_xattn_ln_x_g': _L0_xattn_in['ln_x_g'], 'L0_xattn_ln_x_b': _L0_xattn_in['ln_x_b'], 'L0_xattn_ln_l_g': _L0_xattn_in['ln_l_g'], 'L0_xattn_ln_l_b': _L0_xattn_in['ln_l_b'], 'L0_xattn_qn_g': _L0_xattn_in['qn_g'], 'L0_xattn_kn_g': _L0_xattn_in['kn_g'], 'L0_xattn_Wq': _L0_xattn_in['Wq'], 'L0_xattn_Wkv': _L0_xattn_in['Wkv'], 'L0_xattn_Wout': _L0_xattn_in['Wout'], 'L0_xattn_bout': _L0_xattn_in['bout'], 'L0_attn_Wq': _L0_attn_in['Wq'], 'L0_attn_bq': _L0_attn_in['bq'], 'L0_attn_Wk': _L0_attn_in['Wk'], 'L0_attn_bk': _L0_attn_in['bk'], 'L0_attn_Wv': _L0_attn_in['Wv'], 'L0_attn_bv': _L0_attn_in['bv'], 'L0_attn_Wo': _L0_attn_in['Wo'], 'L0_attn_bo': _L0_attn_in['bo'], 'L0_attn_Wfc': _L0_attn_in['Wfc'], 'L0_attn_bfc': _L0_attn_in['bfc'], 'L0_attn_proj': _L0_attn_in['proj'], 'L0_ffn_Wg': _L0_ffn_in['Wg'], 'L0_ffn_W1': _L0_ffn_in['W1'], 'L0_ffn_b1': _L0_ffn_in['b1'], 'L0_ffn_W2': _L0_ffn_in['W2'], 'L0_ffn_b2': _L0_ffn_in['b2'], 'L0_ffn_Ws1': _L0_ffn_in['Ws1'], 'L0_ffn_bs1': _L0_ffn_in['bs1'], 'L0_ffn_Ws2': _L0_ffn_in['Ws2'], 'L0_ffn_bs2': _L0_ffn_in['bs2']}

def reference(x, ctx_1024, mask_BxS2_bf1, L0_xattn_ln_x_g, L0_xattn_ln_x_b, L0_xattn_ln_l_g, L0_xattn_ln_l_b, L0_xattn_qn_g, L0_xattn_kn_g, L0_xattn_Wq, L0_xattn_Wkv, L0_xattn_Wout, L0_xattn_bout, L0_attn_Wq, L0_attn_bq, L0_attn_Wk, L0_attn_bk, L0_attn_Wv, L0_attn_bv, L0_attn_Wo, L0_attn_bo, L0_attn_Wfc, L0_attn_bfc, L0_attn_proj, L0_ffn_Wg, L0_ffn_W1, L0_ffn_b1, L0_ffn_W2, L0_ffn_b2, L0_ffn_Ws1, L0_ffn_bs1, L0_ffn_Ws2, L0_ffn_bs2):
    import jax
    import jax.numpy as jnp

    def _L0_xattn_ref(x, latents, mask, ln_x_g, ln_x_b, ln_l_g, ln_l_b, qn_g, kn_g, Wq, Wkv, Wout, bout):
        import jax, jax.numpy as jnp
        import numpy as np
        DIM = 256
        DIM_LATENT = 256
        DIM_HEAD = 64
        HEADS = 16
        INNER = HEADS * DIM_HEAD

        def layernorm(x, g, b, eps=1e-05):
            m = jnp.mean(x, axis=-1, keepdims=True)
            v = jnp.mean((x - m) ** 2, axis=-1, keepdims=True)
            return (x - m) / jnp.sqrt(v + eps) * g + b

        def rmsnorm(x, gamma, eps=1e-08):
            n = jnp.linalg.norm(x, axis=-1, keepdims=True) * x.shape[-1] ** (-0.5)
            return x / jnp.maximum(n, eps) * gamma
        b, n, _ = x.shape
        m = latents.shape[1]
        h, d = (HEADS, DIM_HEAD)
        scale = d ** (-0.5)
        xn = layernorm(x, ln_x_g, ln_x_b)
        ln = layernorm(latents, ln_l_g, ln_l_b)
        q = (ln @ Wq).reshape(b, m, h, d).transpose(0, 2, 1, 3)
        kv = jnp.concatenate([xn @ Wkv, ln @ Wkv], axis=1)
        kv = kv.reshape(b, n + m, 2, h, d)
        k = kv[:, :, 0].transpose(0, 2, 1, 3)
        v = kv[:, :, 1].transpose(0, 2, 1, 3)
        qn = rmsnorm(q, qn_g) * scale
        kn = rmsnorm(k, kn_g)
        sim = jnp.einsum('bhid,bhjd->bhij', qn, kn)
        max_neg = -jnp.finfo(sim.dtype).max
        padded_mask = jnp.concatenate([mask, jnp.ones((b, m), bool)], axis=1)
        sim = jnp.where(padded_mask[:, None, None, :], sim, max_neg)
        attn = jax.nn.softmax(sim.astype(jnp.float32), axis=-1).astype(sim.dtype)
        out = jnp.einsum('bhij,bhjd->bhid', attn, v)
        out = out.transpose(0, 2, 1, 3).reshape(b, m, h * d)
        return out @ Wout + bout

    def _L0_attn_ref(x, Wq, bq, Wk, bk, Wv, bv, Wo, bo, Wfc, bfc, proj):
        import jax, jax.numpy as jnp
        import numpy as np
        B, N, D, H = (4, 1024, 256, 16)
        DH = D // H
        M = int(DH * np.log(DH))
        EPS = 0.0001

        def softmax_kernel(t, proj, is_query):
            dn = t.shape[-1] ** (-0.25)
            ratio = proj.shape[0] ** (-0.5)
            td = jnp.einsum('bhnd,md->bhnm', t * dn, proj)
            diag = 0.5 * dn ** 2 * jnp.sum(t * t, axis=-1, keepdims=True)
            if is_query:
                mx = jnp.max(td, axis=-1, keepdims=True)
            else:
                mx = jnp.max(td, axis=(-1, -2), keepdims=True)
            return ratio * (jnp.exp(td - diag - mx) + EPS)
        b, n, d = x.shape

        def heads(t):
            return t.reshape(b, n, H, DH).transpose(0, 2, 1, 3)
        q = heads(x @ Wq.T + bq)
        k = heads(x @ Wk.T + bk)
        v = heads(x @ Wv.T + bv)
        qp = softmax_kernel(q, proj, is_query=True)
        kp = softmax_kernel(k, proj, is_query=False)
        k_sum = jnp.sum(kp, axis=-2)
        d_inv = 1.0 / jnp.einsum('bhnm,bhm->bhn', qp, k_sum)
        context = jnp.einsum('bhnm,bhnd->bhmd', kp, v)
        out = jnp.einsum('bhmd,bhnm,bhn->bhnd', context, qp, d_inv)
        out = out.transpose(0, 2, 1, 3).reshape(b, n, d)
        h = out @ Wo.T + bo
        return jax.nn.relu(h @ Wfc.T + bfc)

    def _L0_ffn_ref(hidden_states, Wg, W1, b1, W2, b2, Ws1, bs1, Ws2, bs2):
        import jax, jax.numpy as jnp
        import numpy as np
        B, S, H = (2, 512, 256)
        F = 1024
        E = 8
        TOP_K = 2
        SHARED_SCALE = 0.1
        EPS = 1e-09

        def _moe_forward(x3, Wg, W1, b1, W2, b2, Ws1, bs1, Ws2, bs2):
            b, s, h = x3.shape
            x = x3.reshape(-1, h)
            T = x.shape[0]
            logits = x @ Wg
            probs = jax.nn.softmax(logits, axis=-1)
            vals, idx = jax.lax.top_k(probs, TOP_K)
            weights = vals / (jnp.sum(vals, axis=-1, keepdims=True) + EPS)
            cw = jnp.zeros((T, E), dtype=x.dtype).at[jnp.arange(T)[:, None], idx].set(weights)
            hpre = jnp.einsum('th,ehf->tef', x, W1) + b1
            act = jax.nn.silu(hpre)
            y = jnp.einsum('tef,efh->teh', act, W2) + b2
            out = jnp.einsum('te,teh->th', cw, y)
            shared = jax.nn.silu(x @ Ws1 + bs1) @ Ws2 + bs2
            out = out + SHARED_SCALE * shared
            return out.reshape(b, s, h)
        return _moe_forward(hidden_states, Wg, W1, b1, W2, b2, Ws1, bs1, Ws2, bs2)
    x = x + _L0_xattn_ref(ctx_1024, _layernorm(x, axis=-1), mask_BxS2_bf1, L0_xattn_ln_x_g, L0_xattn_ln_x_b, L0_xattn_ln_l_g, L0_xattn_ln_l_b, L0_xattn_qn_g, L0_xattn_kn_g, L0_xattn_Wq, L0_xattn_Wkv, L0_xattn_Wout, L0_xattn_bout)
    x = x + _L0_attn_ref(_layernorm(x, axis=-1), L0_attn_Wq, L0_attn_bq, L0_attn_Wk, L0_attn_bk, L0_attn_Wv, L0_attn_bv, L0_attn_Wo, L0_attn_bo, L0_attn_Wfc, L0_attn_bfc, L0_attn_proj)
    x = x + _L0_ffn_ref(_layernorm(x, axis=-1), L0_ffn_Wg, L0_ffn_W1, L0_ffn_b1, L0_ffn_W2, L0_ffn_b2, L0_ffn_Ws1, L0_ffn_bs1, L0_ffn_Ws2, L0_ffn_bs2)
    return x

_drawn_inputs = setup_inputs


def setup_inputs(seed=0):
    import zlib

    import numpy as np

    out = dict(_drawn_inputs(seed))
    spreads = {'L0_xattn_ln_x_g': (1.0, 0.6),
     'L0_xattn_ln_x_b': (0.0, 0.331),
     'L0_xattn_ln_l_g': (1.0, 0.6),
     'L0_xattn_ln_l_b': (0.0, 0.8),
     'L0_xattn_qn_g': (1.0, 0.6),
     'L0_xattn_kn_g': (1.0, 0.6),
     'L0_xattn_bout': (0.0, 0.1),
     'L0_attn_bq': (0.0, 2.0),
     'L0_attn_bk': (0.0, 2.0),
     'L0_attn_bv': (0.0, 0.581),
     'L0_attn_bo': (0.0, 0.328),
     'L0_attn_bfc': (0.0, 0.1),
     'L0_ffn_b1': (0.0, 0.324),
     'L0_ffn_b2': (0.0, 0.1),
     'L0_ffn_bs1': (0.0, 0.8),
     'L0_ffn_bs2': (0.0, 0.793)}
    factors = {'L0_attn_Wq': 64.0,
     'L0_attn_Wk': 64.0,
     'L0_attn_Wv': 8.0,
     'L0_attn_Wo': 4.703,
     'L0_attn_proj': 64.0,
     'L0_ffn_Ws1': 5.52,
     'L0_ffn_Ws2': 5.255}
    for name, (base, spread) in spreads.items():
        noise = np.random.default_rng([zlib.crc32(name.encode()), seed]).standard_normal(out[name].shape)
        drawn = base * np.exp(spread * noise) if base else spread * noise
        out[name] = jnp.asarray(drawn.astype(out[name].dtype))
    for name, factor in factors.items():
        out[name] = (out[name] * factor).astype(out[name].dtype)
    return out
```

```python
from contextlib import ExitStack

import concourse.bass as bass
from concourse import mybir

ALU = mybir.AluOpType
ACT = mybir.ActivationFunctionType
AX_X = mybir.AxisListType.X
F32 = mybir.dt.float32
F32R = mybir.dt.float32r
U32 = mybir.dt.uint32

P = 128
D = 256
KD = D // P
NQ = 256
QT = NQ // P
NCTX = 4096
CT = NCTX // P
NT = CT + QT
H = 16
DH = 64
INNER = H * DH
HQ = 4
NQUAD = H // HQ
QW = HQ * DH
NTILES = NQUAD * NT
GT = 4
NG = CT // GT
LN_EPS = 1e-5
RMS_FLOOR = 1e-8
EXP_ROOM = 70.0

DHP = 16
M = 44
PAIR = 2 * M
NPAIR = H // 2
VW = DHP + 1
FEAT_EPS = 1e-4

E = 8
F = 1024
FT = F // P
SHARED = 0.1
TOP_EPS = 1e-9
NORM_LINKS = 2


class Turn:

    def __init__(self, c, per, i=None):
        self.c, self.per, self.i = c, per, i

    def __add__(self, k):
        return Turn(self.c + k, self.per, self.i)

    @property
    def n(self):
        return self.c if self.i is None else self.i * self.per + self.c

    @property
    def slot(self):
        return self.c % self.per

    @property
    def lap(self):
        return self.c // self.per if self.i is None else self.i + self.c // self.per


def run(eng, body, first, end, per):
    turns = (end - first) // per
    if turns > 1:
        with eng.Fori(0, turns) as i:
            for c in range(per):
                body(Turn(first + c, per, i))
        first += turns * per
    for c in range(first, end):
        body(Turn(c, per))


def perceiver_kernel(nc, a, out, only_attention=False):
    xn_dram = nc.dram_tensor("xn_parts", (NT, P, KD * 2 * P), F32).ap()

    with ExitStack() as outer:
        def sem(name):
            return outer.enter_context(nc.semaphore(name))

        def keep(name, shape, dt=F32):
            return outer.enter_context(nc.sbuf_tensor(name, shape, dt))

        x_res = keep("x_res", [P, QT, D])
        ident = keep("ident", [P, P])
        ones = keep("ones", [P, P])
        neg_half = keep("neg_half", [P, QT * H])

        with ExitStack() as scope:
            def stay(name, shape, dt=F32):
                return scope.enter_context(nc.sbuf_tensor(name, shape, dt))

            attn_out = stay("attn_out", [P, NQUAD, HQ * NQ])
            weight_sum = stay("weight_sum", [P, NQUAD, HQ * NQ])
            with ExitStack() as inner:
                def hold(name, shape, dt=F32):
                    return inner.enter_context(nc.sbuf_tensor(name, shape, dt))

                wkv = hold("wkv", [P, NQUAD, KD, 2, 2 * QW], F32R)
                q_parts = hold("q_parts", [P, H, 2, NQ], F32R)
                score_bias = hold("score_bias", [P, NT])
                queries(nc, sem, a, xn_dram, x_res, ident, ones, neg_half, q_parts, score_bias)
                context(nc, sem, a, xn_dram, ident, neg_half, wkv, weight_sum)
                attention(nc, sem, xn_dram, ident, neg_half, wkv, q_parts, score_bias, attn_out, weight_sum)
            attention_output(nc, sem, a, x_res, ones, attn_out, weight_sum)
        if not only_attention:
            performer(nc, sem, a, x_res, ident, neg_half)
            experts(nc, sem, a, x_res, ident, neg_half)
        store_result(nc, sem, out, x_res)


def queries(nc, sem, a, xn_dram, x_res, ident, ones, neg_half, q_parts, score_bias):
    with ExitStack() as ctx:
        def sb(name, shape, dt=F32):
            return ctx.enter_context(nc.sbuf_tensor(name, shape, dt))

        stats = sb("q_stats", [P, 2, QT, 6])
        mean_var = sb("q_mean_var", [P, 2, QT, 2])
        var_eps = sb("q_var_eps", [P, 2, QT])
        rstd = sb("q_rstd", [P, 2, QT])
        z = sb("q_z", [P, 2, QT, D])
        u = sb("q_u", [P, KD, QT, P])
        parts = sb("q_xparts", [P, QT, KD, 2, P], F32R)
        gains = sb("q_gains", [P, 2, KD])
        gq = sb("gq", [P, 2, DH])
        gqk = sb("gqk", [P, DH])
        bound = sb("bound", [P, DH + 2])
        mask_raw = sb("mask_raw", [P, CT], mybir.dt.uint8)
        mask_f = sb("mask_f", [P, CT])
        wq_raw = sb("wq_raw", [P, KD, INNER])
        wq = sb("wq", [P, KD, 2, INNER], F32R)
        q_sq = sb("q_sq", [P, QT * H, DH])
        q_ss = sb("q_ss", [P, QT * H])
        q_rms = sb("q_rms", [P, QT * H])
        qn = sb("qn", [P, QT * H, DH])
        q_dup = sb("q_dup", [P, QT * H, 2, 2, DH])
        xt_ps = ctx.enter_context(nc.psum_tensor("q_xt_ps", [P, KD, 512], F32))
        q_ps = ctx.enter_context(nc.psum_tensor("q_ps", [P, QT * INNER], F32))

        x_in, gains_in, gqk_in, mask_in, wq_in = sem("x_in"), sem("q_gains_in"), sem("gqk_in"), sem("mask_in"), sem("wq_in")
        pool_const, ident_zeroed, ident_done = sem("pool_const"), sem("ident_zeroed"), sem("ident_done")
        eps_done, root_done = sem("q_eps_done"), sem("q_root_done")
        dve_own = sem("q_dve_own")
        z_done, xt_done, u_done, parts_done, parts_out = (
            sem("q_z_done"), sem("q_xt_done"), sem("q_u_done"), sem("q_parts_done"), sem("q_parts_out"))
        wq_hi, wq_lo = sem("wq_hi"), sem("wq_lo")
        q_done, sq_done, ss_done, rms_done = sem("q_done"), sem("q_sq_done"), sem("q_ss_done"), sem("q_rms_done")
        dup_done, qt_done, qt_odd, qt_even = sem("q_dup_done"), sem("qt_done"), sem("qt_odd"), sem("qt_even")

        block = ctx.enter_context(nc.Block())

        @block.sync
        def _(sp):
            sp.dma_start(x_res[:], a["x"].rearrange("o (j p) d -> p (o j) d", p=P)).then_inc(x_in, 16)
            sp.dma_start(wq_raw[:], a["L0_xattn_Wq"].rearrange("(k p) n -> p k n", p=P)).then_inc(wq_in, 16)
            sp.wait_ge(parts_done, 1)
            sp.dma_start(xn_dram[CT:NT, :, :].rearrange("t p n -> p t n"),
                         parts[:].bitcast(F32).rearrange("p t k s n -> p t (k s n)")).then_inc(parts_out, 16)
            sp.wait_ge(parts_out, 16)

        @block.gpsimd
        def _(pool):
            nc.gpsimd.memset(ident[:], 0.0).then_inc(ident_zeroed, 1)
            nc.gpsimd.memset(neg_half[:], -0.5).then_inc(pool_const, 1)
            nc.gpsimd.memset(ones[:], 1.0).then_inc(pool_const, 1)
            pool.wait_ge(ident_zeroed, 1)
            nc.gpsimd.affine_select(out=ident[:], in_=ident[:], compare_op=ALU.not_equal, fill=1.0,
                                    base=0, pattern=[[-1, P]], channel_multiplier=1).then_inc(ident_done, 1)
            pool.wait_ge(pool_const, 2)
            for n in range(2):
                pool.wait_ge(eps_done, n + 1)
                nc.gpsimd.tensor_tensor(rstd[:, n, :], var_eps[:, n, :], neg_half[:, 0:QT], ALU.pow).then_inc(root_done, 1)
            pool.wait_ge(ss_done, 1)
            nc.gpsimd.tensor_tensor(q_rms[:], q_ss[:], neg_half[:], ALU.pow).then_inc(rms_done, 1)

        @block.scalar
        def _(act):
            with nc.allow_non_contiguous_dma(reason="a vector onto partitions"):
                for n, name in enumerate(("ln_l_g", "ln_l_b")):
                    act.dma_start(gains[:, n, :], a["L0_xattn_" + name].rearrange("(k p) -> p k", p=P)).then_inc(gains_in, 16)
            for n, name in enumerate(("qn_g", "kn_g")):
                act.dma_start(gq[:, n, :], a["L0_xattn_" + name].partition_broadcast(P)).then_inc(gqk_in, 16)
            act.dma_start(mask_raw[:], a["mask_BxS2_bf1"]).then_inc(mask_in, 16)
            act.wait_ge(wq_in, 16)
            nc.scalar.activation(wq[:, :, 0, :], wq_raw[:], ACT.Copy).then_inc(wq_hi, 1)
            act.wait_ge(gains_in, 32)
            act.wait_ge(xt_done, 1)
            for k in range(KD):
                last = nc.scalar.activation(u[:, k], xt_ps[:, k, 0:QT * P], ACT.Identity,
                                            scale=gains[:, 0, k:k + 1], bias=gains[:, 1, k:k + 1])
            last.then_inc(u_done, 1)
            act.wait_ge(q_done, 1)
            nc.scalar.activation(q_sq[:].rearrange("p h d -> p (h d)"), q_ps[:], ACT.Square,
                                 scale=DH ** -0.5).then_inc(sq_done, 1)
            for n in range(1, H // 2, 2):
                act.wait_ge(qt_done, n + 1)
                nc.scalar.activation(q_parts[:, 2 * n:2 * n + 2].rearrange("p h s q -> p (h s q)"),
                                     q_ps[:, 1024:2048], ACT.Copy).then_inc(qt_odd, 1)

        @block.vector
        def _(dve):
            count = [0]

            def link(ins):
                count[0] += 1
                ins.then_inc(dve_own, 1)
                dve.wait_ge(dve_own, count[0])

            def norm(n, src):
                for j in range(QT):
                    link(nc.vector.bn_stats(stats[:, n, j, :], src[:, j, :]))
                    link(nc.vector.bn_aggr(mean_var[:, n, j, :], stats[:, n, j, :]))
                nc.vector.tensor_scalar_add(var_eps[:, n, :], mean_var[:, n, :, 1], LN_EPS).then_inc(eps_done, 1)
                dve.wait_ge(root_done, n + 1)
                for j in range(QT):
                    last = nc.vector.tensor_scalar(z[:, n, j, :], src[:, j, :], mean_var[:, n, j, 0:1],
                                                   rstd[:, n, j:j + 1], ALU.subtract, ALU.mult)
                return last

            dve.wait_ge(x_in, 16)
            link(norm(0, x_res))
            norm(1, z[:, 0]).then_inc(z_done, 1)
            dve.wait_ge(gqk_in, 32)
            link(nc.vector.scalar_tensor_tensor(gqk[:], gq[:, 0, :], DH ** -0.5, gq[:, 1, :], ALU.mult, ALU.mult))
            link(nc.vector.scalar_tensor_tensor(bound[:, 0:DH], gqk[:], -1.0, gqk[:], ALU.mult, ALU.max))
            link(nc.vector.reduce_max(bound[:, DH:DH + 1], bound[:, 0:DH], AX_X))
            link(nc.vector.tensor_scalar(bound[:, DH + 1:DH + 2], bound[:, DH:DH + 1], float(DH), -EXP_ROOM, ALU.mult, ALU.add))
            link(nc.vector.tensor_scalar(bound[:, DH:DH + 1], bound[:, DH + 1:DH + 2], 0.0, -1.0, ALU.max, ALU.mult))
            dve.wait_ge(mask_in, 16)
            link(nc.vector.tensor_copy(mask_f[:], mask_raw[:]))
            link(nc.vector.memset(score_bias[:, CT:NT], 0.0))
            link(nc.vector.tensor_scalar(score_bias[:, 0:CT], mask_f[:], 1e30, -1e30, ALU.mult, ALU.add))
            link(nc.vector.tensor_scalar(score_bias[:], score_bias[:], bound[:, DH:DH + 1], None, ALU.add))
            dve.wait_ge(wq_hi, 1)
            nc.vector.tensor_tensor(wq[:, :, 1, :], wq_raw[:], wq[:, :, 0, :].bitcast(F32), ALU.subtract).then_inc(wq_lo, 1)
            dve.wait_ge(u_done, 1)
            for k in range(KD):
                link(nc.vector.tensor_copy(parts[:, :, k, 0, :], u[:, k]))
                last = nc.vector.tensor_tensor(parts[:, :, k, 1, :], u[:, k], parts[:, :, k, 0, :].bitcast(F32), ALU.subtract)
            last.then_inc(parts_done, 1)
            dve.wait_ge(sq_done, 1)
            link(nc.vector.reduce_sum(q_ss[:], q_sq[:], AX_X))
            nc.vector.tensor_scalar_max(q_ss[:], q_ss[:], RMS_FLOOR ** 2).then_inc(ss_done, 1)
            dve.wait_ge(rms_done, 1)
            heads = [P, QT * H, DH]
            link(nc.vector.tensor_tensor(qn[:], q_ps[:].rearrange("p (h d) -> p h d", d=DH),
                                         q_rms[:].unsqueeze(2).to_broadcast(heads), ALU.mult))
            link(nc.vector.tensor_tensor(qn[:], qn[:], gqk[:].unsqueeze(1).to_broadcast(heads), ALU.mult))
            for c in range(2):
                link(nc.vector.tensor_copy(q_dup[:, :, 0, c, :].bitcast(F32R), qn[:]))
            for c in range(2):
                last = nc.vector.tensor_tensor(q_dup[:, :, 1, c, :].bitcast(F32R), qn[:], q_dup[:, :, 0, c, :], ALU.subtract)
            last.then_inc(dup_done, 1)
            for n in range(0, H // 2, 2):
                dve.wait_ge(qt_done, n + 1)
                nc.vector.tensor_copy(q_parts[:, 2 * n:2 * n + 2].rearrange("p h s q -> p (h s q)"),
                                      q_ps[:, 0:1024]).then_inc(qt_even, 1)

        @block.tensor
        def _(pe):
            pe.wait_ge(ident_done, 1)
            pe.wait_ge(z_done, 1)
            for k in range(KD):
                for j in range(QT):
                    last = nc.tensor.transpose(xt_ps[:, k, j * P:(j + 1) * P], z[:, 1, j, k * P:(k + 1) * P], ident[:])
            last.then_inc(xt_done, 1)
            pe.wait_ge(parts_done, 1)
            pe.wait_ge(wq_lo, 1)
            for j in range(QT):
                for c in range(INNER // 512):
                    last = part_products(nc, q_ps[:, j * INNER + c * 512:j * INNER + (c + 1) * 512],
                                         lambda k, s: parts[:, j, k, s, :],
                                         lambda k, s: wq[:, k, s, c * 512:(c + 1) * 512])
            last.then_inc(q_done, 1)
            pe.wait_ge(dup_done, 1)
            for n in range(H // 2):
                if n >= 2:
                    pe.wait_ge(qt_odd if n % 2 else qt_even, n // 2)
                for h in range(2):
                    for s in range(2):
                        for j in range(QT):
                            at = (n % 2) * 1024 + h * 512 + s * NQ + j * P
                            last = nc.tensor.transpose(q_ps[:, at:at + P],
                                                       q_dup[:, j * H + 2 * n + h, s].rearrange("p c d -> p (c d)"), ident[:])
                last.then_inc(qt_done, 1)


def part_products(nc, out, stationary, moving, kd=KD):
    terms = [(k, s, m) for k in range(kd) for s, m in ((0, 0), (0, 1), (1, 0))]
    for n, (k, s, m) in enumerate(terms):
        last = nc.tensor.matmul(out, stationary(k, s), moving(k, m), start=n == 0, stop=n == len(terms) - 1)
    return last


def context(nc, sem, a, xn_dram, ident, neg_half, wkv, weight_sum):
    ctx_rows = a["ctx_1024"].rearrange("o (g j p) d -> g p (o j) d", p=P, j=GT)
    with ExitStack() as ctx:
        def pair(name, shape, dt=F32):
            return [ctx.enter_context(nc.sbuf_tensor(f"{name}{b}", shape, dt)) for b in range(2)]

        rows = pair("c_rows", [P, GT, D])
        stats = pair("c_stats", [P, GT, 6])
        mean_var = pair("c_mean_var", [P, GT, 2])
        var_eps = pair("c_var_eps", [P, GT])
        rstd = pair("c_rstd", [P, GT])
        z = pair("c_z", [P, GT, D])
        u = pair("c_u", [P, KD, GT, P])
        parts = pair("c_parts", [P, GT, KD, 2, P], F32R)
        gains = ctx.enter_context(nc.sbuf_tensor("c_gains", [P, 2, KD], F32))
        w_raw = ctx.enter_context(nc.sbuf_tensor("wkv_raw", [P, NQUAD, KD, 2 * QW], F32))
        zt_ps = [ctx.enter_context(nc.psum_tensor(f"c_zt_ps{b}", [P, KD, GT * P], F32)) for b in range(2)]

        rows_in = [sem(f"c_rows_in{b}") for b in range(2)]
        parts_out = [sem(f"c_parts_out{b}") for b in range(2)]
        gains_in, w_in = sem("c_gains_in"), sem("wkv_in")
        stats_done, aggr_done, eps_done, root_done = sem("c_stats_done"), sem("c_aggr_done"), sem("c_eps_done"), sem("c_root_done")
        z_done, zt_done, u_done, hi_done, lo_done = (
            sem("c_z_done"), sem("c_zt_done"), sem("c_u_done"), sem("c_hi_done"), sem("c_lo_done"))
        w_hi, w_lo = sem("wkv_hi"), sem("wkv_lo")

        block = ctx.enter_context(nc.Block())

        @block.sync
        def _(sp):
            with nc.allow_non_contiguous_dma(reason="a vector onto partitions"):
                for n, name in enumerate(("ln_x_g", "ln_x_b")):
                    sp.dma_start(gains[:, n, :], a["L0_xattn_" + name].rearrange("(k p) -> p k", p=P)).then_inc(gains_in, 16)
            for b in range(2):
                sp.dma_start(rows[b][:], ctx_rows[b]).then_inc(rows_in[b], 16)

            def store(t):
                sp.wait_ge(lo_done, t.n + 1)
                sp.dma_start(xn_dram[bass.ds(t.n * GT, GT), :, :].rearrange("t p n -> p t n"),
                             parts[t.slot][:].bitcast(F32).rearrange("p t k s n -> p t (k s n)")).then_inc(parts_out[t.slot], 16)

            def store_and_load(t):
                store(t)
                sp.dma_start(rows[t.slot][:], ctx_rows[bass.ds(t.n + 2, 1)].rearrange("g p j d -> p (g j) d")).then_inc(rows_in[t.slot], 16)

            run(sp, store_and_load, 0, NG - 2, 2)
            run(sp, store, NG - 2, NG, 2)
            for b in range(2):
                sp.wait_ge(parts_out[b], 16 * (NG // 2))

        @block.gpsimd
        def _(pool):
            def root(t):
                pool.wait_ge(eps_done, t.n + 1)
                nc.gpsimd.tensor_tensor(rstd[t.slot][:], var_eps[t.slot][:], neg_half[:, 0:GT], ALU.pow).then_inc(root_done, 1)

            run(pool, root, 0, NG, 2)

        @block.scalar
        def _(act):
            w_view = a["L0_xattn_Wkv"].rearrange("(k p) (s q n) -> q s p k n", p=P, s=2, q=NQUAD)
            for quad in range(NQUAD):
                for s in range(2):
                    act.dma_start(w_raw[:, quad, :, s * QW:(s + 1) * QW], w_view[quad, s]).then_inc(w_in, 16)

            def affine(t):
                act.wait_ge(zt_done, t.n + 1)
                if t.c >= 2:
                    act.wait_ge(lo_done, t.n - 1)
                for k in range(KD):
                    last = nc.scalar.activation(u[t.slot][:, k].rearrange("p t n -> p (t n)"), zt_ps[t.slot][:, k, :], ACT.Identity,
                                                scale=gains[:, 0, k:k + 1], bias=gains[:, 1, k:k + 1])
                last.then_inc(u_done, 1)

            act.wait_ge(gains_in, 32)
            run(act, affine, 0, 2, 2)
            act.wait_ge(w_in, 16 * 2 * NQUAD)
            for quad in range(NQUAD):
                nc.scalar.activation(wkv[:, quad, :, 0, :], w_raw[:, quad], ACT.Copy).then_inc(w_hi, 1)
            run(act, affine, 2, NG, 2)

        @block.vector
        def _(dve):
            def statistics(t):
                b = t.slot
                dve.wait_ge(rows_in[b], (t.lap + 1) * 16)
                for j in range(GT):
                    last = nc.vector.bn_stats(stats[b][:, j, :], rows[b][:, j, :])
                last.then_inc(stats_done, 1)

            def variance(t):
                b = t.slot
                for j in range(GT):
                    last = nc.vector.bn_aggr(mean_var[b][:, j, :], stats[b][:, j, :])
                last.then_inc(aggr_done, 1)
                dve.wait_ge(aggr_done, t.n + 1)
                nc.vector.tensor_scalar_add(var_eps[b][:], mean_var[b][:, :, 1], LN_EPS).then_inc(eps_done, 1)

            def normalise(t):
                b = t.slot
                dve.wait_ge(root_done, t.n + 1)
                if t.c >= 2:
                    dve.wait_ge(zt_done, t.n - 1)
                for j in range(GT):
                    last = nc.vector.tensor_scalar(z[b][:, j, :], rows[b][:, j, :], mean_var[b][:, j, 0:1],
                                                   rstd[b][:, j:j + 1], ALU.subtract, ALU.mult)
                last.then_inc(z_done, 1)

            def split_hi(t, more):
                b = t.slot
                dve.wait_ge(u_done, t.n + 1)
                if more:
                    dve.wait_ge(stats_done, t.n + 2)
                if t.c >= 2:
                    dve.wait_ge(parts_out[b], t.lap * 16)
                for k in range(KD):
                    last = nc.vector.tensor_copy(parts[b][:, :, k, 0, :], u[b][:, k])
                last.then_inc(hi_done, 1)

            def split_lo(t):
                b = t.slot
                dve.wait_ge(hi_done, t.n + 1)
                for k in range(KD):
                    last = nc.vector.tensor_tensor(parts[b][:, :, k, 1, :], u[b][:, k], parts[b][:, :, k, 0, :].bitcast(F32), ALU.subtract)
                last.then_inc(lo_done, 1)

            def next_two(t):
                statistics(t + 1)
                split_hi(t, True)
                variance(t + 1)
                split_lo(t)
                normalise(t + 1)

            nc.vector.memset(weight_sum[:], 0.0)
            statistics(Turn(0, 2))
            dve.wait_ge(stats_done, 1)
            variance(Turn(0, 2))
            normalise(Turn(0, 2))
            run(dve, next_two, 0, 2, 2)
            for quad in range(NQUAD):
                dve.wait_ge(w_hi, quad + 1)
                nc.vector.tensor_tensor(wkv[:, quad, :, 1, :], w_raw[:, quad], wkv[:, quad, :, 0, :].bitcast(F32),
                                        ALU.subtract).then_inc(w_lo, 1)
            run(dve, next_two, 2, NG - 2, 2)
            next_two(Turn(NG - 2, 2))
            split_hi(Turn(NG - 1, 2), False)
            split_lo(Turn(NG - 1, 2))

        @block.tensor
        def _(pe):
            def transposes(t):
                pe.wait_ge(z_done, t.n + 1)
                if t.c >= 2:
                    pe.wait_ge(u_done, t.n - 1)
                for k in range(KD):
                    for j in range(GT):
                        last = nc.tensor.transpose(zt_ps[t.slot][:, k, j * P:(j + 1) * P],
                                                   z[t.slot][:, j, k * P:(k + 1) * P], ident[:])
                last.then_inc(zt_done, 1)

            run(pe, transposes, 0, 2, 2)
            run(pe, transposes, 2, NG, 2)


def attention(nc, sem, xn_dram, ident, neg_half, wkv, q_parts, score_bias, attn_out, weight_sum):
    with ExitStack() as ctx:
        def ring(n, name, shape, dt=F32):
            return [ctx.enter_context(nc.sbuf_tensor(f"{name}{b}", shape, dt)) for b in range(n)]

        xn = ring(4, "xn", [P, KD, 2, P], F32R)
        kv = ring(4, "kv", [P, 2 * HQ, 2, DH], F32R)
        k_sq = ring(2, "k_sq", [P, HQ, DH])
        k_ss = ring(4, "k_ss", [P, HQ])
        k_ms = ring(4, "k_ms", [P, HQ])
        k_rms = ring(4, "k_rms", [P, HQ])
        kt = ring(2, "kt", [P, HQ * P], F32R)
        probs = ring(2, "probs", [P, HQ * NQ])
        probs_hi = ring(2, "probs_hi", [P, HQ * NQ], F32R)
        probs_lo = ring(2, "probs_lo", [P, HQ * NQ], F32R)
        kv_ps = ctx.enter_context(nc.psum_tensor("kv_ps", [P, 2 * QW], F32))
        kt_ps = ctx.enter_context(nc.psum_tensor("kt_ps", [P, HQ * P], F32))
        s_ps = [ctx.enter_context(nc.psum_tensor(f"s_ps{b}", [P, HQ * NQ], F32)) for b in range(2)]
        o_ps = ctx.enter_context(nc.psum_tensor("o_ps", [P, HQ * NQ], F32))

        xn_in = [sem(f"xn_in{b}") for b in range(4)]
        kv_done, sq_done, kv_hi, kv_lo = sem("kv_done"), sem("sq_done"), sem("kv_hi"), sem("kv_lo")
        ss_done, ms_done, rms_done = sem("ss_done"), sem("ms_done"), sem("rms_done")
        kt_done, kt_kept, s_done, exp_done = sem("kt_done"), sem("kt_kept"), sem("s_done"), sem("exp_done")
        p_hi, p_lo, pv_done, sum_done, out_kept = sem("p_hi"), sem("p_lo"), sem("pv_done"), sem("sum_done"), sem("out_kept")

        block = ctx.enter_context(nc.Block())

        def steps(eng, step):
            for s in (-1, 0, 1, 2):
                step(Turn(s, 4), 0)
            for quad in range(NQUAD):
                first = quad * NT + 3
                with eng.Fori(0, 7) as i:
                    for c in range(4):
                        step(Turn(first + c, 4, i), quad)
                for s in range(first + 28, (quad + 1) * NT + 3 if quad + 1 < NQUAD else NTILES + 2):
                    step(Turn(s, 4), quad)

        def exists(t):
            return 0 <= t.c < NTILES

        def quad_of(t):
            return t.c // NT

        @block.sync
        def _(sp):
            def load(t, quad):
                if t.c >= 4:
                    sp.wait_ge(kv_done, t.n - 3)
                sp.dma_start(xn[t.slot][:].bitcast(F32).rearrange("p k s n -> p (k s n)"),
                             xn_dram[bass.ds((t + -quad * NT).n, 1)].rearrange("t p n -> p (t n)")).then_inc(xn_in[t.slot], 16)

            for quad in range(NQUAD):
                for c in range(4):
                    load(Turn(quad * NT + c, 4), quad)
                run(sp, lambda t: load(t, quad), quad * NT + 4, (quad + 1) * NT, 4)

        @block.tensor
        def _(pe):
            def project(t):
                quad = quad_of(t)
                pe.wait_ge(xn_in[t.slot], (t.lap + 1) * 16)
                if t.c >= 1:
                    pe.wait_ge(kv_lo, t.n)
                part_products(nc, kv_ps[:], lambda k, s: xn[t.slot][:, k, s, :],
                              lambda k, s: wkv[:, quad, k, s, :]).then_inc(kv_done, 1)

            def transpose_k(t):
                pe.wait_ge(kv_lo, t.n + 1)
                if t.c >= 1:
                    pe.wait_ge(kt_kept, t.n)
                for h in range(HQ):
                    last = nc.tensor.transpose(kt_ps[:, h * P:(h + 1) * P],
                                               kv[t.slot][:, h].bitcast(F32).rearrange("p s d -> p (s d)"), ident[:])
                last.then_inc(kt_done, 1)

            def weight_v(t):
                local = t.c % NT
                pe.wait_ge(p_lo, t.n + 1)
                if local == 0 and t.c:
                    pe.wait_ge(out_kept, t.c // NT)
                b = t.c % 2
                for h in range(HQ):
                    for s, part in enumerate((probs_hi, probs_lo)):
                        last = nc.tensor.matmul(o_ps[:, h * NQ:(h + 1) * NQ],
                                                kv[t.slot][:, HQ + h].rearrange("p s d -> p (s d)"),
                                                part[b][:, h * NQ:(h + 1) * NQ],
                                                start=local == 0 and h % 2 == 0 and s == 0,
                                                stop=local == NT - 1 and s == 1, skip_group_check=True)
                last.then_inc(pv_done, 1)

            def scores(t):
                quad, b = quad_of(t), t.c % 2
                pe.wait_ge(kt_kept, t.n + 1)
                if t.c >= 2:
                    pe.wait_ge(exp_done, t.n - 1)
                for h in range(HQ):
                    for s in range(2):
                        last = nc.tensor.matmul(s_ps[b][:, h * NQ:(h + 1) * NQ], kt[b][:, h * P:(h + 1) * P],
                                                q_parts[:, quad * HQ + h, s, :], start=s == 0, stop=s == 1)
                last.then_inc(s_done, 1)

            def step(s, quad):
                if exists(s + 1):
                    project(s + 1)
                if exists(s):
                    transpose_k(s)
                if exists(s + -2):
                    weight_v(s + -2)
                if exists(s):
                    scores(s)

            steps(pe, step)

        @block.scalar
        def _(act):
            def weights(t):
                b = t.c % 2
                local = (t + -quad_of(t) * NT).n
                act.wait_ge(s_done, t.n + 1)
                act.wait_ge(rms_done, t.n + 1)
                if t.c >= 2:
                    act.wait_ge(p_lo, t.n - 1)
                    act.wait_ge(sum_done, t.n - 1)
                for h in range(HQ):
                    last = nc.scalar.activation(probs[b][:, h * NQ:(h + 1) * NQ], s_ps[b][:, h * NQ:(h + 1) * NQ], ACT.Exp,
                                                scale=k_rms[t.slot][:, h:h + 1], bias=score_bias[:, bass.ds(local, 1)])
                last.then_inc(exp_done, 1)

            def squares_and_hi(t):
                act.wait_ge(kv_done, t.n + 1)
                if t.c >= 2:
                    act.wait_ge(ss_done, t.n - 1)
                nc.scalar.activation(k_sq[t.c % 2][:].rearrange("p h d -> p (h d)"), kv_ps[:, 0:QW], ACT.Square,
                                     scale=DH ** -0.5).then_inc(sq_done, 1)
                if t.c >= 4:
                    act.wait_ge(pv_done, t.n - 3)
                nc.scalar.activation(kv[t.slot][:, :, 0, :], kv_ps[:].rearrange("p (h d) -> p h d", d=DH), ACT.Copy).then_inc(kv_hi, 1)

            def step(s, quad):
                if exists(s + -1):
                    weights(s + -1)
                if exists(s + 1):
                    squares_and_hi(s + 1)

            steps(act, step)

        @block.vector
        def _(dve):
            def keep_kt(t):
                dve.wait_ge(kt_done, t.n + 1)
                if t.c >= 2:
                    dve.wait_ge(s_done, t.n - 1)
                nc.vector.tensor_copy(kt[t.c % 2][:], kt_ps[:]).then_inc(kt_kept, 1)

            def split_weights(t):
                b = t.c % 2
                dve.wait_ge(exp_done, t.n + 1)
                if t.c >= 2:
                    dve.wait_ge(pv_done, t.n - 1)
                nc.vector.tensor_copy(probs_hi[b][:], probs[b][:]).then_inc(p_hi, 1)
                dve.wait_ge(p_hi, t.n + 1)
                nc.vector.tensor_tensor(probs_lo[b][:], probs[b][:], probs_hi[b][:].bitcast(F32), ALU.subtract).then_inc(p_lo, 1)

            def split_kv(t):
                dve.wait_ge(kv_hi, t.n + 1)
                nc.vector.tensor_tensor(kv[t.slot][:, :, 1, :], kv_ps[:].rearrange("p (h d) -> p h d", d=DH),
                                        kv[t.slot][:, :, 0, :].bitcast(F32), ALU.subtract).then_inc(kv_lo, 1)
                dve.wait_ge(sq_done, t.n + 1)
                if t.c >= 4:
                    dve.wait_ge(rms_done, t.n - 3)
                nc.vector.reduce_sum(k_ss[t.slot][:], k_sq[t.c % 2][:], AX_X).then_inc(ss_done, 1)
                dve.wait_ge(ss_done, t.n + 1)
                nc.vector.tensor_scalar_max(k_ms[t.slot][:], k_ss[t.slot][:], RMS_FLOOR ** 2).then_inc(ms_done, 1)

            def step(s, quad):
                if exists(s):
                    keep_kt(s)
                if exists(s + -1):
                    split_weights(s + -1)
                if exists(s + 1):
                    split_kv(s + 1)
                if exists(s + -2) and (s.c - 2) % NT == NT - 1:
                    dve.wait_ge(pv_done, s.c - 1)
                    nc.vector.tensor_copy(attn_out[:, (s.c - 2) // NT, :], o_ps[:]).then_inc(out_kept, 1)

            steps(dve, step)

        @block.gpsimd
        def _(pool):
            def sum_weights(t):
                pool.wait_ge(exp_done, t.n + 1)
                if t.c >= 1:
                    pool.wait_ge(sum_done, t.n)
                total = weight_sum[:, quad_of(t), :]
                nc.gpsimd.tensor_tensor(total, total, probs[t.c % 2][:], ALU.add).then_inc(sum_done, 1)

            def root(t):
                pool.wait_ge(ms_done, t.n + 1)
                if t.c >= 4:
                    pool.wait_ge(exp_done, t.n - 3)
                nc.gpsimd.tensor_tensor(k_rms[t.slot][:], k_ms[t.slot][:], neg_half[:, 0:HQ], ALU.pow).then_inc(rms_done, 1)

            def step(s, quad):
                if exists(s + -1):
                    sum_weights(s + -1)
                if exists(s + 1):
                    root(s + 1)

            steps(pool, step)


def attention_output(nc, sem, a, x_res, ones, attn_out, weight_sum):
    with ExitStack() as ctx:
        wout = ctx.enter_context(nc.sbuf_tensor("wout", [P, H, D], F32))
        bout = ctx.enter_context(nc.sbuf_tensor("bout", [P, D], F32))
        inverse = [ctx.enter_context(nc.sbuf_tensor(f"inverse{b}", [P, HQ * NQ], F32)) for b in range(2)]
        sum_ps = [ctx.enter_context(nc.psum_tensor(f"sum_ps{b}", [P, HQ * NQ], F32)) for b in range(2)]
        y_ps = ctx.enter_context(nc.psum_tensor("y_ps", [P, QT, 512], F32))
        wout_in, bout_in = sem("wout_in"), sem("bout_in")
        sum_ready, inverse_done, scaled, y_done, own = sem("sum_ready"), sem("inverse_done"), sem("scaled"), sem("y_done"), sem("y_own")

        block = ctx.enter_context(nc.Block())

        @block.sync
        def _(sp):
            rows = a["L0_xattn_Wout"].rearrange("(h d) n -> d h n", d=DH)
            for c in range(2):
                sp.dma_start(wout[c * DH:(c + 1) * DH], rows).then_inc(wout_in, 16)
            sp.dma_start(bout[:], a["L0_xattn_bout"].partition_broadcast(P)).then_inc(bout_in, 16)

        @block.tensor
        def _(pe):
            for quad in range(NQUAD):
                if quad >= 2:
                    pe.wait_ge(inverse_done, quad - 1)
                for c in range(2):
                    last = nc.tensor.matmul(sum_ps[quad % 2][:, c * 512:(c + 1) * 512], ones[:],
                                            weight_sum[:, quad, c * 512:(c + 1) * 512], start=True, stop=True)
                last.then_inc(sum_ready, 1)
            pe.wait_ge(wout_in, 32)
            for h in range(H):
                if h % HQ == 0:
                    pe.wait_ge(scaled, h // HQ + 1)
                for j in range(QT):
                    at = (h % HQ) * NQ + j * P
                    last = nc.tensor.matmul(y_ps[:, j, 0:D], attn_out[:, h // HQ, at:at + P], wout[:, h, :],
                                            start=h == 0, stop=h == H - 1)
            last.then_inc(y_done, 1)

        @block.vector
        def _(dve):
            for quad in range(NQUAD):
                dve.wait_ge(sum_ready, quad + 1)
                nc.vector.reciprocal(inverse[quad % 2][:], sum_ps[quad % 2][:]).then_inc(inverse_done, 1)
                dve.wait_ge(inverse_done, quad + 1)
                nc.vector.tensor_tensor(attn_out[:, quad, :], attn_out[:, quad, :], inverse[quad % 2][:], ALU.mult).then_inc(scaled, 1)
            dve.wait_ge(bout_in, 16)
            nc.vector.tensor_tensor(x_res[:], x_res[:], bout[:].unsqueeze(1).to_broadcast([P, QT, D]), ALU.add).then_inc(own, 1)
            dve.wait_ge(own, 1)
            dve.wait_ge(y_done, 1)
            nc.vector.tensor_tensor(x_res[:], x_res[:], y_ps[:, :, 0:D], ALU.add).then_inc(own, 1)


def row_norm(nc, dve, own, eps_done, root_done, src, dst, stats, mean_var, var_eps, rstd):
    for j in range(QT):
        last = nc.vector.bn_stats(stats[:, j, :], src[:, j, :])
    last.then_inc(own, 1)
    dve.wait_ge(own, 1)
    for j in range(QT):
        last = nc.vector.bn_aggr(mean_var[:, j, :], stats[:, j, :])
    last.then_inc(own, 1)
    dve.wait_ge(own, 2)
    nc.vector.tensor_scalar_add(var_eps[:], mean_var[:, :, 1], LN_EPS).then_inc(eps_done, 1)
    dve.wait_ge(root_done, 1)
    for j in range(QT):
        last = nc.vector.tensor_scalar(dst[:, j, :], src[:, j, :], mean_var[:, j, 0:1], rstd[:, j:j + 1],
                                       ALU.subtract, ALU.mult)
    return last


def performer(nc, sem, a, x_res, ident, neg_half):
    HH = H // KD
    with ExitStack() as ctx:
        def sb(name, shape, dt=F32):
            return ctx.enter_context(nc.sbuf_tensor("f_" + name, shape, dt))

        w = {name: sb(name, [P, KD, D]) for name in ("Wq", "Wk", "Wv", "Wo", "Wfc")}
        columns = {name: sb(name, [P, KD]) for name in ("bq", "bk", "bo")}
        spread = {name: sb(name, [P, D]) for name in ("bv", "bfc")}
        stats, mean_var, var_eps, rstd = sb("stats", [P, QT, 6]), sb("mean_var", [P, QT, 2]), sb("var_eps", [P, QT]), sb("rstd", [P, QT])
        z, zt = sb("z", [P, QT, D]), sb("zt", [P, KD, NQ])
        proj_bd = sb("proj_bd", [P, HH, M])
        diag_bd = sb("diag_bd", [P, HH])
        pair_mask = sb("pair_mask", [PAIR, 2, VW])
        qk_t = sb("qk_t", [P, 2, KD, NQ])
        qk_sq = sb("qk_sq", [P, 2, KD, NQ])
        v_one = sb("v_one", [P, QT, H, VW])
        top = sb("top", [P, 2, QT, KD, HH])
        top_key = sb("top_key", [P, 2, H])
        less = sb("less", [P, 2, QT, KD, HH])
        feats = sb("feats", [P, 2, QT, KD * HH * M])
        kv_ctx = sb("kv_ctx", [PAIR, NPAIR, 2 * VW])
        qp_t = sb("qp_t", [PAIR, NPAIR * NQ])
        inverse = sb("inverse", [P, QT, H])
        o, o_t, h_t = sb("o", [P, QT, H, DHP]), sb("o_t", [P, KD, NQ]), sb("h_t", [P, KD, NQ])
        y = sb("y", [P, QT, D])
        ps = ctx.enter_context(nc.psum_tensor("f_ps", [P, 8, 512], F32))

        w_in, bias_in, proj_in = sem("f_w_in"), sem("f_bias_in"), sem("f_proj_in")
        blocks_started, blocks_zeroed, blocks_half, blocks_done = (
            sem("f_blocks_started"), sem("f_blocks_zeroed"), sem("f_blocks_half"), sem("f_blocks_done"))
        own, eps_done, root_done, z_done, zt_done, zt_kept = (
            sem("f_own"), sem("f_eps_done"), sem("f_root_done"), sem("f_z_done"), sem("f_zt_done"), sem("f_zt_kept"))
        qkv_done, qk_kept, v_kept, proj_scaled = sem("f_qkv_done"), sem("f_qk_kept"), sem("f_v_kept"), sem("f_proj_scaled")
        exponents_done, key_top, key_top_all = sem("f_exponents_done"), sem("f_key_top"), sem("f_key_top_all")
        less_done, exp_done, feats_done = sem("f_less_done"), sem("f_exp_done"), sem("f_feats_done")
        context_done, qp_done, context_kept, qp_kept = (
            sem("f_context_done"), sem("f_qp_done"), sem("f_context_kept"), sem("f_qp_kept"))
        o_ready, o_kept, ot_done, ot_kept = sem("f_o_ready"), sem("f_o_kept"), sem("f_ot_done"), sem("f_ot_kept")
        ht_done, ht_kept, fc_done = sem("f_ht_done"), sem("f_ht_kept"), sem("f_fc_done")

        block = ctx.enter_context(nc.Block())

        @block.sync
        def _(sp):
            for name, tile in w.items():
                sp.dma_start(tile[:], a["L0_attn_" + name].rearrange("(k p) n -> p k n", p=P)).then_inc(w_in, 16)
            with nc.allow_non_contiguous_dma(reason="a vector onto partitions"):
                for name, tile in columns.items():
                    sp.dma_start(tile[:], a["L0_attn_" + name].rearrange("(k p) -> p k", p=P)).then_inc(bias_in, 16)
            for name, tile in spread.items():
                sp.dma_start(tile[:], a["L0_attn_" + name].partition_broadcast(P)).then_inc(bias_in, 16)
            sp.wait_ge(blocks_zeroed, 1)
            for h in range(HH):
                sp.dma_start(proj_bd[DHP * h:DHP * (h + 1), h, :], a["L0_attn_proj"]).then_inc(proj_in, 16)

        @block.gpsimd
        def _(pool):
            nc.gpsimd.memset(proj_bd[:], 0.0).then_inc(blocks_zeroed, 1)
            nc.gpsimd.memset(diag_bd[:], 0.5 * DHP ** -0.5).then_inc(blocks_started, 1)
            nc.gpsimd.memset(pair_mask[:], 1.0).then_inc(blocks_started, 1)
            pool.wait_ge(blocks_started, 2)
            for n, (tile, pattern, rows) in enumerate(((diag_bd, [[-DHP, HH]], DHP), (pair_mask, [[-M, 2], [0, VW]], M))):
                nc.gpsimd.affine_select(out=tile[:], in_=tile[:], compare_op=ALU.is_ge, fill=0.0, base=0,
                                        pattern=pattern, channel_multiplier=1).then_inc(blocks_half, 1)
                pool.wait_ge(blocks_half, 1 + n)
                nc.gpsimd.affine_select(out=tile[:], in_=tile[:], compare_op=ALU.is_ge, fill=0.0, base=rows - 1,
                                        pattern=[[-s, c] for s, c in pattern], channel_multiplier=-1).then_inc(blocks_done, 1)
            pool.wait_ge(eps_done, 1)
            nc.gpsimd.tensor_tensor(rstd[:], var_eps[:], neg_half[:, 0:QT], ALU.pow).then_inc(root_done, 1)
            pool.wait_ge(key_top, 1)
            nc.gpsimd.partition_all_reduce(top_key[:, 1, :], top_key[:, 0, :], P, bass.bass_isa.ReduceOp.max).then_inc(key_top_all, 1)

        @block.tensor
        def _(pe):
            pe.wait_ge(z_done, 1)
            for k in range(KD):
                for j in range(QT):
                    last = nc.tensor.transpose(ps[:, k, j * P:(j + 1) * P], z[:, j, k * P:(k + 1) * P], ident[:])
            last.then_inc(zt_done, 1)
            pe.wait_ge(w_in, 16 * len(w))
            pe.wait_ge(zt_kept, 1)
            for n, name in enumerate(("Wq", "Wk")):
                for half in range(KD):
                    for k in range(KD):
                        nc.tensor.matmul(ps[:, 2 + 2 * n + half, 0:NQ], w[name][:, k, half * P:(half + 1) * P],
                                         zt[:, k, :], start=k == 0, stop=k == KD - 1)
            for j in range(QT):
                for k in range(KD):
                    last = nc.tensor.matmul(ps[:, 6 + j, 0:D], zt[:, k, j * P:(j + 1) * P], w["Wv"][:, k, :],
                                            start=k == 0, stop=k == KD - 1)
            last.then_inc(qkv_done, 1)
            pe.wait_ge(qk_kept, 1)
            pe.wait_ge(v_kept, 1)
            pe.wait_ge(proj_scaled, 1)
            pe.wait_ge(blocks_done, 2)
            for n in range(2):
                for j in range(QT):
                    for half in range(KD):
                        bank = ps[:, 4 * n + 2 * j + half]
                        nc.tensor.matmul(bank[:, 0:HH * M], qk_t[:, n, half, j * P:(j + 1) * P],
                                         proj_bd[:].rearrange("p h m -> p (h m)"), start=True, stop=True)
                        last = nc.tensor.matmul(bank[:, HH * M:HH * M + HH], qk_sq[:, n, half, j * P:(j + 1) * P],
                                                diag_bd[:], start=True, stop=True)
                last.then_inc(exponents_done, 1)
            pe.wait_ge(feats_done, 2)
            for g in range(NPAIR):
                for j in range(QT):
                    last = nc.tensor.matmul(ps[0:PAIR, 4, g * 2 * VW:(g + 1) * 2 * VW], feats[:, 1, j, g * PAIR:(g + 1) * PAIR],
                                            v_one[:, j, 2 * g:2 * g + 2, :].rearrange("p h d -> p (h d)"),
                                            start=j == 0, stop=j == QT - 1)
            last.then_inc(context_done, 1)
            for g in range(NPAIR):
                for j in range(QT):
                    at = g * NQ + j * P
                    last = nc.tensor.transpose(ps[0:PAIR, at // 512, at % 512:at % 512 + P],
                                               feats[:, 0, j, g * PAIR:(g + 1) * PAIR], ident[:])
            last.then_inc(qp_done, 1)
            pe.wait_ge(context_kept, 1)
            pe.wait_ge(qp_kept, 1)
            for j in range(QT):
                for g in range(NPAIR):
                    last = nc.tensor.matmul(ps[:, 6 + j, g * 2 * VW:(g + 1) * 2 * VW], qp_t[:, g * NQ + j * P:g * NQ + (j + 1) * P],
                                            kv_ctx[:, g, :], start=True, stop=True)
            last.then_inc(o_ready, 1)
            pe.wait_ge(o_kept, 1)
            for k in range(KD):
                for j in range(QT):
                    last = nc.tensor.transpose(ps[:, k, j * P:(j + 1) * P],
                                               o[:, j].rearrange("p h d -> p (h d)")[:, k * P:(k + 1) * P], ident[:])
            last.then_inc(ot_done, 1)
            pe.wait_ge(ot_kept, 1)
            for half in range(KD):
                for k in range(KD):
                    last = nc.tensor.matmul(ps[:, 2 + half, 0:NQ], w["Wo"][:, k, half * P:(half + 1) * P], o_t[:, k, :],
                                            start=k == 0, stop=k == KD - 1)
            last.then_inc(ht_done, 1)
            pe.wait_ge(ht_kept, 1)
            for j in range(QT):
                for k in range(KD):
                    last = nc.tensor.matmul(ps[:, 4 + j, 0:D], h_t[:, k, j * P:(j + 1) * P], w["Wfc"][:, k, :],
                                            start=k == 0, stop=k == KD - 1)
            last.then_inc(fc_done, 1)

        @block.scalar
        def _(act):
            act.wait_ge(bias_in, 16 * 5)
            act.wait_ge(qkv_done, 1)
            for n, name in enumerate(("bq", "bk")):
                for half in range(KD):
                    nc.scalar.activation(qk_t[:, n, half, :], ps[:, 2 + 2 * n + half, 0:NQ], ACT.Identity,
                                         bias=columns[name][:, half:half + 1])
                    last = nc.scalar.activation(qk_sq[:, n, half, :], ps[:, 2 + 2 * n + half, 0:NQ], ACT.Square,
                                                bias=columns[name][:, half:half + 1])
            last.then_inc(qk_kept, 1)
            for n in range(2):
                side = feats[:, n].rearrange("p j m -> p (j m)")
                act.wait_ge(less_done, n + 1)
                nc.scalar.activation(side, side, ACT.Exp).then_inc(exp_done, 1)
            act.wait_ge(qp_done, 1)
            nc.scalar.activation(qp_t[:], ps[0:PAIR, 0:4].rearrange("p b n -> p (b n)"), ACT.Copy).then_inc(qp_kept, 1)
            act.wait_ge(ht_done, 1)
            for half in range(KD):
                last = nc.scalar.activation(h_t[:, half, :], ps[:, 2 + half, 0:NQ], ACT.Identity,
                                            bias=columns["bo"][:, half:half + 1])
            last.then_inc(ht_kept, 1)

        @block.vector
        def _(dve):
            row_norm(nc, dve, own, eps_done, root_done, x_res, z, stats, mean_var, var_eps, rstd).then_inc(z_done, 1)
            count = [NORM_LINKS]

            def link(ins):
                count[0] += 1
                ins.then_inc(own, 1)
                dve.wait_ge(own, count[0])

            dve.wait_ge(zt_done, 1)
            nc.vector.tensor_copy(zt[:], ps[:, 0:KD, 0:NQ]).then_inc(zt_kept, 1)
            dve.wait_ge(proj_in, 16 * HH)
            nc.vector.tensor_scalar_mul(proj_bd[:], proj_bd[:], DHP ** -0.25).then_inc(proj_scaled, 1)
            link(nc.vector.memset(v_one[:], 1.0))
            dve.wait_ge(bias_in, 16 * 5)
            dve.wait_ge(qkv_done, 1)
            for j in range(QT):
                last = nc.vector.tensor_tensor(v_one[:, j, :, 0:DHP], ps[:, 6 + j, 0:D].rearrange("p (h d) -> p h d", d=DHP),
                                               spread["bv"][:].rearrange("p (h d) -> p h d", d=DHP), ALU.add)
            last.then_inc(v_kept, 1)

            for n in range(2):
                dve.wait_ge(exponents_done, n + 1)
                for j in range(QT):
                    exponents = ps[:, 4 * n + 2 * j:4 * n + 2 * j + 2, 0:HH * M].rearrange("p k (h m) -> p k h m", m=M)
                    link(nc.vector.reduce_max(top[:, n, j], exponents, AX_X))
                if n == 1:
                    nc.vector.tensor_tensor(top_key[:, 0, :], top[:, 1, 0].rearrange("p k h -> p (k h)"),
                                            top[:, 1, 1].rearrange("p k h -> p (k h)"), ALU.max).then_inc(key_top, 1)
                    dve.wait_ge(key_top_all, 1)
                for j in range(QT):
                    diagonal = ps[:, 4 * n + 2 * j:4 * n + 2 * j + 2, HH * M:HH * M + HH]
                    highest = top[:, 0, j] if n == 0 else top_key[:, 1, :].rearrange("p (k h) -> p k h", k=KD)
                    link(nc.vector.tensor_tensor(less[:, n, j], diagonal, highest, ALU.add))
                    for half in range(KD):
                        last = nc.vector.tensor_tensor(
                            feats[:, n, j, half * HH * M:(half + 1) * HH * M].rearrange("p (h m) -> p h m", m=M),
                            ps[:, 4 * n + 2 * j + half, 0:HH * M].rearrange("p (h m) -> p h m", m=M),
                            less[:, n, j, half].unsqueeze(2).to_broadcast([P, HH, M]), ALU.subtract)
                last.then_inc(less_done, 1)
            for n in range(2):
                dve.wait_ge(exp_done, n + 1)
                nc.vector.tensor_scalar(feats[:, n], feats[:, n], FEAT_EPS, M ** -0.5, ALU.add, ALU.mult).then_inc(feats_done, 1)
            dve.wait_ge(blocks_done, 2)
            dve.wait_ge(context_done, 1)
            nc.vector.tensor_tensor(kv_ctx[:], ps[0:PAIR, 4, 0:NPAIR * 2 * VW].rearrange("p (g n) -> p g n", g=NPAIR),
                                    pair_mask[:].rearrange("p c n -> p (c n)").unsqueeze(1).to_broadcast([PAIR, NPAIR, 2 * VW]),
                                    ALU.mult).then_inc(context_kept, 1)
            dve.wait_ge(o_ready, 1)
            sums = ps[:, 6:8, 0:H * VW].rearrange("p j (h d) -> p j h d", d=VW)
            link(nc.vector.reciprocal(inverse[:], sums[:, :, :, DHP]))
            for j in range(QT):
                last = nc.vector.tensor_tensor(o[:, j], sums[:, j, :, 0:DHP], inverse[:, j].unsqueeze(2).to_broadcast([P, H, DHP]), ALU.mult)
            last.then_inc(o_kept, 1)
            dve.wait_ge(ot_done, 1)
            nc.vector.tensor_copy(o_t[:], ps[:, 0:KD, 0:NQ]).then_inc(ot_kept, 1)
            dve.wait_ge(fc_done, 1)
            link(nc.vector.tensor_tensor(y[:], ps[:, 4:6, 0:D], spread["bfc"][:].unsqueeze(1).to_broadcast([P, QT, D]), ALU.add))
            for j in range(QT):
                last = nc.vector.scalar_tensor_tensor(x_res[:, j, :], y[:, j, :], 0.0, x_res[:, j, :], ALU.max, ALU.add)
            link(last)


def experts(nc, sem, a, x_res, ident, neg_half):
    E1 = E + 1
    with ExitStack() as ctx:
        def sb(name, shape, dt=F32):
            return ctx.enter_context(nc.sbuf_tensor("e_" + name, shape, dt))

        def pair(name, shape, dt=F32):
            return [sb(f"{name}{b}", shape, dt) for b in range(2)]

        w1_raw, w2_raw = pair("w1_raw", [P, KD, F]), pair("w2_raw", [P, FT, D])
        w1, w2 = pair("w1", [P, KD, 2, F], F32R), pair("w2", [P, FT, 2, D], F32R)
        b1 = sb("b1", [P, E1, FT])
        b2 = sb("b2", [E1, D])
        wg = sb("wg", [P, KD, E])
        stats, mean_var, var_eps, rstd = sb("stats", [P, QT, 6]), sb("mean_var", [P, QT, 2]), sb("var_eps", [P, QT]), sb("rstd", [P, QT])
        z, zt = sb("z", [P, QT, D]), sb("zt", [P, KD, NQ])
        zp = sb("zp", [P, KD, 2, NQ], F32R)
        logit_top, neg_top = sb("logit_top", [P, QT, 8]), sb("neg_top", [P, QT])
        gate_exp, gate_sum, gate_inv = sb("gate_exp", [P, QT, E]), sb("gate_sum", [P, QT]), sb("gate_inv", [P, QT])
        gate = sb("gate", [P, QT, E])
        best, best_at = sb("best", [P, QT, 8]), sb("best_at", [P, QT, 8], U32)
        best_f, two = sb("best_f", [P, QT, 2]), sb("two", [P, QT, 4])
        number, number_f = sb("number", [P, E], mybir.dt.int32), sb("number_f", [P, E])
        picked = sb("picked", [P, QT, 2, E])
        share = sb("share", [P, QT, E1])
        share_t = sb("share_t", [E1, NQ])
        act_f = sb("act_f", [P, FT, NQ])
        act_p = sb("act_p", [P, 2, FT, NQ], F32R)
        h_ps = ctx.enter_context(nc.psum_tensor("e_h_ps", [P, FT, NQ], F32))
        y_ps = [ctx.enter_context(nc.psum_tensor(f"e_y_ps{b}", [P, QT, D], F32)) for b in range(2)]
        gate_ps = ctx.enter_context(nc.psum_tensor("e_gate_ps", [P, 512], F32))
        bias_ps = ctx.enter_context(nc.psum_tensor("e_bias_ps", [P, QT, D], F32))

        w1_in, w2_in = [sem(f"e_w1_in{b}") for b in range(2)], [sem(f"e_w2_in{b}") for b in range(2)]
        b1_in, b2_in, wg_in = sem("e_b1_in"), sem("e_b2_in"), sem("e_wg_in")
        numbered = sem("e_numbered")
        own, eps_done, root_done, z_done, zt_done, zt_kept = (
            sem("e_own"), sem("e_eps_done"), sem("e_root_done"), sem("e_z_done"), sem("e_zt_done"), sem("e_zt_kept"))
        zp_done, logits_done, neg_done, gate_exp_done = sem("e_zp_done"), sem("e_logits_done"), sem("e_neg_done"), sem("e_gate_exp_done")
        share_done, share_t_done, share_t_kept, bias_done = (
            sem("e_share_done"), sem("e_share_t_done"), sem("e_share_t_kept"), sem("e_bias_done"))
        w1_hi, w1_lo, w2_hi, w2_lo = sem("e_w1_hi"), sem("e_w1_lo"), sem("e_w2_hi"), sem("e_w2_lo")
        up_done, silu_done, act_hi, act_lo, down_done, added = (
            sem("e_up_done"), sem("e_silu_done"), sem("e_act_hi"), sem("e_act_lo"), sem("e_down_done"), sem("e_added"))

        block = ctx.enter_context(nc.Block())

        @block.sync
        def _(sp):
            def load(t):
                e = bass.ds(t.n, 1)
                if t.c >= 2:
                    sp.wait_ge(w1_lo, t.n - 1)
                    sp.wait_ge(w2_lo, t.n - 1)
                sp.dma_start(w1_raw[t.slot][:], a["ffn_W1"][e].rearrange("e (k p) f -> p (e k) f", p=P)).then_inc(w1_in[t.slot], 16)
                sp.dma_start(w2_raw[t.slot][:], a["ffn_W2"][e].rearrange("e (t p) n -> p (e t) n", p=P)).then_inc(w2_in[t.slot], 16)

            run(sp, load, 0, 2, 2)
            sp.dma_start(wg[:], a["L0_ffn_Wg"].rearrange("(k p) e -> p k e", p=P)).then_inc(wg_in, 16)
            sp.dma_start(b2[:], a["ffn_b2"]).then_inc(b2_in, 16)
            with nc.allow_non_contiguous_dma(reason="a vector onto partitions"):
                sp.dma_start(b1[:], a["ffn_b1"].rearrange("e (t p) -> p e t", p=P)).then_inc(b1_in, 16)
            run(sp, load, 2, E1, 2)

        @block.gpsimd
        def _(pool):
            nc.gpsimd.iota(number[:], [[1, E]], base=0, channel_multiplier=0).then_inc(numbered, 1)
            pool.wait_ge(eps_done, 1)
            nc.gpsimd.tensor_tensor(rstd[:], var_eps[:], neg_half[:, 0:QT], ALU.pow).then_inc(root_done, 1)

        @block.tensor
        def _(pe):
            pe.wait_ge(z_done, 1)
            for k in range(KD):
                for j in range(QT):
                    last = nc.tensor.transpose(y_ps[0][:, k, j * P:(j + 1) * P], z[:, j, k * P:(k + 1) * P], ident[:])
            last.then_inc(zt_done, 1)
            pe.wait_ge(zt_kept, 1)
            pe.wait_ge(wg_in, 16)
            for j in range(QT):
                for k in range(KD):
                    last = nc.tensor.matmul(gate_ps[:, j * E:(j + 1) * E], zt[:, k, j * P:(j + 1) * P], wg[:, k, :],
                                            start=k == 0, stop=k == KD - 1)
            last.then_inc(logits_done, 1)
            pe.wait_ge(zp_done, 1)

            def up(t):
                pe.wait_ge(w1_lo, t.n + 1)
                if t.c >= 1:
                    pe.wait_ge(silu_done, t.n)
                for f in range(FT):
                    last = part_products(nc, h_ps[:, f, :], lambda k, s: w1[t.slot][:, k, s, f * P:(f + 1) * P],
                                         lambda k, s: zp[:, k, s, :])
                last.then_inc(up_done, 1)

            def down(t):
                b = t.slot
                pe.wait_ge(w2_lo, t.n + 1)
                pe.wait_ge(act_lo, t.n + 1)
                if t.c >= 2:
                    pe.wait_ge(added, t.n - 1)
                for j in range(QT):
                    last = part_products(nc, y_ps[b][:, j, :], lambda f, s: act_p[:, s, f, j * P:(j + 1) * P],
                                         lambda f, s: w2[b][:, f, s, :], FT)
                last.then_inc(down_done, 1)

            def turn(t):
                up(t)
                down(t + -1)

            up(Turn(0, 2))
            pe.wait_ge(share_done, 1)
            for j in range(QT):
                last = nc.tensor.transpose(bias_ps[0:E1, j, 0:P], share[:, j, :], ident[:])
            last.then_inc(share_t_done, 1)
            pe.wait_ge(share_t_kept, 1)
            pe.wait_ge(b2_in, 16)
            for j in range(QT):
                last = nc.tensor.matmul(bias_ps[:, j, :], share_t[:, j * P:(j + 1) * P], b2[:], start=True, stop=True)
            last.then_inc(bias_done, 1)
            run(pe, turn, 1, E1, 2)
            down(Turn(E1 - 1, 2))

        @block.scalar
        def _(act):
            def hi1(t):
                act.wait_ge(w1_in[t.slot], (t.lap + 1) * 16)
                if t.c >= 2:
                    act.wait_ge(up_done, t.n - 1)
                nc.scalar.activation(w1[t.slot][:, :, 0, :], w1_raw[t.slot][:], ACT.Copy).then_inc(w1_hi, 1)

            def hi2(t):
                act.wait_ge(w2_in[t.slot], (t.lap + 1) * 16)
                if t.c >= 2:
                    act.wait_ge(down_done, t.n - 1)
                nc.scalar.activation(w2[t.slot][:, :, 0, :], w2_raw[t.slot][:], ACT.Copy).then_inc(w2_hi, 1)

            def silu(t):
                act.wait_ge(up_done, t.n + 1)
                if t.c >= 1:
                    act.wait_ge(act_lo, t.n)
                for f in range(FT):
                    last = nc.scalar.activation(act_f[:, f, :], h_ps[:, f, :], ACT.Silu,
                                                bias=b1[:, bass.ds(t.n, 1), f:f + 1].rearrange("p e f -> p (e f)"))
                last.then_inc(silu_done, 1)

            def turn(t):
                hi1(t + 1)
                silu(t)
                hi2(t + 1)

            hi1(Turn(0, 2))
            hi2(Turn(0, 2))
            act.wait_ge(neg_done, 1)
            for j in range(QT):
                last = nc.scalar.activation(gate_exp[:, j, :], gate_ps[:, j * E:(j + 1) * E], ACT.Exp,
                                            bias=neg_top[:, j:j + 1], accum_out=gate_sum[:, j:j + 1])
            last.then_inc(gate_exp_done, 1)
            act.wait_ge(b1_in, 16)
            turn(Turn(0, 2))
            run(act, turn, 1, E1 - 1, 2)
            silu(Turn(E1 - 1, 2))

        @block.vector
        def _(dve):
            row_norm(nc, dve, own, eps_done, root_done, x_res, z, stats, mean_var, var_eps, rstd).then_inc(z_done, 1)
            count = [NORM_LINKS]

            def link(ins):
                count[0] += 1
                ins.then_inc(own, 1)
                dve.wait_ge(own, count[0])

            def lo1(t):
                dve.wait_ge(w1_hi, t.n + 1)
                nc.vector.tensor_tensor(w1[t.slot][:, :, 1, :], w1_raw[t.slot][:], w1[t.slot][:, :, 0, :].bitcast(F32), ALU.subtract).then_inc(w1_lo, 1)

            def lo2(t):
                dve.wait_ge(w2_hi, t.n + 1)
                nc.vector.tensor_tensor(w2[t.slot][:, :, 1, :], w2_raw[t.slot][:], w2[t.slot][:, :, 0, :].bitcast(F32), ALU.subtract).then_inc(w2_lo, 1)

            def split_act(t):
                dve.wait_ge(silu_done, t.n + 1)
                if t.c >= 1:
                    dve.wait_ge(down_done, t.n)
                nc.vector.tensor_copy(act_p[:, 0], act_f[:]).then_inc(act_hi, 1)
                dve.wait_ge(act_hi, t.n + 1)
                nc.vector.tensor_tensor(act_p[:, 1], act_f[:], act_p[:, 0].bitcast(F32), ALU.subtract).then_inc(act_lo, 1)

            def add(t):
                dve.wait_ge(down_done, t.n + 1)
                if t.c >= 1:
                    dve.wait_ge(added, t.n)
                for j in range(QT):
                    last = nc.vector.scalar_tensor_tensor(x_res[:, j, :], y_ps[t.slot][:, j, :], share[:, j, bass.ds(t.n, 1)],
                                                          x_res[:, j, :], ALU.mult, ALU.add)
                last.then_inc(added, 1)

            def turn(t):
                lo1(t + 1)
                add(t + -1)
                split_act(t)
                lo2(t + 1)

            dve.wait_ge(zt_done, 1)
            nc.vector.tensor_copy(zt[:], y_ps[0][:]).then_inc(zt_kept, 1)
            dve.wait_ge(zt_kept, 1)
            link(nc.vector.tensor_copy(zp[:, :, 0, :], zt[:]))
            nc.vector.tensor_tensor(zp[:, :, 1, :], zt[:], zp[:, :, 0, :].bitcast(F32), ALU.subtract).then_inc(zp_done, 1)
            lo1(Turn(0, 2))
            dve.wait_ge(logits_done, 1)
            for j in range(QT):
                link(nc.vector.max(logit_top[:, j, :], gate_ps[:, j * E:(j + 1) * E]))
            nc.vector.tensor_scalar_mul(neg_top[:], logit_top[:, :, 0], -1.0).then_inc(neg_done, 1)
            dve.wait_ge(numbered, 1)
            link(nc.vector.tensor_copy(number_f[:], number[:]))
            dve.wait_ge(gate_exp_done, 1)
            link(nc.vector.reciprocal(gate_inv[:], gate_sum[:]))
            for j in range(QT):
                link(nc.vector.tensor_scalar(gate[:, j, :], gate_exp[:, j, :], gate_inv[:, j:j + 1], None, ALU.mult))
                link(nc.vector.max(best[:, j, :], gate[:, j, :]))
                link(nc.vector.max_index(best_at[:, j, :], best[:, j, :], gate[:, j, :]))
            link(nc.vector.tensor_copy(best_f[:], best_at[:, :, 0:2]))
            link(nc.vector.tensor_tensor(two[:, :, 0], best[:, :, 0], best[:, :, 1], ALU.add))
            link(nc.vector.tensor_scalar_add(two[:, :, 0], two[:, :, 0], TOP_EPS))
            link(nc.vector.reciprocal(two[:, :, 1], two[:, :, 0]))
            link(nc.vector.memset(share[:], SHARED))
            for j in range(QT):
                link(nc.vector.tensor_scalar(two[:, j, 2:4], best[:, j, 0:2], two[:, j, 1:2], None, ALU.mult))
                for c in range(2):
                    link(nc.vector.tensor_scalar(picked[:, j, c, :], number_f[:], best_f[:, j, c:c + 1],
                                                 two[:, j, 2 + c:3 + c], ALU.is_equal, ALU.mult))
                last = nc.vector.tensor_tensor(share[:, j, 0:E], picked[:, j, 0, :], picked[:, j, 1, :], ALU.add)
            last.then_inc(share_done, 1)
            dve.wait_ge(share_t_done, 1)
            nc.vector.tensor_copy(share_t[:].rearrange("e (j n) -> e j n", j=QT), bias_ps[0:E1, :, 0:P]).then_inc(share_t_kept, 1)
            dve.wait_ge(bias_done, 1)
            link(nc.vector.tensor_tensor(x_res[:], x_res[:], bias_ps[:], ALU.add))
            lo2(Turn(0, 2))
            lo1(Turn(1, 2))
            split_act(Turn(0, 2))
            lo2(Turn(1, 2))
            run(dve, turn, 1, E1 - 1, 2)
            add(Turn(E1 - 2, 2))
            split_act(Turn(E1 - 1, 2))
            add(Turn(E1 - 1, 2))


def store_result(nc, sem, out, x_res):
    with ExitStack() as ctx:
        stored = sem("stored")
        block = ctx.enter_context(nc.Block())

        @block.sync
        def _(sp):
            sp.dma_start(out.rearrange("o (j p) d -> p (o j) d", p=P), x_res[:]).then_inc(stored, 16)
            sp.wait_ge(stored, 16)


def kernel(**inputs):
    import numpy as np
    import concourse.bacc as bacc
    from concourse.bass_utils import run_bass_kernel_spmd

    arrays = laid_out(np, inputs)
    nc = bacc.Bacc("TRN2", target_bir_lowering=False, num_devices=1)
    aps = {name: nc.dram_tensor("in_" + name, x.shape, mybir.dt.from_np(x.dtype), kind="ExternalInput").ap()
           for name, x in arrays.items()}
    out = nc.dram_tensor("out", (1, NQ, D), F32, kind="ExternalOutput").ap()
    perceiver_kernel(nc, aps, out)
    result = run_bass_kernel_spmd(nc, [{"in_" + name: x for name, x in arrays.items()}], core_ids=[0])
    return result.results[0]["out"]


def laid_out(np, inputs):
    arrays = {name: np.ascontiguousarray(x) for name, x in inputs.items()}
    arrays["mask_BxS2_bf1"] = np.ascontiguousarray(arrays["mask_BxS2_bf1"].reshape(CT, P).T)
    for name in ("Wq", "Wk", "Wv", "Wo", "Wfc", "proj"):
        arrays["L0_attn_" + name] = np.ascontiguousarray(arrays["L0_attn_" + name].T)
    for name in ("W1", "b1", "W2", "b2"):
        own, shared = arrays.pop("L0_ffn_" + name), arrays.pop(f"L0_ffn_{name[0]}s{name[1]}")
        arrays["ffn_" + name] = np.concatenate([own, shared[None]])
    return arrays
```

```python
from contextlib import ExitStack

import concourse.bass as bass
from concourse import mybir

ALU = mybir.AluOpType
ACT = mybir.ActivationFunctionType
AX_X = mybir.AxisListType.X
F32 = mybir.dt.float32
F32R = mybir.dt.float32r
U32 = mybir.dt.uint32

P = 128
D = 256
KD = D // P
NQ = 256
QT = NQ // P
NCTX = 4096
CT = NCTX // P
NT = CT + QT
H = 16
DH = 64
INNER = H * DH
HQ = 4
NQUAD = H // HQ
QW = HQ * DH
NTILES = NQUAD * NT
GT = 4
NG = CT // GT
LN_EPS = 1e-5
RMS_FLOOR = 1e-8
EXP_ROOM = 70.0

DHP = 16
M = 44
PAIR = 2 * M
NPAIR = H // 2
VW = DHP + 1
FEAT_EPS = 1e-4

E = 8
F = 1024
FT = F // P
SHARED = 0.1
TOP_EPS = 1e-9
NORM_LINKS = 2


class Turn:

    def __init__(self, c, per, i=None):
        self.c, self.per, self.i = c, per, i

    def __add__(self, k):
        return Turn(self.c + k, self.per, self.i)

    @property
    def n(self):
        return self.c if self.i is None else self.i * self.per + self.c

    @property
    def slot(self):
        return self.c % self.per

    @property
    def lap(self):
        return self.c // self.per if self.i is None else self.i + self.c // self.per


def run(eng, body, first, end, per):
    turns = (end - first) // per
    if turns > 1:
        with eng.Fori(0, turns) as i:
            for c in range(per):
                body(Turn(first + c, per, i))
        first += turns * per
    for c in range(first, end):
        body(Turn(c, per))


def perceiver_kernel(nc, a, out, only_attention=False):
    xn_dram = nc.dram_tensor("xn_parts", (NT, P, KD * 2 * P), F32).ap()

    with ExitStack() as outer:
        def sem(name):
            return outer.enter_context(nc.semaphore(name))

        def keep(name, shape, dt=F32):
            return outer.enter_context(nc.sbuf_tensor(name, shape, dt))

        x_res = keep("x_res", [P, QT, D])
        ident = keep("ident", [P, P])
        ones = keep("ones", [P, P])
        neg_half = keep("neg_half", [P, QT * H])

        with ExitStack() as scope:
            def stay(name, shape, dt=F32):
                return scope.enter_context(nc.sbuf_tensor(name, shape, dt))

            attn_out = stay("attn_out", [P, NQUAD, HQ * NQ])
            weight_sum = stay("weight_sum", [P, NQUAD, HQ * NQ])
            with ExitStack() as inner:
                def hold(name, shape, dt=F32):
                    return inner.enter_context(nc.sbuf_tensor(name, shape, dt))

                wkv = hold("wkv", [P, NQUAD, KD, 2, 2 * QW], F32R)
                q_parts = hold("q_parts", [P, H, 2, NQ], F32R)
                score_bias = hold("score_bias", [P, NT])
                prepare(nc, sem, a, xn_dram, x_res, ident, ones, neg_half, wkv, q_parts, score_bias, weight_sum)
                attention(nc, sem, xn_dram, ident, neg_half, wkv, q_parts, score_bias, attn_out, weight_sum)
            attention_output(nc, sem, a, x_res, ones, attn_out, weight_sum)
        if not only_attention:
            performer(nc, sem, a, x_res, ident, neg_half)
            experts(nc, sem, a, x_res, ident, neg_half)
        store_result(nc, sem, out, x_res)


def prepare(nc, sem, a, xn_dram, x_res, ident, ones, neg_half, wkv, q_parts, score_bias, weight_sum):
    groups = NG + 1
    ctx_rows = a["ctx_1024"].rearrange("o (g j p) d -> g p (o j) d", p=P, j=GT)
    with ExitStack() as ctx:
        def sb(name, shape, dt=F32):
            return ctx.enter_context(nc.sbuf_tensor("p_" + name, shape, dt))

        def ring(n, name, shape, dt=F32):
            return [sb(f"{name}{b}", shape, dt) for b in range(n)]

        rows = ring(3, "rows", [P, GT, D])
        stats = ring(2, "stats", [P, GT, 6])
        mean_var = ring(2, "mean_var", [P, GT, 2])
        var_eps = ring(2, "var_eps", [P, GT])
        rstd = ring(2, "rstd", [P, GT])
        first_stats, first_mv = sb("first_stats", [P, QT, 6]), sb("first_mv", [P, QT, 2])
        first_var, first_rstd = sb("first_var", [P, QT]), sb("first_rstd", [P, QT])
        z = ring(2, "z", [P, GT, D])
        u = ring(2, "u", [P, KD, GT, P])
        parts = ring(2, "parts", [P, GT, KD, 2, P], F32R)
        gains = sb("gains", [P, 2, 2, KD])
        w_raw = ring(2, "w_raw", [P, KD, 2 * QW])
        wq_raw = sb("wq_raw", [P, KD, INNER])
        wq = sb("wq", [P, KD, 2, INNER], F32R)
        gq = sb("gq", [P, 2, DH])
        gqk = sb("gqk", [P, DH])
        gq_col = sb("gq_col", [P, 2])
        gqk_col = sb("gqk_col", [P, 1])
        bound = sb("bound", [P, DH + 2])
        mask_raw = sb("mask_raw", [P, CT], mybir.dt.uint8)
        mask_f = sb("mask_f", [P, CT])
        q_sq = sb("q_sq", [P, H, DH])
        q_ss, q_ms, q_rms = sb("q_ss", [P, QT, H]), sb("q_ms", [P, QT, H]), sb("q_rms", [P, QT, H])
        qn = sb("qn", [P, QT, H, 2, DH])
        zt_ps = [ctx.enter_context(nc.psum_tensor(f"p_zt_ps{b}", [P, KD, GT * P], F32)) for b in range(2)]
        q_ps = ctx.enter_context(nc.psum_tensor("p_q_ps", [P, QT, INNER], F32))

        x_in, gains_in, gq_in, mask_in, wq_in = sem("x_in"), sem("gains_in"), sem("gq_in"), sem("mask_in"), sem("wq_in")
        rows_in, w_in = [sem(f"rows_in{b}") for b in range(3)], [sem(f"w_in{b}") for b in range(2)]
        parts_out = [sem(f"parts_out{b}") for b in range(2)]
        ident_zeroed, const_done, ident_done = sem("ident_zeroed"), sem("const_done"), sem("ident_done")
        first_eps, first_root, first_done = sem("first_eps"), sem("first_root"), sem("first_done")
        own, stats_done, aggr_done, eps_done, root_done = (
            sem("p_own"), sem("stats_done"), sem("aggr_done"), sem("eps_done"), sem("root_done"))
        z_done, zt_done, u_done, hi_done, lo_done = sem("z_done"), sem("zt_done"), sem("u_done"), sem("hi_done"), sem("lo_done")
        w_hi, w_lo, wq_hi, wq_lo = sem("w_hi"), sem("w_lo"), sem("wq_hi"), sem("wq_lo")
        q_done, q_sq_done, q_ss_done, q_ms_done, q_rms_done, qn_done = (
            sem("q_done"), sem("q_sq_done"), sem("q_ss_done"), sem("q_ms_done"), sem("q_rms_done"), sem("qn_done"))
        qt_done, qt_hi, qt_lo, col_done = sem("qt_done"), sem("qt_hi"), sem("qt_lo"), sem("col_done")

        def tiles_of(n):
            return QT if n == 0 else GT

        block = ctx.enter_context(nc.Block())

        @block.sync
        def _(sp):
            sp.dma_start(x_res[:], a["x"].rearrange("o (j p) d -> p (o j) d", p=P)).then_inc(x_in, 16)
            sp.dma_start(rows[1][:], ctx_rows[0]).then_inc(rows_in[1], 16)
            sp.dma_start(rows[2][:], ctx_rows[1]).then_inc(rows_in[2], 16)
            sp.dma_start(rows[0][:], ctx_rows[2]).then_inc(rows_in[0], 16)
            for n in range(groups):
                if n >= 1 and n + 3 < groups:
                    sp.wait_ge(z_done, n + 1)
                    sp.dma_start(rows[n % 3][:], ctx_rows[n + 2]).then_inc(rows_in[n % 3], 16)
                t, first = tiles_of(n), CT if n == 0 else (n - 1) * GT
                sp.wait_ge(lo_done, n + 1)
                sp.dma_start(xn_dram[first:first + t, :, :].rearrange("t p n -> p t n"),
                             parts[n % 2][:, 0:t].bitcast(F32).rearrange("p t k s n -> p t (k s n)")).then_inc(parts_out[n % 2], 16)
            for b in range(2):
                sp.wait_ge(parts_out[b], 16 * len(range(b, groups, 2)))

        @block.gpsimd
        def _(pool):
            nc.gpsimd.memset(ident[:], 0.0).then_inc(ident_zeroed, 1)
            nc.gpsimd.memset(neg_half[:], -0.5).then_inc(const_done, 1)
            nc.gpsimd.memset(ones[:], 1.0).then_inc(const_done, 1)
            pool.wait_ge(ident_zeroed, 1)
            nc.gpsimd.affine_select(out=ident[:], in_=ident[:], compare_op=ALU.not_equal, fill=1.0,
                                    base=0, pattern=[[-1, P]], channel_multiplier=1).then_inc(ident_done, 1)
            pool.wait_ge(const_done, 2)
            pool.wait_ge(first_eps, 1)
            nc.gpsimd.tensor_tensor(first_rstd[:], first_var[:], neg_half[:, 0:QT], ALU.pow).then_inc(first_root, 1)

            def root(n):
                t = tiles_of(n)
                pool.wait_ge(eps_done, n + 1)
                nc.gpsimd.tensor_tensor(rstd[n % 2][:, 0:t], var_eps[n % 2][:, 0:t], neg_half[:, 0:t], ALU.pow).then_inc(root_done, 1)

            def weights_lo(quad):
                pool.wait_ge(w_hi, quad + 1)
                nc.gpsimd.tensor_tensor(wkv[:, quad, :, 1, :], w_raw[quad % 2][:], wkv[:, quad, :, 0, :].bitcast(F32),
                                        ALU.subtract).then_inc(w_lo, 1)

            for n in range(5):
                root(n)
            for j in range(QT):
                pool.wait_ge(q_ms_done, j + 1)
                nc.gpsimd.tensor_tensor(q_rms[:, j, :], q_ms[:, j, :], neg_half[:, 0:H], ALU.pow).then_inc(q_rms_done, 1)
                root(5 + j)
            for n in range(7, groups):
                root(n)
                weights_lo(n - 7)
            for quad in range(groups - 7, NQUAD):
                weights_lo(quad)

        @block.scalar
        def _(act):
            act.dma_start(wq_raw[:], a["L0_xattn_Wq"].rearrange("(k p) n -> p k n", p=P)).then_inc(wq_in, 16)
            with nc.allow_non_contiguous_dma(reason="a vector onto partitions"):
                for n, name in enumerate(("ln_l_g", "ln_l_b", "ln_x_g", "ln_x_b")):
                    act.dma_start(gains[:, n // 2, n % 2, :], a["L0_xattn_" + name].rearrange("(k p) -> p k", p=P)).then_inc(gains_in, 16)
                for n, name in enumerate(("qn_g", "kn_g")):
                    act.dma_start(gq[:, n, :], a["L0_xattn_" + name].partition_broadcast(P)).then_inc(gq_in, 16)
                    for c in range(2):
                        act.dma_start(gq_col[c * DH:(c + 1) * DH, n:n + 1], a["L0_xattn_" + name].rearrange("(p o) -> p o", o=1)).then_inc(gq_in, 16)
            act.dma_start(mask_raw[:], a["mask_BxS2_bf1"]).then_inc(mask_in, 16)
            w_view = a["L0_xattn_Wkv"].rearrange("(k p) (s q n) -> q s p k n", p=P, s=2, q=NQUAD)

            def load_weights(quad):
                for s in range(2):
                    act.dma_start(w_raw[quad % 2][:, :, s * QW:(s + 1) * QW], w_view[quad, s]).then_inc(w_in[quad % 2], 16)

            load_weights(0)
            load_weights(1)

            def affine_and_hi(n):
                t, which = tiles_of(n), 0 if n == 0 else 1
                act.wait_ge(zt_done, n + 1)
                if n >= 2:
                    act.wait_ge(lo_done, n - 1)
                for k in range(KD):
                    last = nc.scalar.activation(u[n % 2][:, k, 0:t].rearrange("p t n -> p (t n)"), zt_ps[n % 2][:, k, 0:t * P],
                                                ACT.Identity, scale=gains[:, which, 0, k:k + 1], bias=gains[:, which, 1, k:k + 1])
                last.then_inc(u_done, 1)
                act.wait_ge(u_done, n + 1)
                if n >= 2:
                    act.wait_ge(parts_out[n % 2], 16 * (n // 2))
                for k in range(KD):
                    last = nc.scalar.activation(parts[n % 2][:, 0:t, k, 0, :], u[n % 2][:, k, 0:t], ACT.Copy)
                last.then_inc(hi_done, 1)

            def squares(j):
                act.wait_ge(q_done, j + 1)
                if j:
                    act.wait_ge(q_ss_done, j)
                nc.scalar.activation(q_sq[:].rearrange("p h d -> p (h d)"), q_ps[:, j, :], ACT.Square,
                                     scale=DH ** -0.5).then_inc(q_sq_done, 1)

            def weights_hi(quad):
                act.wait_ge(w_in[quad % 2], 32 * (quad // 2 + 1))
                nc.scalar.activation(wkv[:, quad, :, 0, :], w_raw[quad % 2][:], ACT.Copy).then_inc(w_hi, 1)

            def keep_qt(c):
                act.wait_ge(qt_done, c + 1)
                nc.scalar.activation(q_parts[:, 4 * c:4 * c + 4, 0, :], q_ps[:, c % 2, :].rearrange("p (h q) -> p h q", h=4),
                                     ACT.Copy, scale=gqk_col[:]).then_inc(qt_hi, 1)

            act.wait_ge(wq_in, 16)
            nc.scalar.activation(wq[:, :, 0, :], wq_raw[:], ACT.Copy).then_inc(wq_hi, 1)
            act.wait_ge(gains_in, 64)
            affine_and_hi(0)
            affine_and_hi(1)
            weights_hi(0)
            affine_and_hi(2)
            squares(0)
            affine_and_hi(3)
            squares(1)
            affine_and_hi(4)
            weights_hi(1)
            affine_and_hi(5)
            affine_and_hi(6)
            act.wait_ge(col_done, 1)
            keep_qt(0)
            affine_and_hi(7)
            keep_qt(1)
            keep_qt(2)
            affine_and_hi(8)
            keep_qt(3)
            for quad in range(2, NQUAD):
                act.wait_ge(w_lo, quad - 1)
                load_weights(quad)
            for quad in range(2, NQUAD):
                weights_hi(quad)

        @block.vector
        def _(dve):
            count = [0]

            def link(ins):
                count[0] += 1
                ins.then_inc(own, 1)
                dve.wait_ge(own, count[0])

            def statistics(n, src):
                b, t = n % 2, tiles_of(n)
                for j in range(t):
                    last = nc.vector.bn_stats(stats[b][:, j, :], src[:, j, :])
                last.then_inc(stats_done, 1)
                dve.wait_ge(stats_done, n + 1)
                for j in range(t):
                    last = nc.vector.bn_aggr(mean_var[b][:, j, :], stats[b][:, j, :])
                last.then_inc(aggr_done, 1)
                dve.wait_ge(aggr_done, n + 1)
                nc.vector.tensor_scalar_add(var_eps[b][:, 0:t], mean_var[b][:, 0:t, 1], LN_EPS).then_inc(eps_done, 1)

            def normalise(n, src):
                b = n % 2
                dve.wait_ge(root_done, n + 1)
                if n >= 2:
                    dve.wait_ge(zt_done, n - 1)
                for j in range(tiles_of(n)):
                    last = nc.vector.tensor_scalar(z[b][:, j, :], src[:, j, :], mean_var[b][:, j, 0:1],
                                                   rstd[b][:, j:j + 1], ALU.subtract, ALU.mult)
                last.then_inc(z_done, 1)

            def lo(n):
                b, t = n % 2, tiles_of(n)
                dve.wait_ge(hi_done, n + 1)
                for k in range(KD):
                    last = nc.vector.tensor_tensor(parts[b][:, 0:t, k, 1, :], u[b][:, k, 0:t], parts[b][:, 0:t, k, 0, :].bitcast(F32), ALU.subtract)
                last.then_inc(lo_done, 1)

            def arrived(n):
                dve.wait_ge(rows_in[n % 3], 16 * (n // 3 + (0 if n % 3 == 0 else 1)))
                return rows[n % 3]

            def mean_squares(j):
                dve.wait_ge(q_sq_done, j + 1)
                nc.vector.reduce_sum(q_ss[:, j, :], q_sq[:], AX_X).then_inc(q_ss_done, 1)
                dve.wait_ge(q_ss_done, j + 1)
                nc.vector.tensor_scalar_max(q_ms[:, j, :], q_ss[:, j, :], RMS_FLOOR ** 2).then_inc(q_ms_done, 1)

            def scale_queries(j):
                dve.wait_ge(q_rms_done, j + 1)
                heads = [P, H, DH]
                for c in range(2):
                    last = nc.vector.tensor_tensor(qn[:, j, :, c, :], q_ps[:, j, :].rearrange("p (h d) -> p h d", d=DH),
                                                   q_rms[:, j, :].unsqueeze(2).to_broadcast(heads), ALU.mult)
                last.then_inc(qn_done, 1)

            def qt_lo_part(c):
                dve.wait_ge(qt_hi, c + 1)
                nc.vector.scalar_tensor_tensor(q_parts[:, 4 * c:4 * c + 4, 1, :], q_ps[:, c % 2, :].rearrange("p (h q) -> p h q", h=4),
                                               gqk_col[:], q_parts[:, 4 * c:4 * c + 4, 0, :].bitcast(F32),
                                               ALU.mult, ALU.subtract).then_inc(qt_lo, 1)

            dve.wait_ge(x_in, 16)
            for j in range(QT):
                link(nc.vector.bn_stats(first_stats[:, j, :], x_res[:, j, :]))
                link(nc.vector.bn_aggr(first_mv[:, j, :], first_stats[:, j, :]))
            nc.vector.tensor_scalar_add(first_var[:], first_mv[:, :, 1], LN_EPS).then_inc(first_eps, 1)
            dve.wait_ge(first_root, 1)
            for j in range(QT):
                link(nc.vector.tensor_scalar(z[1][:, j, :], x_res[:, j, :], first_mv[:, j, 0:1],
                                             first_rstd[:, j:j + 1], ALU.subtract, ALU.mult))
            statistics(0, z[1])
            statistics(1, arrived(1))
            normalise(0, z[1])
            link(nc.vector.memset(score_bias[:, CT:NT], 0.0))
            normalise(1, rows[1])
            dve.wait_ge(wq_hi, 1)
            nc.vector.tensor_tensor(wq[:, :, 1, :], wq_raw[:], wq[:, :, 0, :].bitcast(F32), ALU.subtract).then_inc(wq_lo, 1)
            lo(0)
            statistics(2, arrived(2))
            lo(1)
            normalise(2, rows[2])
            dve.wait_ge(gq_in, 16 * 6)
            nc.vector.scalar_tensor_tensor(gqk_col[:], gq_col[:, 0:1], DH ** -0.5, gq_col[:, 1:2], ALU.mult, ALU.mult).then_inc(col_done, 1)
            link(nc.vector.scalar_tensor_tensor(gqk[:], gq[:, 0, :], DH ** -0.5, gq[:, 1, :], ALU.mult, ALU.mult))
            statistics(3, arrived(3))
            link(nc.vector.scalar_tensor_tensor(bound[:, 0:DH], gqk[:], -1.0, gqk[:], ALU.mult, ALU.max))
            lo(2)
            normalise(3, rows[0])
            mean_squares(0)
            statistics(4, arrived(4))
            lo(3)
            mean_squares(1)
            normalise(4, rows[1])
            link(nc.vector.reduce_max(bound[:, DH:DH + 1], bound[:, 0:DH], AX_X))
            statistics(5, arrived(5))
            scale_queries(0)
            lo(4)
            scale_queries(1)
            normalise(5, rows[2])
            link(nc.vector.tensor_scalar(bound[:, DH + 1:DH + 2], bound[:, DH:DH + 1], float(DH), -EXP_ROOM, ALU.mult, ALU.add))
            statistics(6, arrived(6))
            link(nc.vector.tensor_scalar(bound[:, DH:DH + 1], bound[:, DH + 1:DH + 2], 0.0, -1.0, ALU.max, ALU.mult))
            lo(5)
            normalise(6, rows[0])
            dve.wait_ge(mask_in, 16)
            link(nc.vector.tensor_copy(mask_f[:], mask_raw[:]))
            statistics(7, arrived(7))
            link(nc.vector.tensor_scalar(score_bias[:, 0:CT], mask_f[:], 1e30, -1e30, ALU.mult, ALU.add))
            lo(6)
            qt_lo_part(0)
            normalise(7, rows[1])
            link(nc.vector.tensor_scalar(score_bias[:], score_bias[:], bound[:, DH:DH + 1], None, ALU.add))
            statistics(8, arrived(8))
            lo(7)
            qt_lo_part(1)
            normalise(8, rows[2])
            qt_lo_part(2)
            nc.vector.memset(weight_sum[:], 0.0)
            lo(8)
            qt_lo_part(3)

        @block.tensor
        def _(pe):
            def transposes(n):
                pe.wait_ge(z_done, n + 1)
                if n >= 2:
                    pe.wait_ge(u_done, n - 1)
                for k in range(KD):
                    for j in range(tiles_of(n)):
                        last = nc.tensor.transpose(zt_ps[n % 2][:, k, j * P:(j + 1) * P],
                                                   z[n % 2][:, j, k * P:(k + 1) * P], ident[:])
                last.then_inc(zt_done, 1)

            pe.wait_ge(ident_done, 1)
            transposes(0)
            transposes(1)
            pe.wait_ge(lo_done, 1)
            pe.wait_ge(wq_lo, 1)
            for j in range(QT):
                for c in range(INNER // 512):
                    last = part_products(nc, q_ps[:, j, c * 512:(c + 1) * 512],
                                         lambda k, s: parts[0][:, j, k, s, :],
                                         lambda k, s: wq[:, k, s, c * 512:(c + 1) * 512])
                last.then_inc(q_done, 1)
            for n in range(2, 7):
                transposes(n)

            def transpose_queries(c):
                if c >= 2:
                    pe.wait_ge(qt_lo, c - 1)
                for h in range(4):
                    for j in range(QT):
                        at = h * NQ + j * P
                        last = nc.tensor.transpose(q_ps[:, c % 2, at:at + P], qn[:, j, 4 * c + h].rearrange("p c d -> p (c d)"), ident[:])
                last.then_inc(qt_done, 1)

            pe.wait_ge(qn_done, QT)
            transpose_queries(0)
            transpose_queries(1)
            transposes(7)
            transpose_queries(2)
            transposes(8)
            transpose_queries(3)


def part_products(nc, out, stationary, moving, kd=KD):
    terms = [(k, s, m) for k in range(kd) for s, m in ((0, 0), (0, 1), (1, 0))]
    for n, (k, s, m) in enumerate(terms):
        last = nc.tensor.matmul(out, stationary(k, s), moving(k, m), start=n == 0, stop=n == len(terms) - 1)
    return last


def attention(nc, sem, xn_dram, ident, neg_half, wkv, q_parts, score_bias, attn_out, weight_sum):
    with ExitStack() as ctx:
        def ring(n, name, shape, dt=F32):
            return [ctx.enter_context(nc.sbuf_tensor(f"{name}{b}", shape, dt)) for b in range(n)]

        xn = ring(4, "xn", [P, KD, 2, P], F32R)
        kv = ring(4, "kv", [P, 2 * HQ, 2, DH], F32R)
        k_sq = ring(2, "k_sq", [P, HQ, DH])
        k_ss = ring(4, "k_ss", [P, HQ])
        k_ms = ring(4, "k_ms", [P, HQ])
        k_rms = ring(4, "k_rms", [P, HQ])
        bias_now = ring(4, "bias_now", [P, 1])
        kt = ring(2, "kt", [P, HQ * P], F32R)
        probs = ring(2, "probs", [P, HQ * NQ])
        probs_hi = ring(2, "probs_hi", [P, HQ * NQ], F32R)
        probs_lo = ring(2, "probs_lo", [P, HQ * NQ], F32R)
        kv_ps = ctx.enter_context(nc.psum_tensor("kv_ps", [P, 2 * QW], F32))
        kt_ps = ctx.enter_context(nc.psum_tensor("kt_ps", [P, HQ * P], F32))
        s_ps = [ctx.enter_context(nc.psum_tensor(f"s_ps{b}", [P, HQ * NQ], F32)) for b in range(2)]
        o_ps = ctx.enter_context(nc.psum_tensor("o_ps", [P, HQ * NQ], F32))

        xn_in = [sem(f"xn_in{b}") for b in range(4)]
        kv_done, sq_done, kv_hi, kv_lo = sem("kv_done"), sem("sq_done"), sem("kv_hi"), sem("kv_lo")
        ss_done, ms_done, rms_done, bias_done = sem("ss_done"), sem("ms_done"), sem("rms_done"), sem("bias_done")
        kt_done, kt_kept, s_done, exp_done = sem("kt_done"), sem("kt_kept"), sem("s_done"), sem("exp_done")
        p_hi, p_lo, pv_done, sum_done, out_kept = sem("p_hi"), sem("p_lo"), sem("pv_done"), sem("sum_done"), sem("out_kept")

        block = ctx.enter_context(nc.Block())

        def steps(eng, step):
            for s in (-1, 0, 1, 2):
                step(Turn(s, 4), 0)
            for quad in range(NQUAD):
                first = quad * NT + 3
                with eng.Fori(0, 7) as i:
                    for c in range(4):
                        step(Turn(first + c, 4, i), quad)
                for s in range(first + 28, (quad + 1) * NT + 3 if quad + 1 < NQUAD else NTILES + 2):
                    step(Turn(s, 4), quad)

        def exists(t):
            return 0 <= t.c < NTILES

        def quad_of(t):
            return t.c // NT

        @block.sync
        def _(sp):
            def load(t, quad):
                if t.c >= 4:
                    sp.wait_ge(kv_done, t.n - 3)
                sp.dma_start(xn[t.slot][:].bitcast(F32).rearrange("p k s n -> p (k s n)"),
                             xn_dram[bass.ds((t + -quad * NT).n, 1)].rearrange("t p n -> p (t n)")).then_inc(xn_in[t.slot], 16)

            for quad in range(NQUAD):
                for c in range(4):
                    load(Turn(quad * NT + c, 4), quad)
                run(sp, lambda t: load(t, quad), quad * NT + 4, (quad + 1) * NT, 4)

        @block.tensor
        def _(pe):
            def project(t):
                quad = quad_of(t)
                pe.wait_ge(xn_in[t.slot], (t.lap + 1) * 16)
                if t.c >= 1:
                    pe.wait_ge(kv_lo, t.n)
                part_products(nc, kv_ps[:], lambda k, s: xn[t.slot][:, k, s, :],
                              lambda k, s: wkv[:, quad, k, s, :]).then_inc(kv_done, 1)

            def transpose_k(t):
                pe.wait_ge(kv_lo, t.n + 1)
                if t.c >= 1:
                    pe.wait_ge(kt_kept, t.n)
                for h in range(HQ):
                    last = nc.tensor.transpose(kt_ps[:, h * P:(h + 1) * P],
                                               kv[t.slot][:, h].bitcast(F32).rearrange("p s d -> p (s d)"), ident[:])
                last.then_inc(kt_done, 1)

            def weight_v(t):
                local = t.c % NT
                pe.wait_ge(p_lo, t.n * 2 + 2)
                if local == 0 and t.c:
                    pe.wait_ge(out_kept, t.c // NT)
                b = t.c % 2
                for h in range(HQ):
                    for s, part in enumerate((probs_hi, probs_lo)):
                        last = nc.tensor.matmul(o_ps[:, h * NQ:(h + 1) * NQ],
                                                kv[t.slot][:, HQ + h].rearrange("p s d -> p (s d)"),
                                                part[b][:, h * NQ:(h + 1) * NQ],
                                                start=local == 0 and h % 2 == 0 and s == 0,
                                                stop=local == NT - 1 and s == 1, skip_group_check=True)
                last.then_inc(pv_done, 1)

            def scores(t):
                quad, b = quad_of(t), t.c % 2
                pe.wait_ge(kt_kept, t.n + 1)
                if t.c >= 2:
                    pe.wait_ge(exp_done, t.n * 2 - 2)
                for h in range(HQ):
                    for s in range(2):
                        last = nc.tensor.matmul(s_ps[b][:, h * NQ:(h + 1) * NQ], kt[b][:, h * P:(h + 1) * P],
                                                q_parts[:, quad * HQ + h, s, :], start=s == 0, stop=s == 1)
                    if h % 2:
                        last.then_inc(s_done, 1)

            def step(s, quad):
                if exists(s + 1):
                    project(s + 1)
                if exists(s):
                    scores(s)
                if exists(s + -2):
                    weight_v(s + -2)
                if exists(s + 1):
                    transpose_k(s + 1)

            steps(pe, step)

        @block.scalar
        def _(act):
            def weights(t):
                b = t.c % 2
                act.wait_ge(rms_done, t.n + 1)
                act.wait_ge(bias_done, t.n + 1)
                if t.c >= 2:
                    act.wait_ge(p_lo, t.n * 2 - 2)
                    act.wait_ge(sum_done, t.n - 1)
                for h in range(HQ):
                    if h % 2 == 0:
                        act.wait_ge(s_done, t.n * 2 + (1 + h // 2))
                    last = nc.scalar.activation(probs[b][:, h * NQ:(h + 1) * NQ], s_ps[b][:, h * NQ:(h + 1) * NQ], ACT.Exp,
                                                scale=k_rms[t.slot][:, h:h + 1], bias=bias_now[t.slot][:])
                    if h % 2:
                        last.then_inc(exp_done, 1)

            def keep_kt(t):
                act.wait_ge(kt_done, t.n + 1)
                if t.c >= 2:
                    act.wait_ge(s_done, t.n * 2 - 2)
                nc.scalar.activation(kt[t.c % 2][:], kt_ps[:], ACT.Copy).then_inc(kt_kept, 1)

            def squares_and_hi(t):
                act.wait_ge(kv_done, t.n + 1)
                if t.c >= 2:
                    act.wait_ge(ss_done, t.n - 1)
                nc.scalar.activation(k_sq[t.c % 2][:].rearrange("p h d -> p (h d)"), kv_ps[:, 0:QW], ACT.Square,
                                     scale=DH ** -0.5).then_inc(sq_done, 1)
                if t.c >= 4:
                    act.wait_ge(pv_done, t.n - 3)
                nc.scalar.activation(kv[t.slot][:, :, 0, :], kv_ps[:].rearrange("p (h d) -> p h d", d=DH), ACT.Copy).then_inc(kv_hi, 1)

            def step(s, quad):
                if exists(s + 1):
                    squares_and_hi(s + 1)
                if exists(s):
                    weights(s)
                if exists(s + 1):
                    keep_kt(s + 1)

            steps(act, step)

        @block.vector
        def _(dve):
            def split_weights(t):
                b = t.c % 2
                if t.c >= 2:
                    dve.wait_ge(pv_done, t.n - 1)
                for c in range(2):
                    two = slice(c * 2 * NQ, (c + 1) * 2 * NQ)
                    dve.wait_ge(exp_done, t.n * 2 + (1 + c))
                    nc.vector.tensor_copy(probs_hi[b][:, two], probs[b][:, two]).then_inc(p_hi, 1)
                    dve.wait_ge(p_hi, t.n * 2 + (1 + c))
                    nc.vector.tensor_tensor(probs_lo[b][:, two], probs[b][:, two], probs_hi[b][:, two].bitcast(F32),
                                            ALU.subtract).then_inc(p_lo, 1)

            def split_kv(t):
                dve.wait_ge(kv_hi, t.n + 1)
                nc.vector.tensor_tensor(kv[t.slot][:, :, 1, :], kv_ps[:].rearrange("p (h d) -> p h d", d=DH),
                                        kv[t.slot][:, :, 0, :].bitcast(F32), ALU.subtract).then_inc(kv_lo, 1)
                dve.wait_ge(sq_done, t.n + 1)
                if t.c >= 4:
                    dve.wait_ge(rms_done, t.n - 3)
                nc.vector.reduce_sum(k_ss[t.slot][:], k_sq[t.c % 2][:], AX_X).then_inc(ss_done, 1)
                dve.wait_ge(ss_done, t.n + 1)
                nc.vector.tensor_scalar_max(k_ms[t.slot][:], k_ss[t.slot][:], RMS_FLOOR ** 2).then_inc(ms_done, 1)

            def step(s, quad):
                if exists(s + -1):
                    split_weights(s + -1)
                if exists(s + 1):
                    split_kv(s + 1)
                if exists(s + -2) and (s.c - 2) % NT == NT - 1:
                    dve.wait_ge(pv_done, s.c - 1)
                    nc.vector.tensor_copy(attn_out[:, (s.c - 2) // NT, :], o_ps[:]).then_inc(out_kept, 1)

            steps(dve, step)

        @block.gpsimd
        def _(pool):
            def sum_weights(t):
                pool.wait_ge(exp_done, t.n * 2 + 2)
                if t.c >= 1:
                    pool.wait_ge(sum_done, t.n)
                total = weight_sum[:, quad_of(t), :]
                nc.gpsimd.tensor_tensor(total, total, probs[t.c % 2][:], ALU.add).then_inc(sum_done, 1)

            def root(t):
                pool.wait_ge(ms_done, t.n + 1)
                if t.c >= 4:
                    pool.wait_ge(exp_done, t.n * 2 - 6)
                nc.gpsimd.tensor_tensor(k_rms[t.slot][:], k_ms[t.slot][:], neg_half[:, 0:HQ], ALU.pow).then_inc(rms_done, 1)
                nc.gpsimd.tensor_copy(bias_now[t.slot][:], score_bias[:, bass.ds((t + -quad_of(t) * NT).n, 1)]).then_inc(bias_done, 1)

            def step(s, quad):
                if exists(s + -1):
                    sum_weights(s + -1)
                if exists(s + 1):
                    root(s + 1)

            steps(pool, step)


def attention_output(nc, sem, a, x_res, ones, attn_out, weight_sum):
    with ExitStack() as ctx:
        wout = ctx.enter_context(nc.sbuf_tensor("wout", [P, H, D], F32))
        bout = ctx.enter_context(nc.sbuf_tensor("bout", [P, D], F32))
        inverse = [ctx.enter_context(nc.sbuf_tensor(f"inverse{b}", [P, HQ * NQ], F32)) for b in range(2)]
        sum_ps = [ctx.enter_context(nc.psum_tensor(f"sum_ps{b}", [P, HQ * NQ], F32)) for b in range(2)]
        y_ps = ctx.enter_context(nc.psum_tensor("y_ps", [P, QT, 512], F32))
        wout_in, bout_in = sem("wout_in"), sem("bout_in")
        sum_ready, inverse_done, scaled, y_done, own = sem("sum_ready"), sem("inverse_done"), sem("scaled"), sem("y_done"), sem("y_own")

        block = ctx.enter_context(nc.Block())

        @block.sync
        def _(sp):
            rows = a["L0_xattn_Wout"].rearrange("(h d) n -> d h n", d=DH)
            for c in range(2):
                sp.dma_start(wout[c * DH:(c + 1) * DH], rows).then_inc(wout_in, 16)
            sp.dma_start(bout[:], a["L0_xattn_bout"].partition_broadcast(P)).then_inc(bout_in, 16)

        @block.tensor
        def _(pe):
            for quad in range(NQUAD):
                if quad >= 2:
                    pe.wait_ge(inverse_done, quad - 1)
                for c in range(2):
                    last = nc.tensor.matmul(sum_ps[quad % 2][:, c * 512:(c + 1) * 512], ones[:],
                                            weight_sum[:, quad, c * 512:(c + 1) * 512], start=True, stop=True)
                last.then_inc(sum_ready, 1)
            pe.wait_ge(wout_in, 32)
            for h in range(H):
                if h % HQ == 0:
                    pe.wait_ge(scaled, h // HQ + 1)
                for j in range(QT):
                    at = (h % HQ) * NQ + j * P
                    last = nc.tensor.matmul(y_ps[:, j, 0:D], attn_out[:, h // HQ, at:at + P], wout[:, h, :],
                                            start=h == 0, stop=h == H - 1)
            last.then_inc(y_done, 1)

        @block.vector
        def _(dve):
            for quad in range(NQUAD):
                dve.wait_ge(sum_ready, quad + 1)
                nc.vector.reciprocal(inverse[quad % 2][:], sum_ps[quad % 2][:]).then_inc(inverse_done, 1)
                dve.wait_ge(inverse_done, quad + 1)
                nc.vector.tensor_tensor(attn_out[:, quad, :], attn_out[:, quad, :], inverse[quad % 2][:], ALU.mult).then_inc(scaled, 1)
            dve.wait_ge(bout_in, 16)
            nc.vector.tensor_tensor(x_res[:], x_res[:], bout[:].unsqueeze(1).to_broadcast([P, QT, D]), ALU.add).then_inc(own, 1)
            dve.wait_ge(own, 1)
            dve.wait_ge(y_done, 1)
            nc.vector.tensor_tensor(x_res[:], x_res[:], y_ps[:, :, 0:D], ALU.add).then_inc(own, 1)


def row_norm(nc, dve, own, eps_done, root_done, src, dst, stats, mean_var, var_eps, rstd):
    for j in range(QT):
        last = nc.vector.bn_stats(stats[:, j, :], src[:, j, :])
    last.then_inc(own, 1)
    dve.wait_ge(own, 1)
    for j in range(QT):
        last = nc.vector.bn_aggr(mean_var[:, j, :], stats[:, j, :])
    last.then_inc(own, 1)
    dve.wait_ge(own, 2)
    nc.vector.tensor_scalar_add(var_eps[:], mean_var[:, :, 1], LN_EPS).then_inc(eps_done, 1)
    dve.wait_ge(root_done, 1)
    for j in range(QT):
        last = nc.vector.tensor_scalar(dst[:, j, :], src[:, j, :], mean_var[:, j, 0:1], rstd[:, j:j + 1],
                                       ALU.subtract, ALU.mult)
    return last


def performer(nc, sem, a, x_res, ident, neg_half):
    HH = H // KD
    with ExitStack() as ctx:
        def sb(name, shape, dt=F32):
            return ctx.enter_context(nc.sbuf_tensor("f_" + name, shape, dt))

        w = {name: sb(name, [P, KD, D]) for name in ("Wq", "Wk", "Wv", "Wo", "Wfc")}
        columns = {name: sb(name, [P, KD]) for name in ("bq", "bk", "bo")}
        spread = {name: sb(name, [P, D]) for name in ("bv", "bfc")}
        stats, mean_var, var_eps, rstd = sb("stats", [P, QT, 6]), sb("mean_var", [P, QT, 2]), sb("var_eps", [P, QT]), sb("rstd", [P, QT])
        z, zt = sb("z", [P, QT, D]), sb("zt", [P, KD, NQ])
        proj_bd = sb("proj_bd", [P, HH, M])
        diag_bd = sb("diag_bd", [P, HH])
        pair_mask = sb("pair_mask", [PAIR, 2, VW])
        qk_t = sb("qk_t", [P, 2, KD, NQ])
        qk_sq = sb("qk_sq", [P, 2, KD, NQ])
        v_one = sb("v_one", [P, QT, H, VW])
        top = sb("top", [P, 2, QT, KD, HH])
        top_key = sb("top_key", [P, 2, H])
        less = sb("less", [P, 2, QT, KD, HH])
        feats = sb("feats", [P, 2, QT, KD * HH * M])
        kv_ctx = sb("kv_ctx", [PAIR, NPAIR, 2 * VW])
        qp_t = sb("qp_t", [PAIR, NPAIR * NQ])
        inverse = sb("inverse", [P, QT, H])
        o, o_t, h_t = sb("o", [P, QT, H, DHP]), sb("o_t", [P, KD, NQ]), sb("h_t", [P, KD, NQ])
        y = sb("y", [P, QT, D])
        ps = ctx.enter_context(nc.psum_tensor("f_ps", [P, 8, 512], F32))

        w_in, bias_in, proj_in = sem("f_w_in"), sem("f_bias_in"), sem("f_proj_in")
        blocks_started, blocks_zeroed, blocks_half, blocks_done = (
            sem("f_blocks_started"), sem("f_blocks_zeroed"), sem("f_blocks_half"), sem("f_blocks_done"))
        own, eps_done, root_done, z_done, zt_done, zt_kept = (
            sem("f_own"), sem("f_eps_done"), sem("f_root_done"), sem("f_z_done"), sem("f_zt_done"), sem("f_zt_kept"))
        qkv_done, qk_kept, v_kept, proj_scaled = sem("f_qkv_done"), sem("f_qk_kept"), sem("f_v_kept"), sem("f_proj_scaled")
        exponents_done, key_top, key_top_all = sem("f_exponents_done"), sem("f_key_top"), sem("f_key_top_all")
        less_done, exp_done, feats_done = sem("f_less_done"), sem("f_exp_done"), sem("f_feats_done")
        context_done, qp_done, context_kept, qp_kept = (
            sem("f_context_done"), sem("f_qp_done"), sem("f_context_kept"), sem("f_qp_kept"))
        o_ready, o_kept, ot_done, ot_kept = sem("f_o_ready"), sem("f_o_kept"), sem("f_ot_done"), sem("f_ot_kept")
        ht_done, ht_kept, fc_done = sem("f_ht_done"), sem("f_ht_kept"), sem("f_fc_done")

        block = ctx.enter_context(nc.Block())

        @block.sync
        def _(sp):
            for name, tile in w.items():
                sp.dma_start(tile[:], a["L0_attn_" + name].rearrange("(k p) n -> p k n", p=P)).then_inc(w_in, 16)
            with nc.allow_non_contiguous_dma(reason="a vector onto partitions"):
                for name, tile in columns.items():
                    sp.dma_start(tile[:], a["L0_attn_" + name].rearrange("(k p) -> p k", p=P)).then_inc(bias_in, 16)
            for name, tile in spread.items():
                sp.dma_start(tile[:], a["L0_attn_" + name].partition_broadcast(P)).then_inc(bias_in, 16)
            sp.wait_ge(blocks_zeroed, 1)
            for h in range(HH):
                sp.dma_start(proj_bd[DHP * h:DHP * (h + 1), h, :], a["L0_attn_proj"]).then_inc(proj_in, 16)

        @block.gpsimd
        def _(pool):
            nc.gpsimd.memset(proj_bd[:], 0.0).then_inc(blocks_zeroed, 1)
            nc.gpsimd.memset(diag_bd[:], 0.5 * DHP ** -0.5).then_inc(blocks_started, 1)
            nc.gpsimd.memset(pair_mask[:], 1.0).then_inc(blocks_started, 1)
            pool.wait_ge(blocks_started, 2)
            for n, (tile, pattern, rows) in enumerate(((diag_bd, [[-DHP, HH]], DHP), (pair_mask, [[-M, 2], [0, VW]], M))):
                nc.gpsimd.affine_select(out=tile[:], in_=tile[:], compare_op=ALU.is_ge, fill=0.0, base=0,
                                        pattern=pattern, channel_multiplier=1).then_inc(blocks_half, 1)
                pool.wait_ge(blocks_half, 1 + n)
                nc.gpsimd.affine_select(out=tile[:], in_=tile[:], compare_op=ALU.is_ge, fill=0.0, base=rows - 1,
                                        pattern=[[-s, c] for s, c in pattern], channel_multiplier=-1).then_inc(blocks_done, 1)
            pool.wait_ge(eps_done, 1)
            nc.gpsimd.tensor_tensor(rstd[:], var_eps[:], neg_half[:, 0:QT], ALU.pow).then_inc(root_done, 1)
            pool.wait_ge(key_top, 1)
            nc.gpsimd.partition_all_reduce(top_key[:, 1, :], top_key[:, 0, :], P, bass.bass_isa.ReduceOp.max).then_inc(key_top_all, 1)

        @block.tensor
        def _(pe):
            pe.wait_ge(z_done, 1)
            for k in range(KD):
                for j in range(QT):
                    last = nc.tensor.transpose(ps[:, k, j * P:(j + 1) * P], z[:, j, k * P:(k + 1) * P], ident[:])
            last.then_inc(zt_done, 1)
            pe.wait_ge(w_in, 16 * len(w))
            pe.wait_ge(zt_kept, 1)
            for n, name in enumerate(("Wq", "Wk")):
                for half in range(KD):
                    for k in range(KD):
                        nc.tensor.matmul(ps[:, 2 + 2 * n + half, 0:NQ], w[name][:, k, half * P:(half + 1) * P],
                                         zt[:, k, :], start=k == 0, stop=k == KD - 1)
            for j in range(QT):
                for k in range(KD):
                    last = nc.tensor.matmul(ps[:, 6 + j, 0:D], zt[:, k, j * P:(j + 1) * P], w["Wv"][:, k, :],
                                            start=k == 0, stop=k == KD - 1)
            last.then_inc(qkv_done, 1)
            pe.wait_ge(qk_kept, 1)
            pe.wait_ge(v_kept, 1)
            pe.wait_ge(proj_scaled, 1)
            pe.wait_ge(blocks_done, 2)
            for n in range(2):
                for j in range(QT):
                    for half in range(KD):
                        bank = ps[:, 4 * n + 2 * j + half]
                        nc.tensor.matmul(bank[:, 0:HH * M], qk_t[:, n, half, j * P:(j + 1) * P],
                                         proj_bd[:].rearrange("p h m -> p (h m)"), start=True, stop=True)
                        last = nc.tensor.matmul(bank[:, HH * M:HH * M + HH], qk_sq[:, n, half, j * P:(j + 1) * P],
                                                diag_bd[:], start=True, stop=True)
                last.then_inc(exponents_done, 1)
            pe.wait_ge(feats_done, 2)
            for g in range(NPAIR):
                for j in range(QT):
                    last = nc.tensor.matmul(ps[0:PAIR, 4, g * 2 * VW:(g + 1) * 2 * VW], feats[:, 1, j, g * PAIR:(g + 1) * PAIR],
                                            v_one[:, j, 2 * g:2 * g + 2, :].rearrange("p h d -> p (h d)"),
                                            start=j == 0, stop=j == QT - 1)
            last.then_inc(context_done, 1)
            for g in range(NPAIR):
                for j in range(QT):
                    at = g * NQ + j * P
                    last = nc.tensor.transpose(ps[0:PAIR, at // 512, at % 512:at % 512 + P],
                                               feats[:, 0, j, g * PAIR:(g + 1) * PAIR], ident[:])
            last.then_inc(qp_done, 1)
            pe.wait_ge(context_kept, 1)
            pe.wait_ge(qp_kept, 1)
            for j in range(QT):
                for g in range(NPAIR):
                    last = nc.tensor.matmul(ps[:, 6 + j, g * 2 * VW:(g + 1) * 2 * VW], qp_t[:, g * NQ + j * P:g * NQ + (j + 1) * P],
                                            kv_ctx[:, g, :], start=True, stop=True)
            last.then_inc(o_ready, 1)
            pe.wait_ge(o_kept, 1)
            for k in range(KD):
                for j in range(QT):
                    last = nc.tensor.transpose(ps[:, k, j * P:(j + 1) * P],
                                               o[:, j].rearrange("p h d -> p (h d)")[:, k * P:(k + 1) * P], ident[:])
            last.then_inc(ot_done, 1)
            pe.wait_ge(ot_kept, 1)
            for half in range(KD):
                for k in range(KD):
                    last = nc.tensor.matmul(ps[:, 2 + half, 0:NQ], w["Wo"][:, k, half * P:(half + 1) * P], o_t[:, k, :],
                                            start=k == 0, stop=k == KD - 1)
            last.then_inc(ht_done, 1)
            pe.wait_ge(ht_kept, 1)
            for j in range(QT):
                for k in range(KD):
                    last = nc.tensor.matmul(ps[:, 4 + j, 0:D], h_t[:, k, j * P:(j + 1) * P], w["Wfc"][:, k, :],
                                            start=k == 0, stop=k == KD - 1)
            last.then_inc(fc_done, 1)

        @block.scalar
        def _(act):
            act.wait_ge(bias_in, 16 * 5)
            act.wait_ge(qkv_done, 1)
            for n, name in enumerate(("bq", "bk")):
                for half in range(KD):
                    nc.scalar.activation(qk_t[:, n, half, :], ps[:, 2 + 2 * n + half, 0:NQ], ACT.Identity,
                                         bias=columns[name][:, half:half + 1])
                    last = nc.scalar.activation(qk_sq[:, n, half, :], ps[:, 2 + 2 * n + half, 0:NQ], ACT.Square,
                                                bias=columns[name][:, half:half + 1])
            last.then_inc(qk_kept, 1)
            for n in range(2):
                side = feats[:, n].rearrange("p j m -> p (j m)")
                act.wait_ge(less_done, n + 1)
                nc.scalar.activation(side, side, ACT.Exp).then_inc(exp_done, 1)
            act.wait_ge(qp_done, 1)
            nc.scalar.activation(qp_t[:], ps[0:PAIR, 0:4].rearrange("p b n -> p (b n)"), ACT.Copy).then_inc(qp_kept, 1)
            act.wait_ge(ht_done, 1)
            for half in range(KD):
                last = nc.scalar.activation(h_t[:, half, :], ps[:, 2 + half, 0:NQ], ACT.Identity,
                                            bias=columns["bo"][:, half:half + 1])
            last.then_inc(ht_kept, 1)

        @block.vector
        def _(dve):
            row_norm(nc, dve, own, eps_done, root_done, x_res, z, stats, mean_var, var_eps, rstd).then_inc(z_done, 1)
            count = [NORM_LINKS]

            def link(ins):
                count[0] += 1
                ins.then_inc(own, 1)
                dve.wait_ge(own, count[0])

            dve.wait_ge(zt_done, 1)
            nc.vector.tensor_copy(zt[:], ps[:, 0:KD, 0:NQ]).then_inc(zt_kept, 1)
            dve.wait_ge(proj_in, 16 * HH)
            nc.vector.tensor_scalar_mul(proj_bd[:], proj_bd[:], DHP ** -0.25).then_inc(proj_scaled, 1)
            link(nc.vector.memset(v_one[:], 1.0))
            dve.wait_ge(bias_in, 16 * 5)
            dve.wait_ge(qkv_done, 1)
            for j in range(QT):
                last = nc.vector.tensor_tensor(v_one[:, j, :, 0:DHP], ps[:, 6 + j, 0:D].rearrange("p (h d) -> p h d", d=DHP),
                                               spread["bv"][:].rearrange("p (h d) -> p h d", d=DHP), ALU.add)
            last.then_inc(v_kept, 1)

            for n in range(2):
                dve.wait_ge(exponents_done, n + 1)
                for j in range(QT):
                    exponents = ps[:, 4 * n + 2 * j:4 * n + 2 * j + 2, 0:HH * M].rearrange("p k (h m) -> p k h m", m=M)
                    link(nc.vector.reduce_max(top[:, n, j], exponents, AX_X))
                if n == 1:
                    nc.vector.tensor_tensor(top_key[:, 0, :], top[:, 1, 0].rearrange("p k h -> p (k h)"),
                                            top[:, 1, 1].rearrange("p k h -> p (k h)"), ALU.max).then_inc(key_top, 1)
                    dve.wait_ge(key_top_all, 1)
                for j in range(QT):
                    diagonal = ps[:, 4 * n + 2 * j:4 * n + 2 * j + 2, HH * M:HH * M + HH]
                    highest = top[:, 0, j] if n == 0 else top_key[:, 1, :].rearrange("p (k h) -> p k h", k=KD)
                    link(nc.vector.tensor_tensor(less[:, n, j], diagonal, highest, ALU.add))
                    for half in range(KD):
                        last = nc.vector.tensor_tensor(
                            feats[:, n, j, half * HH * M:(half + 1) * HH * M].rearrange("p (h m) -> p h m", m=M),
                            ps[:, 4 * n + 2 * j + half, 0:HH * M].rearrange("p (h m) -> p h m", m=M),
                            less[:, n, j, half].unsqueeze(2).to_broadcast([P, HH, M]), ALU.subtract)
                last.then_inc(less_done, 1)
            for n in range(2):
                dve.wait_ge(exp_done, n + 1)
                nc.vector.tensor_scalar(feats[:, n], feats[:, n], FEAT_EPS, M ** -0.5, ALU.add, ALU.mult).then_inc(feats_done, 1)
            dve.wait_ge(blocks_done, 2)
            dve.wait_ge(context_done, 1)
            nc.vector.tensor_tensor(kv_ctx[:], ps[0:PAIR, 4, 0:NPAIR * 2 * VW].rearrange("p (g n) -> p g n", g=NPAIR),
                                    pair_mask[:].rearrange("p c n -> p (c n)").unsqueeze(1).to_broadcast([PAIR, NPAIR, 2 * VW]),
                                    ALU.mult).then_inc(context_kept, 1)
            dve.wait_ge(o_ready, 1)
            sums = ps[:, 6:8, 0:H * VW].rearrange("p j (h d) -> p j h d", d=VW)
            link(nc.vector.reciprocal(inverse[:], sums[:, :, :, DHP]))
            for j in range(QT):
                last = nc.vector.tensor_tensor(o[:, j], sums[:, j, :, 0:DHP], inverse[:, j].unsqueeze(2).to_broadcast([P, H, DHP]), ALU.mult)
            last.then_inc(o_kept, 1)
            dve.wait_ge(ot_done, 1)
            nc.vector.tensor_copy(o_t[:], ps[:, 0:KD, 0:NQ]).then_inc(ot_kept, 1)
            dve.wait_ge(fc_done, 1)
            link(nc.vector.tensor_tensor(y[:], ps[:, 4:6, 0:D], spread["bfc"][:].unsqueeze(1).to_broadcast([P, QT, D]), ALU.add))
            for j in range(QT):
                last = nc.vector.scalar_tensor_tensor(x_res[:, j, :], y[:, j, :], 0.0, x_res[:, j, :], ALU.max, ALU.add)
            link(last)


def experts(nc, sem, a, x_res, ident, neg_half):
    E1 = E + 1
    with ExitStack() as ctx:
        def sb(name, shape, dt=F32):
            return ctx.enter_context(nc.sbuf_tensor("e_" + name, shape, dt))

        def pair(name, shape, dt=F32):
            return [sb(f"{name}{b}", shape, dt) for b in range(2)]

        w1_raw, w2_raw = pair("w1_raw", [P, KD, F]), pair("w2_raw", [P, FT, D])
        w1, w2 = pair("w1", [P, KD, 2, F], F32R), pair("w2", [P, FT, 2, D], F32R)
        b1 = sb("b1", [P, E1, FT])
        b2 = sb("b2", [E1, D])
        wg = sb("wg", [P, KD, E])
        stats, mean_var, var_eps, rstd = sb("stats", [P, QT, 6]), sb("mean_var", [P, QT, 2]), sb("var_eps", [P, QT]), sb("rstd", [P, QT])
        z, zt = sb("z", [P, QT, D]), sb("zt", [P, KD, NQ])
        zp = sb("zp", [P, KD, 2, NQ], F32R)
        logit_top, neg_top = sb("logit_top", [P, QT, 8]), sb("neg_top", [P, QT])
        gate_exp, gate_sum, gate_inv = sb("gate_exp", [P, QT, E]), sb("gate_sum", [P, QT]), sb("gate_inv", [P, QT])
        gate = sb("gate", [P, QT, E])
        best, best_at = sb("best", [P, QT, 8]), sb("best_at", [P, QT, 8], U32)
        best_f, two = sb("best_f", [P, QT, 2]), sb("two", [P, QT, 4])
        number, number_f = sb("number", [P, E], mybir.dt.int32), sb("number_f", [P, E])
        picked = sb("picked", [P, QT, 2, E])
        share = sb("share", [P, QT, E1])
        share_t = sb("share_t", [E1, NQ])
        act_f = sb("act_f", [P, FT, NQ])
        act_p = sb("act_p", [P, 2, FT, NQ], F32R)
        h_ps = ctx.enter_context(nc.psum_tensor("e_h_ps", [P, FT, NQ], F32))
        y_ps = [ctx.enter_context(nc.psum_tensor(f"e_y_ps{b}", [P, QT, D], F32)) for b in range(2)]
        gate_ps = ctx.enter_context(nc.psum_tensor("e_gate_ps", [P, 512], F32))
        bias_ps = ctx.enter_context(nc.psum_tensor("e_bias_ps", [P, QT, D], F32))

        w1_in, w2_in = [sem(f"e_w1_in{b}") for b in range(2)], [sem(f"e_w2_in{b}") for b in range(2)]
        b1_in, b2_in, wg_in = sem("e_b1_in"), sem("e_b2_in"), sem("e_wg_in")
        numbered = sem("e_numbered")
        own, eps_done, root_done, z_done, zt_done, zt_kept = (
            sem("e_own"), sem("e_eps_done"), sem("e_root_done"), sem("e_z_done"), sem("e_zt_done"), sem("e_zt_kept"))
        zp_done, logits_done, neg_done, gate_exp_done = sem("e_zp_done"), sem("e_logits_done"), sem("e_neg_done"), sem("e_gate_exp_done")
        share_done, share_t_done, share_t_kept, bias_done = (
            sem("e_share_done"), sem("e_share_t_done"), sem("e_share_t_kept"), sem("e_bias_done"))
        w1_hi, w1_lo, w2_hi, w2_lo = sem("e_w1_hi"), sem("e_w1_lo"), sem("e_w2_hi"), sem("e_w2_lo")
        up_done, silu_done, act_hi, act_lo, down_done, added = (
            sem("e_up_done"), sem("e_silu_done"), sem("e_act_hi"), sem("e_act_lo"), sem("e_down_done"), sem("e_added"))

        block = ctx.enter_context(nc.Block())

        @block.sync
        def _(sp):
            def load(t):
                e = bass.ds(t.n, 1)
                if t.c >= 2:
                    sp.wait_ge(w1_lo, t.n - 1)
                    sp.wait_ge(w2_lo, t.n - 1)
                sp.dma_start(w1_raw[t.slot][:], a["ffn_W1"][e].rearrange("e (k p) f -> p (e k) f", p=P)).then_inc(w1_in[t.slot], 16)
                sp.dma_start(w2_raw[t.slot][:], a["ffn_W2"][e].rearrange("e (t p) n -> p (e t) n", p=P)).then_inc(w2_in[t.slot], 16)

            run(sp, load, 0, 2, 2)
            sp.dma_start(wg[:], a["L0_ffn_Wg"].rearrange("(k p) e -> p k e", p=P)).then_inc(wg_in, 16)
            sp.dma_start(b2[:], a["ffn_b2"]).then_inc(b2_in, 16)
            with nc.allow_non_contiguous_dma(reason="a vector onto partitions"):
                sp.dma_start(b1[:], a["ffn_b1"].rearrange("e (t p) -> p e t", p=P)).then_inc(b1_in, 16)
            run(sp, load, 2, E1, 2)

        @block.gpsimd
        def _(pool):
            nc.gpsimd.iota(number[:], [[1, E]], base=0, channel_multiplier=0).then_inc(numbered, 1)
            pool.wait_ge(eps_done, 1)
            nc.gpsimd.tensor_tensor(rstd[:], var_eps[:], neg_half[:, 0:QT], ALU.pow).then_inc(root_done, 1)

        @block.tensor
        def _(pe):
            pe.wait_ge(z_done, 1)
            for k in range(KD):
                for j in range(QT):
                    last = nc.tensor.transpose(y_ps[0][:, k, j * P:(j + 1) * P], z[:, j, k * P:(k + 1) * P], ident[:])
            last.then_inc(zt_done, 1)
            pe.wait_ge(zt_kept, 1)
            pe.wait_ge(wg_in, 16)
            for j in range(QT):
                for k in range(KD):
                    last = nc.tensor.matmul(gate_ps[:, j * E:(j + 1) * E], zt[:, k, j * P:(j + 1) * P], wg[:, k, :],
                                            start=k == 0, stop=k == KD - 1)
            last.then_inc(logits_done, 1)
            pe.wait_ge(zp_done, 1)

            def up(t):
                pe.wait_ge(w1_lo, t.n + 1)
                if t.c >= 1:
                    pe.wait_ge(silu_done, t.n)
                for f in range(FT):
                    last = part_products(nc, h_ps[:, f, :], lambda k, s: w1[t.slot][:, k, s, f * P:(f + 1) * P],
                                         lambda k, s: zp[:, k, s, :])
                last.then_inc(up_done, 1)

            def down(t):
                b = t.slot
                pe.wait_ge(w2_lo, t.n + 1)
                pe.wait_ge(act_lo, t.n + 1)
                if t.c >= 2:
                    pe.wait_ge(added, t.n - 1)
                for j in range(QT):
                    last = part_products(nc, y_ps[b][:, j, :], lambda f, s: act_p[:, s, f, j * P:(j + 1) * P],
                                         lambda f, s: w2[b][:, f, s, :], FT)
                last.then_inc(down_done, 1)

            def turn(t):
                up(t)
                down(t + -1)

            up(Turn(0, 2))
            pe.wait_ge(share_done, 1)
            for j in range(QT):
                last = nc.tensor.transpose(bias_ps[0:E1, j, 0:P], share[:, j, :], ident[:])
            last.then_inc(share_t_done, 1)
            pe.wait_ge(share_t_kept, 1)
            pe.wait_ge(b2_in, 16)
            for j in range(QT):
                last = nc.tensor.matmul(bias_ps[:, j, :], share_t[:, j * P:(j + 1) * P], b2[:], start=True, stop=True)
            last.then_inc(bias_done, 1)
            run(pe, turn, 1, E1, 2)
            down(Turn(E1 - 1, 2))

        @block.scalar
        def _(act):
            def hi1(t):
                act.wait_ge(w1_in[t.slot], (t.lap + 1) * 16)
                if t.c >= 2:
                    act.wait_ge(up_done, t.n - 1)
                nc.scalar.activation(w1[t.slot][:, :, 0, :], w1_raw[t.slot][:], ACT.Copy).then_inc(w1_hi, 1)

            def hi2(t):
                act.wait_ge(w2_in[t.slot], (t.lap + 1) * 16)
                if t.c >= 2:
                    act.wait_ge(down_done, t.n - 1)
                nc.scalar.activation(w2[t.slot][:, :, 0, :], w2_raw[t.slot][:], ACT.Copy).then_inc(w2_hi, 1)

            def silu(t):
                act.wait_ge(up_done, t.n + 1)
                if t.c >= 1:
                    act.wait_ge(act_lo, t.n)
                for f in range(FT):
                    last = nc.scalar.activation(act_f[:, f, :], h_ps[:, f, :], ACT.Silu,
                                                bias=b1[:, bass.ds(t.n, 1), f:f + 1].rearrange("p e f -> p (e f)"))
                last.then_inc(silu_done, 1)

            def turn(t):
                hi1(t + 1)
                silu(t)
                hi2(t + 1)

            hi1(Turn(0, 2))
            hi2(Turn(0, 2))
            act.wait_ge(neg_done, 1)
            for j in range(QT):
                last = nc.scalar.activation(gate_exp[:, j, :], gate_ps[:, j * E:(j + 1) * E], ACT.Exp,
                                            bias=neg_top[:, j:j + 1], accum_out=gate_sum[:, j:j + 1])
            last.then_inc(gate_exp_done, 1)
            act.wait_ge(b1_in, 16)
            turn(Turn(0, 2))
            run(act, turn, 1, E1 - 1, 2)
            silu(Turn(E1 - 1, 2))

        @block.vector
        def _(dve):
            row_norm(nc, dve, own, eps_done, root_done, x_res, z, stats, mean_var, var_eps, rstd).then_inc(z_done, 1)
            count = [NORM_LINKS]

            def link(ins):
                count[0] += 1
                ins.then_inc(own, 1)
                dve.wait_ge(own, count[0])

            def lo1(t):
                dve.wait_ge(w1_hi, t.n + 1)
                nc.vector.tensor_tensor(w1[t.slot][:, :, 1, :], w1_raw[t.slot][:], w1[t.slot][:, :, 0, :].bitcast(F32), ALU.subtract).then_inc(w1_lo, 1)

            def lo2(t):
                dve.wait_ge(w2_hi, t.n + 1)
                nc.vector.tensor_tensor(w2[t.slot][:, :, 1, :], w2_raw[t.slot][:], w2[t.slot][:, :, 0, :].bitcast(F32), ALU.subtract).then_inc(w2_lo, 1)

            def split_act(t):
                dve.wait_ge(silu_done, t.n + 1)
                if t.c >= 1:
                    dve.wait_ge(down_done, t.n)
                nc.vector.tensor_copy(act_p[:, 0], act_f[:]).then_inc(act_hi, 1)
                dve.wait_ge(act_hi, t.n + 1)
                nc.vector.tensor_tensor(act_p[:, 1], act_f[:], act_p[:, 0].bitcast(F32), ALU.subtract).then_inc(act_lo, 1)

            def add(t):
                dve.wait_ge(down_done, t.n + 1)
                if t.c >= 1:
                    dve.wait_ge(added, t.n)
                for j in range(QT):
                    last = nc.vector.scalar_tensor_tensor(x_res[:, j, :], y_ps[t.slot][:, j, :], share[:, j, bass.ds(t.n, 1)],
                                                          x_res[:, j, :], ALU.mult, ALU.add)
                last.then_inc(added, 1)

            def turn(t):
                lo1(t + 1)
                add(t + -1)
                split_act(t)
                lo2(t + 1)

            dve.wait_ge(zt_done, 1)
            nc.vector.tensor_copy(zt[:], y_ps[0][:]).then_inc(zt_kept, 1)
            dve.wait_ge(zt_kept, 1)
            link(nc.vector.tensor_copy(zp[:, :, 0, :], zt[:]))
            nc.vector.tensor_tensor(zp[:, :, 1, :], zt[:], zp[:, :, 0, :].bitcast(F32), ALU.subtract).then_inc(zp_done, 1)
            lo1(Turn(0, 2))
            dve.wait_ge(logits_done, 1)
            for j in range(QT):
                link(nc.vector.max(logit_top[:, j, :], gate_ps[:, j * E:(j + 1) * E]))
            nc.vector.tensor_scalar_mul(neg_top[:], logit_top[:, :, 0], -1.0).then_inc(neg_done, 1)
            dve.wait_ge(numbered, 1)
            link(nc.vector.tensor_copy(number_f[:], number[:]))
            dve.wait_ge(gate_exp_done, 1)
            link(nc.vector.reciprocal(gate_inv[:], gate_sum[:]))
            for j in range(QT):
                link(nc.vector.tensor_scalar(gate[:, j, :], gate_exp[:, j, :], gate_inv[:, j:j + 1], None, ALU.mult))
                link(nc.vector.max(best[:, j, :], gate[:, j, :]))
                link(nc.vector.max_index(best_at[:, j, :], best[:, j, :], gate[:, j, :]))
            link(nc.vector.tensor_copy(best_f[:], best_at[:, :, 0:2]))
            link(nc.vector.tensor_tensor(two[:, :, 0], best[:, :, 0], best[:, :, 1], ALU.add))
            link(nc.vector.tensor_scalar_add(two[:, :, 0], two[:, :, 0], TOP_EPS))
            link(nc.vector.reciprocal(two[:, :, 1], two[:, :, 0]))
            link(nc.vector.memset(share[:], SHARED))
            for j in range(QT):
                link(nc.vector.tensor_scalar(two[:, j, 2:4], best[:, j, 0:2], two[:, j, 1:2], None, ALU.mult))
                for c in range(2):
                    link(nc.vector.tensor_scalar(picked[:, j, c, :], number_f[:], best_f[:, j, c:c + 1],
                                                 two[:, j, 2 + c:3 + c], ALU.is_equal, ALU.mult))
                last = nc.vector.tensor_tensor(share[:, j, 0:E], picked[:, j, 0, :], picked[:, j, 1, :], ALU.add)
            last.then_inc(share_done, 1)
            dve.wait_ge(share_t_done, 1)
            nc.vector.tensor_copy(share_t[:].rearrange("e (j n) -> e j n", j=QT), bias_ps[0:E1, :, 0:P]).then_inc(share_t_kept, 1)
            dve.wait_ge(bias_done, 1)
            link(nc.vector.tensor_tensor(x_res[:], x_res[:], bias_ps[:], ALU.add))
            lo2(Turn(0, 2))
            lo1(Turn(1, 2))
            split_act(Turn(0, 2))
            lo2(Turn(1, 2))
            run(dve, turn, 1, E1 - 1, 2)
            add(Turn(E1 - 2, 2))
            split_act(Turn(E1 - 1, 2))
            add(Turn(E1 - 1, 2))


def store_result(nc, sem, out, x_res):
    with ExitStack() as ctx:
        stored = sem("stored")
        block = ctx.enter_context(nc.Block())

        @block.sync
        def _(sp):
            sp.dma_start(out.rearrange("o (j p) d -> p (o j) d", p=P), x_res[:]).then_inc(stored, 16)
            sp.wait_ge(stored, 16)


def kernel(**inputs):
    import numpy as np
    import concourse.bacc as bacc
    from concourse.bass_utils import run_bass_kernel_spmd

    arrays = laid_out(np, inputs)
    nc = bacc.Bacc("TRN2", target_bir_lowering=False, num_devices=1)
    aps = {name: nc.dram_tensor("in_" + name, x.shape, mybir.dt.from_np(x.dtype), kind="ExternalInput").ap()
           for name, x in arrays.items()}
    out = nc.dram_tensor("out", (1, NQ, D), F32, kind="ExternalOutput").ap()
    perceiver_kernel(nc, aps, out)
    result = run_bass_kernel_spmd(nc, [{"in_" + name: x for name, x in arrays.items()}], core_ids=[0])
    return result.results[0]["out"]


def laid_out(np, inputs):
    arrays = {name: np.ascontiguousarray(x) for name, x in inputs.items()}
    arrays["mask_BxS2_bf1"] = np.ascontiguousarray(arrays["mask_BxS2_bf1"].reshape(CT, P).T)
    for name in ("Wq", "Wk", "Wv", "Wo", "Wfc", "proj"):
        arrays["L0_attn_" + name] = np.ascontiguousarray(arrays["L0_attn_" + name].T)
    for name in ("W1", "b1", "W2", "b2"):
        own, shared = arrays.pop("L0_ffn_" + name), arrays.pop(f"L0_ffn_{name[0]}s{name[1]}")
        arrays["ffn_" + name] = np.concatenate([own, shared[None]])
    return arrays
```

```python
from contextlib import ExitStack

import concourse.bass as bass
from concourse import mybir

ALU = mybir.AluOpType
ACT = mybir.ActivationFunctionType
AX_X = mybir.AxisListType.X
F32 = mybir.dt.float32
F32R = mybir.dt.float32r
U32 = mybir.dt.uint32

P = 128
D = 256
KD = D // P
NQ = 256
QT = NQ // P
NCTX = 4096
CT = NCTX // P
NT = CT + QT
H = 16
DH = 64
INNER = H * DH
HQ = 4
NQUAD = H // HQ
QW = HQ * DH
NTILES = NQUAD * NT
GT = 4
NG = CT // GT
LN_EPS = 1e-5
RMS_FLOOR = 1e-8
EXP_ROOM = 70.0

DHP = 16
M = 44
PAIR = 2 * M
NPAIR = H // 2
VW = DHP + 1
FEAT_EPS = 1e-4

E = 8
F = 1024
FT = F // P
SHARED = 0.1
TOP_EPS = 1e-9
NORM_LINKS = 2


class Turn:

    def __init__(self, c, per, i=None, ring=None):
        self.c, self.per, self.i, self.ring = c, per, i, ring or per

    def __add__(self, k):
        return Turn(self.c + k, self.per, self.i, self.ring)

    @property
    def n(self):
        return self.c if self.i is None else self.i * self.per + self.c

    @property
    def slot(self):
        return self.c % self.ring

    @property
    def lap(self):
        c = self.c // self.ring
        return c if self.i is None else self.i * (self.per // self.ring) + c


def run(eng, body, first, end, per):
    turns = (end - first) // per
    if turns > 1:
        with eng.Fori(0, turns) as i:
            for c in range(per):
                body(Turn(first + c, per, i))
        first += turns * per
    for c in range(first, end):
        body(Turn(c, per))


class PerformerWeights:

    def __init__(self, hold, sem):
        self.w = {name: hold(name, [P, KD, D]) for name in ("Wq", "Wk", "Wv", "Wo", "Wfc")}
        self.columns = {name: hold(name, [P, KD]) for name in ("bq", "bk", "bo")}
        self.spread = {name: hold(name, [P, D]) for name in ("bv", "bfc")}
        self.proj_bd = hold("proj_bd", [P, H // KD, M])
        self.diag_bd = hold("diag_bd", [P, H // KD])
        self.pair_mask = hold("pair_mask", [PAIR, 2, VW])
        self.w_in, self.bias_in, self.proj_in = sem("f_w_in"), sem("f_bias_in"), sem("f_proj_in")
        self.blocks_zeroed, self.blocks_started = sem("f_blocks_zeroed"), sem("f_blocks_started")
        self.blocks_half, self.blocks_done = sem("f_blocks_half"), sem("f_blocks_done")


class ExpertWeights:

    def __init__(self, stay, sem):
        self.w1_raw = [stay(f"w1_raw{b}", [P, KD, F]) for b in range(2)]
        self.w2_raw = [stay(f"w2_raw{b}", [P, FT, D]) for b in range(2)]
        self.b1 = stay("b1", [P, E + 1, FT])
        self.w1_first = stay("w1_first", [P, KD, 2, F], F32R)
        self.w2_first = stay("w2_first", [P, FT, 2, D], F32R)
        self.w1_in, self.w2_in = [sem(f"w1_in{b}") for b in range(2)], [sem(f"w2_in{b}") for b in range(2)]
        self.b1_in = sem("b1_in")
        self.w1_hi, self.w1_lo, self.w2_hi, self.w2_lo = sem("w1_hi"), sem("w1_lo"), sem("w2_hi"), sem("w2_lo")


def perceiver_kernel(nc, a, out):
    xn_dram = nc.dram_tensor("xn_parts", (NT, P, KD * 2 * P), F32).ap()

    with ExitStack() as outer:
        def sem(name):
            return outer.enter_context(nc.semaphore(name))

        def keep(name, shape, dt=F32):
            return outer.enter_context(nc.sbuf_tensor(name, shape, dt))

        x_res = keep("x_res", [P, QT, D])
        ident = keep("ident", [P, P])
        neg_half = keep("neg_half", [P, QT * H])

        with ExitStack() as scope:
            def stay(name, shape, dt=F32):
                return scope.enter_context(nc.sbuf_tensor(name, shape, dt))

            attn_out = stay("attn_out", [P, NQUAD, HQ * NQ])
            weight_sum = stay("weight_sum", [P, NQUAD, HQ * NQ])
            wout = stay("wout", [P, H, 2, D], F32R)
            bout = stay("bout", [P, D])
            bout_in = sem("bout_in")
            with ExitStack() as inner:
                def hold(name, shape, dt=F32):
                    return inner.enter_context(nc.sbuf_tensor(name, shape, dt))

                wkv = hold("wkv", [P, NQUAD, KD, 2, 2 * QW], F32R)
                q_parts = hold("q_parts", [P, H, 2, NQ], F32R)
                score_bias = hold("score_bias", [P, NT])
                even_parts = hold("even_parts", [P, GT, KD, 2, P], F32R)
                even_parts_out = sem("even_parts_out")
                xn = [hold(f"xn{b}", [P, KD, 2, P], F32R) for b in range(4)]
                xn_in = [sem(f"xn_in{b}") for b in range(4)]
                prepare(nc, sem, a, xn_dram, x_res, ident, neg_half, wkv, q_parts, score_bias, attn_out,
                        weight_sum, wout, even_parts, even_parts_out, xn, xn_in)
                attention(nc, sem, a, xn_dram, ident, neg_half, wkv, q_parts, score_bias, attn_out, weight_sum,
                          even_parts_out, wout, bout, bout_in, xn, xn_in)
            ew = ExpertWeights(stay, sem)
            with ExitStack() as inner:
                def hold(name, shape, dt=F32):
                    return inner.enter_context(nc.sbuf_tensor("f_" + name, shape, dt))

                fw = PerformerWeights(hold, sem)
                attention_output(nc, sem, a, x_res, ident, attn_out, weight_sum, wout, bout, bout_in, fw, ew)
                performer(nc, sem, x_res, ident, neg_half, fw, ew)
            experts(nc, sem, a, x_res, ident, neg_half, ew)
        store_result(nc, sem, out, x_res)


def prepare(nc, sem, a, xn_dram, x_res, ident, neg_half, wkv, q_parts, score_bias, attn_out,
            weight_sum, wout, even_parts, even_parts_out, xn, xn_in):
    groups = NG + 1
    ctx_rows = a["ctx_1024"].rearrange("o (g j p) d -> g p (o j) d", p=P, j=GT)
    with ExitStack() as ctx:
        def sb(name, shape, dt=F32):
            return ctx.enter_context(nc.sbuf_tensor("p_" + name, shape, dt))

        def ring(n, name, shape, dt=F32):
            return [sb(f"{name}{b}", shape, dt) for b in range(n)]

        rows = ring(3, "rows", [P, GT, D])
        stats = ring(2, "stats", [P, GT, 6])
        mean_var = ring(2, "mean_var", [P, GT, 2])
        var_eps = ring(2, "var_eps", [P, GT])
        rstd = ring(2, "rstd", [P, GT])
        first_stats, first_mv = sb("first_stats", [P, QT, 6]), sb("first_mv", [P, QT, 2])
        first_var, first_rstd = sb("first_var", [P, QT]), sb("first_rstd", [P, QT])
        z = ring(2, "z", [P, GT, D])
        u = ring(2, "u", [P, KD, GT, P])
        latent_parts = sb("latent_parts", [P, QT, KD, 2, P], F32R)
        odd_parts = sb("odd_parts", [P, GT, KD, 2, P], F32R)
        gains = sb("gains", [P, 2, 2, KD])
        w_raw = ring(2, "w_raw", [P, KD, 2 * QW])
        wq = wout[:, 0:KD * 2 * INNER // (2 * D)].rearrange("p h s n -> p (h s n)").rearrange("p (k s n) -> p k s n", k=KD, s=2)
        wq_raw = weight_sum[:, 0:KD, :]
        q_sq = weight_sum[:, KD, :].rearrange("p (h d) -> p h d", h=H)
        gq = sb("gq", [P, 2, DH])
        gqk = sb("gqk", [P, DH])
        gq_col = sb("gq_col", [P, 2])
        gqk_col = sb("gqk_col", [P, 1])
        bound = sb("bound", [P, DH + 2])
        mask_raw = sb("mask_raw", [P, CT], mybir.dt.uint8)
        mask_f = sb("mask_f", [P, CT])
        q_ss, q_ms, q_rms = sb("q_ss", [P, QT, H]), sb("q_ms", [P, QT, H]), sb("q_rms", [P, QT, H])
        qn = attn_out[:].rearrange("p q n -> p (q n)").rearrange("p (j h c d) -> p j h c d", j=QT, h=H, c=2)
        zt_ps = [ctx.enter_context(nc.psum_tensor(f"p_zt_ps{b}", [P, KD, GT * P], F32)) for b in range(2)]
        q_ps = ctx.enter_context(nc.psum_tensor("p_q_ps", [P, QT, INNER], F32))

        x_in, gains_in, gq_in, mask_in, wq_in = sem("x_in"), sem("gains_in"), sem("gq_in"), sem("mask_in"), sem("wq_in")
        rows_in, w_in = [sem(f"rows_in{b}") for b in range(3)], [sem(f"w_in{b}") for b in range(2)]
        parts_out = [even_parts_out, sem("odd_parts_out")]
        ident_zeroed, const_done, ident_done = sem("ident_zeroed"), sem("const_done"), sem("ident_done")
        first_eps, first_root, first_done = sem("first_eps"), sem("first_root"), sem("first_done")
        own, stats_done, aggr_done, eps_done, root_done = (
            sem("p_own"), sem("stats_done"), sem("aggr_done"), sem("eps_done"), sem("root_done"))
        z_done, zt_done, u_done, hi_done, lo_done = sem("z_done"), sem("zt_done"), sem("u_done"), sem("hi_done"), sem("lo_done")
        w_hi, w_lo, wq_hi, wq_lo = sem("w_hi"), sem("w_lo"), sem("wq_hi"), sem("wq_lo")
        q_done, q_sq_done, q_ss_done, q_ms_done, q_rms_done, qn_done = (
            sem("q_done"), sem("q_sq_done"), sem("q_ss_done"), sem("q_ms_done"), sem("q_rms_done"), sem("qn_done"))
        qn_twice, qt_done, qt_hi, qt_lo, col_done = sem("qn_twice"), sem("qt_done"), sem("qt_hi"), sem("qt_lo"), sem("col_done")

        def parts_of(n):
            return latent_parts if n == 0 else (even_parts, odd_parts)[n % 2]

        def tiles_of(n):
            return QT if n == 0 else GT

        block = ctx.enter_context(nc.Block())

        @block.sync
        def _(sp):
            sp.dma_start(x_res[:], a["x"].rearrange("o (j p) d -> p (o j) d", p=P)).then_inc(x_in, 16)
            sp.dma_start(rows[1][:], ctx_rows[0]).then_inc(rows_in[1], 16)
            sp.dma_start(rows[2][:], ctx_rows[1]).then_inc(rows_in[2], 16)
            sp.dma_start(rows[0][:], ctx_rows[2]).then_inc(rows_in[0], 16)
            for n in range(groups):
                if n >= 1 and n + 3 < groups:
                    sp.wait_ge(z_done, n + 1)
                    sp.dma_start(rows[n % 3][:], ctx_rows[n + 2]).then_inc(rows_in[n % 3], 16)
                if n == groups - 2:
                    sp.wait_ge(parts_out[1], 16)
                    for t in range(len(xn)):
                        sp.dma_start(xn[t][:].bitcast(F32).rearrange("p k s n -> p (k s n)"), xn_dram[t]).then_inc(xn_in[t], 16)
                t, first = tiles_of(n), CT if n == 0 else (n - 1) * GT
                sp.wait_ge(lo_done, n + 1)
                sp.dma_start(xn_dram[first:first + t, :, :].rearrange("t p n -> p t n"),
                             parts_of(n)[:, 0:t].bitcast(F32).rearrange("p t k s n -> p t (k s n)")).then_inc(parts_out[n % 2], 16)
            sp.wait_ge(parts_out[0], 16 * (groups // 2))
            sp.wait_ge(parts_out[1], 16 * (groups // 2))

        @block.gpsimd
        def _(pool):
            nc.gpsimd.memset(ident[:], 0.0).then_inc(ident_zeroed, 1)
            nc.gpsimd.memset(neg_half[:], -0.5).then_inc(const_done, 1)
            pool.wait_ge(ident_zeroed, 1)
            nc.gpsimd.affine_select(out=ident[:], in_=ident[:], compare_op=ALU.not_equal, fill=1.0,
                                    base=0, pattern=[[-1, P]], channel_multiplier=1).then_inc(ident_done, 1)
            pool.wait_ge(const_done, 1)
            pool.wait_ge(first_eps, 1)
            nc.gpsimd.tensor_tensor(first_rstd[:], first_var[:], neg_half[:, 0:QT], ALU.pow).then_inc(first_root, 1)

            def root(n):
                t = tiles_of(n)
                pool.wait_ge(eps_done, n + 1)
                nc.gpsimd.tensor_tensor(rstd[n % 2][:, 0:t], var_eps[n % 2][:, 0:t], neg_half[:, 0:t], ALU.pow).then_inc(root_done, 1)

            def weights_lo(quad):
                pool.wait_ge(w_hi, quad + 1)
                nc.gpsimd.tensor_tensor(wkv[:, quad, :, 1, :], w_raw[quad % 2][:], wkv[:, quad, :, 0, :].bitcast(F32),
                                        ALU.subtract).then_inc(w_lo, 1)

            def queries_root(j):
                pool.wait_ge(q_ms_done, j + 1)
                nc.gpsimd.tensor_tensor(q_rms[:, j, :], q_ms[:, j, :], neg_half[:, 0:H], ALU.pow).then_inc(q_rms_done, 1)

            for n in range(3):
                root(n)
            pool.wait_ge(wq_hi, 1)
            nc.gpsimd.tensor_tensor(wq[:, :, 1, :], wq_raw, wq[:, :, 0, :].bitcast(F32), ALU.subtract).then_inc(wq_lo, 1)
            root(3)
            weights_lo(0)
            root(4)
            weights_lo(1)
            queries_root(0)
            root(5)
            queries_root(1)
            root(6)
            root(7)
            root(8)
            weights_lo(2)
            pool.wait_ge(wq_lo, 1)
            pool.wait_ge(q_ss_done, QT)
            nc.gpsimd.memset(weight_sum[:], 0.0)
            weights_lo(3)

        @block.scalar
        def _(act):
            act.dma_start(wq_raw, a["L0_xattn_Wq"].rearrange("(k p) n -> p k n", p=P)).then_inc(wq_in, 16)
            with nc.allow_non_contiguous_dma(reason="a vector onto partitions"):
                for n, name in enumerate(("ln_l_g", "ln_l_b", "ln_x_g", "ln_x_b")):
                    act.dma_start(gains[:, n // 2, n % 2, :], a["L0_xattn_" + name].rearrange("(k p) -> p k", p=P)).then_inc(gains_in, 16)
                for n, name in enumerate(("qn_g", "kn_g")):
                    act.dma_start(gq[:, n, :], a["L0_xattn_" + name].partition_broadcast(P)).then_inc(gq_in, 16)
                    for c in range(2):
                        act.dma_start(gq_col[c * DH:(c + 1) * DH, n:n + 1], a["L0_xattn_" + name].rearrange("(p o) -> p o", o=1)).then_inc(gq_in, 16)
            act.dma_start(mask_raw[:], a["mask_BxS2_bf1"]).then_inc(mask_in, 16)
            w_view = a["L0_xattn_Wkv"].rearrange("(k p) (s q n) -> q s p k n", p=P, s=2, q=NQUAD)

            def load_weights(quad):
                for s in range(2):
                    act.dma_start(w_raw[quad % 2][:, :, s * QW:(s + 1) * QW], w_view[quad, s]).then_inc(w_in[quad % 2], 16)

            load_weights(0)
            load_weights(1)

            def affine_and_hi(n):
                t, which = tiles_of(n), 0 if n == 0 else 1
                act.wait_ge(zt_done, n + 1)
                if n >= 2:
                    act.wait_ge(lo_done, n - 1)
                for k in range(KD):
                    last = nc.scalar.activation(u[n % 2][:, k, 0:t].rearrange("p t n -> p (t n)"), zt_ps[n % 2][:, k, 0:t * P],
                                                ACT.Identity, scale=gains[:, which, 0, k:k + 1], bias=gains[:, which, 1, k:k + 1])
                last.then_inc(u_done, 1)
                act.wait_ge(u_done, n + 1)
                if n >= 2:
                    act.wait_ge(parts_out[n % 2], 16 * (n // 2))
                for k in range(KD):
                    last = nc.scalar.activation(parts_of(n)[:, 0:t, k, 0, :], u[n % 2][:, k, 0:t], ACT.Copy)
                last.then_inc(hi_done, 1)

            def squares(j):
                act.wait_ge(q_done, j + 1)
                if j:
                    act.wait_ge(q_ss_done, j)
                nc.scalar.activation(q_sq.rearrange("p h d -> p (h d)"), q_ps[:, j, :], ACT.Square,
                                     scale=DH ** -0.5).then_inc(q_sq_done, 1)

            def weights_hi(quad):
                act.wait_ge(w_in[quad % 2], 32 * (quad // 2 + 1))
                nc.scalar.activation(wkv[:, quad, :, 0, :], w_raw[quad % 2][:], ACT.Copy).then_inc(w_hi, 1)

            def repeat_queries(j):
                act.wait_ge(qn_done, j + 1)
                nc.scalar.activation(qn[:, j, :, 1, :], qn[:, j, :, 0, :], ACT.Copy).then_inc(qn_twice, 1)

            def keep_qt(c):
                act.wait_ge(qt_done, c + 1)
                nc.scalar.activation(q_parts[:, 4 * c:4 * c + 4, 0, :], q_ps[:, c % 2, :].rearrange("p (h q) -> p h q", h=4),
                                     ACT.Copy, scale=gqk_col[:]).then_inc(qt_hi, 1)

            act.wait_ge(wq_in, 16)
            nc.scalar.activation(wq[:, :, 0, :], wq_raw, ACT.Copy).then_inc(wq_hi, 1)
            act.wait_ge(gains_in, 64)
            affine_and_hi(0)
            affine_and_hi(1)
            weights_hi(0)
            affine_and_hi(2)
            weights_hi(1)
            squares(0)
            affine_and_hi(3)
            squares(1)
            affine_and_hi(4)
            for quad in range(2, NQUAD):
                act.wait_ge(w_lo, quad - 1)
                load_weights(quad)
            affine_and_hi(5)
            repeat_queries(0)
            affine_and_hi(6)
            repeat_queries(1)
            weights_hi(2)
            act.wait_ge(col_done, 1)
            keep_qt(0)
            affine_and_hi(7)
            keep_qt(1)
            weights_hi(3)
            keep_qt(2)
            affine_and_hi(8)
            keep_qt(3)

        @block.vector
        def _(dve):
            count = [0]

            def link(ins):
                count[0] += 1
                ins.then_inc(own, 1)
                dve.wait_ge(own, count[0])

            def statistics(n, src):
                b, t = n % 2, tiles_of(n)
                for j in range(t):
                    last = nc.vector.bn_stats(stats[b][:, j, :], src[:, j, :])
                last.then_inc(stats_done, 1)
                dve.wait_ge(stats_done, n + 1)
                for j in range(t):
                    last = nc.vector.bn_aggr(mean_var[b][:, j, :], stats[b][:, j, :])
                last.then_inc(aggr_done, 1)
                dve.wait_ge(aggr_done, n + 1)
                nc.vector.tensor_scalar_add(var_eps[b][:, 0:t], mean_var[b][:, 0:t, 1], LN_EPS).then_inc(eps_done, 1)

            def normalise(n, src):
                b = n % 2
                dve.wait_ge(root_done, n + 1)
                if n >= 2:
                    dve.wait_ge(zt_done, n - 1)
                for j in range(tiles_of(n)):
                    last = nc.vector.tensor_scalar(z[b][:, j, :], src[:, j, :], mean_var[b][:, j, 0:1],
                                                   rstd[b][:, j:j + 1], ALU.subtract, ALU.mult)
                last.then_inc(z_done, 1)

            def lo(n):
                b, t = n % 2, tiles_of(n)
                dve.wait_ge(hi_done, n + 1)
                for k in range(KD):
                    last = nc.vector.tensor_tensor(parts_of(n)[:, 0:t, k, 1, :], u[b][:, k, 0:t], parts_of(n)[:, 0:t, k, 0, :].bitcast(F32), ALU.subtract)
                last.then_inc(lo_done, 1)

            def arrived(n):
                dve.wait_ge(rows_in[n % 3], 16 * (n // 3 + (0 if n % 3 == 0 else 1)))
                return rows[n % 3]

            def mean_squares(j):
                dve.wait_ge(q_sq_done, j + 1)
                nc.vector.reduce_sum(q_ss[:, j, :], q_sq, AX_X).then_inc(q_ss_done, 1)
                dve.wait_ge(q_ss_done, j + 1)
                nc.vector.tensor_scalar_max(q_ms[:, j, :], q_ss[:, j, :], RMS_FLOOR ** 2).then_inc(q_ms_done, 1)

            def scale_queries(j):
                dve.wait_ge(q_rms_done, j + 1)
                nc.vector.tensor_tensor(qn[:, j, :, 0, :], q_ps[:, j, :].rearrange("p (h d) -> p h d", d=DH),
                                        q_rms[:, j, :].unsqueeze(2).to_broadcast([P, H, DH]), ALU.mult).then_inc(qn_done, 1)

            def qt_lo_part(c):
                dve.wait_ge(qt_hi, c + 1)
                nc.vector.scalar_tensor_tensor(q_parts[:, 4 * c:4 * c + 4, 1, :], q_ps[:, c % 2, :].rearrange("p (h q) -> p h q", h=4),
                                               gqk_col[:], q_parts[:, 4 * c:4 * c + 4, 0, :].bitcast(F32),
                                               ALU.mult, ALU.subtract).then_inc(qt_lo, 1)

            dve.wait_ge(x_in, 16)
            for j in range(QT):
                link(nc.vector.bn_stats(first_stats[:, j, :], x_res[:, j, :]))
                link(nc.vector.bn_aggr(first_mv[:, j, :], first_stats[:, j, :]))
            nc.vector.tensor_scalar_add(first_var[:], first_mv[:, :, 1], LN_EPS).then_inc(first_eps, 1)
            dve.wait_ge(first_root, 1)
            for j in range(QT):
                link(nc.vector.tensor_scalar(z[1][:, j, :], x_res[:, j, :], first_mv[:, j, 0:1],
                                             first_rstd[:, j:j + 1], ALU.subtract, ALU.mult))
            statistics(0, z[1])
            statistics(1, arrived(1))
            normalise(0, z[1])
            link(nc.vector.memset(score_bias[:, CT:NT], 0.0))
            normalise(1, rows[1])
            statistics(2, arrived(2))
            normalise(2, rows[2])
            lo(0)
            statistics(3, arrived(3))
            lo(1)
            normalise(3, rows[0])
            dve.wait_ge(gq_in, 16 * 6)
            nc.vector.scalar_tensor_tensor(gqk_col[:], gq_col[:, 0:1], DH ** -0.5, gq_col[:, 1:2], ALU.mult, ALU.mult).then_inc(col_done, 1)
            link(nc.vector.scalar_tensor_tensor(gqk[:], gq[:, 0, :], DH ** -0.5, gq[:, 1, :], ALU.mult, ALU.mult))
            statistics(4, arrived(4))
            link(nc.vector.scalar_tensor_tensor(bound[:, 0:DH], gqk[:], -1.0, gqk[:], ALU.mult, ALU.max))
            lo(2)
            mean_squares(0)
            normalise(4, rows[1])
            statistics(5, arrived(5))
            lo(3)
            mean_squares(1)
            normalise(5, rows[2])
            link(nc.vector.reduce_max(bound[:, DH:DH + 1], bound[:, 0:DH], AX_X))
            statistics(6, arrived(6))
            lo(4)
            scale_queries(0)
            normalise(6, rows[0])
            link(nc.vector.tensor_scalar(bound[:, DH + 1:DH + 2], bound[:, DH:DH + 1], float(DH), -EXP_ROOM, ALU.mult, ALU.add))
            statistics(7, arrived(7))
            link(nc.vector.tensor_scalar(bound[:, DH:DH + 1], bound[:, DH + 1:DH + 2], 0.0, -1.0, ALU.max, ALU.mult))
            scale_queries(1)
            lo(5)
            normalise(7, rows[1])
            dve.wait_ge(mask_in, 16)
            link(nc.vector.tensor_copy(mask_f[:], mask_raw[:]))
            statistics(8, arrived(8))
            link(nc.vector.tensor_scalar(score_bias[:, 0:CT], mask_f[:], 1e30, -1e30, ALU.mult, ALU.add))
            lo(6)
            normalise(8, rows[2])
            link(nc.vector.tensor_scalar(score_bias[:], score_bias[:], bound[:, DH:DH + 1], None, ALU.add))
            qt_lo_part(0)
            lo(7)
            qt_lo_part(1)
            qt_lo_part(2)
            lo(8)
            qt_lo_part(3)

        @block.tensor
        def _(pe):
            def transposes(n):
                pe.wait_ge(z_done, n + 1)
                if n >= 2:
                    pe.wait_ge(u_done, n - 1)
                for k in range(KD):
                    for j in range(tiles_of(n)):
                        last = nc.tensor.transpose(zt_ps[n % 2][:, k, j * P:(j + 1) * P],
                                                   z[n % 2][:, j, k * P:(k + 1) * P], ident[:])
                last.then_inc(zt_done, 1)

            pe.wait_ge(ident_done, 1)
            transposes(0)
            transposes(1)
            transposes(2)
            pe.wait_ge(lo_done, 1)
            pe.wait_ge(wq_lo, 1)
            for j in range(QT):
                for c in range(INNER // 512):
                    last = part_products(nc, q_ps[:, j, c * 512:(c + 1) * 512],
                                         lambda k, s: latent_parts[:, j, k, s, :],
                                         lambda k, s: wq[:, k, s, c * 512:(c + 1) * 512])
                last.then_inc(q_done, 1)
                transposes(3 + j)
            for n in range(5, 8):
                transposes(n)

            def transpose_queries(c):
                if c >= 2:
                    pe.wait_ge(qt_lo, c - 1)
                for h in range(4):
                    for j in range(QT):
                        at = h * NQ + j * P
                        last = nc.tensor.transpose(q_ps[:, c % 2, at:at + P], qn[:, j, 4 * c + h].rearrange("p c d -> p (c d)"), ident[:])
                last.then_inc(qt_done, 1)

            pe.wait_ge(qn_twice, QT)
            transpose_queries(0)
            transpose_queries(1)
            transposes(8)
            transpose_queries(2)
            transpose_queries(3)


def part_products(nc, out, stationary, moving, kd=KD):
    terms = [(k, s, m) for k in range(kd) for s, m in ((0, 0), (0, 1), (1, 0))]
    for n, (k, s, m) in enumerate(terms):
        last = nc.tensor.matmul(out, stationary(k, s), moving(k, m), start=n == 0, stop=n == len(terms) - 1)
    return last


def attention(nc, sem, a, xn_dram, ident, neg_half, wkv, q_parts, score_bias, attn_out, weight_sum,
              even_parts_out, wout, bout, bout_in, xn, xn_in):
    RING = 4
    UNROLL = 2 * RING
    with ExitStack() as ctx:
        def ring(n, name, shape, dt=F32):
            return [ctx.enter_context(nc.sbuf_tensor(f"{name}{b}", shape, dt)) for b in range(n)]

        kv = ring(4, "kv", [P, 2 * HQ, 2, DH], F32R)
        k_sq = ring(2, "k_sq", [P, HQ, DH])
        k_ss = ring(4, "k_ss", [P, HQ])
        k_ms = ring(4, "k_ms", [P, HQ])
        k_rms = ring(4, "k_rms", [P, HQ])
        bias_now = ring(4, "bias_now", [P, 1])
        kt = ring(2, "kt", [P, HQ * P], F32R)
        probs = ring(2, "probs", [P, HQ * NQ])
        probs_hi = ring(2, "probs_hi", [P, HQ * NQ], F32R)
        probs_lo = ring(2, "probs_lo", [P, HQ * NQ], F32R)
        wout_raw = ring(1, "wout_raw", [P, HQ, D])[0]
        kv_ps = ctx.enter_context(nc.psum_tensor("kv_ps", [P, 2 * QW], F32))
        kt_ps = ctx.enter_context(nc.psum_tensor("kt_ps", [P, HQ * P], F32))
        s_ps = [ctx.enter_context(nc.psum_tensor(f"s_ps{b}", [P, HQ * NQ], F32)) for b in range(2)]
        o_ps = ctx.enter_context(nc.psum_tensor("o_ps", [P, HQ * NQ], F32))

        kv_done, sq_done, kv_hi, kv_lo = sem("kv_done"), sem("sq_done"), sem("kv_hi"), sem("kv_lo")
        ss_done, ms_done, rms_done, bias_done = sem("ss_done"), sem("ms_done"), sem("rms_done"), sem("bias_done")
        kt_done, kt_kept, s_done, exp_done = sem("kt_done"), sem("kt_kept"), sem("s_done"), sem("exp_done")
        wout_in, wout_hi, wout_lo = sem("wout_in"), sem("wout_hi"), sem("wout_lo")
        p_hi, p_lo, pv_done, sum_done, out_kept = sem("p_hi"), sem("p_lo"), sem("pv_done"), sem("sum_done"), sem("out_kept")

        block = ctx.enter_context(nc.Block())

        def steps(eng, step):
            for s in (-1, 0, 1, 2):
                step(Turn(s, UNROLL, ring=RING), 0)
            turns = (NT - 5) // UNROLL
            for quad in range(NQUAD):
                first = quad * NT + 3
                with eng.Fori(0, turns) as i:
                    for c in range(UNROLL):
                        step(Turn(first + c, UNROLL, i, RING), quad)
                for s in range(first + turns * UNROLL, (quad + 1) * NT + 3 if quad + 1 < NQUAD else NTILES + 2):
                    step(Turn(s, UNROLL, ring=RING), quad)

        def exists(t):
            return 0 <= t.c < NTILES

        def quad_of(t):
            return t.c // NT

        @block.sync
        def _(sp):
            def load(t, quad):
                if t.c >= 4:
                    sp.wait_ge(kv_done, t.n - 3)
                sp.dma_start(xn[t.slot][:].bitcast(F32).rearrange("p k s n -> p (k s n)"),
                             xn_dram[bass.ds((t + -quad * NT).n, 1)].rearrange("t p n -> p (t n)")).then_inc(xn_in[t.slot], 16)

            wout_rows = a["L0_xattn_Wout"].rearrange("(h d) n -> d h n", d=DH)
            for quad in range(NQUAD):
                for c in range(4):
                    if quad:
                        load(Turn(quad * NT + c, 4), quad)
                if quad == 0:
                    sp.dma_start(bout[:], a["L0_xattn_bout"].partition_broadcast(P)).then_inc(bout_in, 16)
                    sp.wait_ge(even_parts_out, 16 * ((NG + 2) // 2))
                run(sp, lambda t: load(t, quad), quad * NT + 4, (quad + 1) * NT, 4)
                if quad:
                    sp.wait_ge(wout_lo, quad)
                for c in range(2):
                    sp.dma_start(wout_raw[c * DH:(c + 1) * DH], wout_rows[:, quad * HQ:(quad + 1) * HQ, :]).then_inc(wout_in, 16)

        @block.tensor
        def _(pe):
            def project(t):
                quad = quad_of(t)
                pe.wait_ge(xn_in[t.slot], (t.lap + 1) * 16)
                if t.c >= 1:
                    pe.wait_ge(kv_lo, t.n * 2)
                part_products(nc, kv_ps[:], lambda k, s: xn[t.slot][:, k, s, :],
                              lambda k, s: wkv[:, quad, k, s, :]).then_inc(kv_done, 1)

            def transpose_k(t):
                pe.wait_ge(kv_lo, t.n * 2 + 1)
                if t.c >= 1:
                    pe.wait_ge(kt_kept, t.n)
                for h in range(HQ):
                    last = nc.tensor.transpose(kt_ps[:, h * P:(h + 1) * P],
                                               kv[t.slot][:, h].bitcast(F32).rearrange("p s d -> p (s d)"), ident[:])
                last.then_inc(kt_done, 1)

            def weight_v(t):
                local = t.c % NT
                pe.wait_ge(p_lo, t.n * 2 + 2)
                b = t.c % 2
                for h in range(HQ):
                    if local == 0 and t.c and h % 2 == 0:
                        pe.wait_ge(out_kept, (t.c // NT - 1) * 2 + 1 + h // 2)
                    for s, part in enumerate((probs_hi, probs_lo)):
                        last = nc.tensor.matmul(o_ps[:, h * NQ:(h + 1) * NQ],
                                                kv[t.slot][:, HQ + h].rearrange("p s d -> p (s d)"),
                                                part[b][:, h * NQ:(h + 1) * NQ],
                                                start=local == 0 and h % 2 == 0 and s == 0,
                                                stop=local == NT - 1 and s == 1, skip_group_check=True)
                last.then_inc(pv_done, 1)

            def scores(t):
                quad, b = quad_of(t), t.c % 2
                pe.wait_ge(kt_kept, t.n + 1)
                if t.c >= 2:
                    pe.wait_ge(exp_done, t.n * 2 - 2)
                for h in range(HQ):
                    for s in range(2):
                        last = nc.tensor.matmul(s_ps[b][:, h * NQ:(h + 1) * NQ], kt[b][:, h * P:(h + 1) * P],
                                                q_parts[:, quad * HQ + h, s, :], start=s == 0, stop=s == 1)
                    if h % 2:
                        last.then_inc(s_done, 1)

            def step(s, quad):
                if exists(s + 1):
                    project(s + 1)
                if exists(s):
                    scores(s)
                if exists(s + -2):
                    weight_v(s + -2)
                if exists(s + 1):
                    transpose_k(s + 1)

            steps(pe, step)

        @block.scalar
        def _(act):
            def weights(t):
                b = t.c % 2
                act.wait_ge(rms_done, t.n + 1)
                act.wait_ge(bias_done, t.n + 1)
                if t.c >= 2:
                    act.wait_ge(p_lo, t.n * 2 - 2)
                    act.wait_ge(sum_done, t.n - 1)
                for h in range(HQ):
                    if h % 2 == 0:
                        act.wait_ge(s_done, t.n * 2 + (1 + h // 2))
                    last = nc.scalar.activation(probs[b][:, h * NQ:(h + 1) * NQ], s_ps[b][:, h * NQ:(h + 1) * NQ], ACT.Exp,
                                                scale=k_rms[t.slot][:, h:h + 1], bias=bias_now[t.slot][:])
                    if h % 2:
                        last.then_inc(exp_done, 1)

            def keep_kt(t):
                act.wait_ge(kt_done, t.n + 1)
                if t.c >= 2:
                    act.wait_ge(s_done, t.n * 2 - 2)
                nc.scalar.activation(kt[t.c % 2][:], kt_ps[:], ACT.Copy).then_inc(kt_kept, 1)

            def squares_and_hi(t):
                act.wait_ge(kv_done, t.n + 1)
                if t.c >= 2:
                    act.wait_ge(ss_done, t.n - 1)
                nc.scalar.activation(k_sq[t.c % 2][:].rearrange("p h d -> p (h d)"), kv_ps[:, 0:QW], ACT.Square,
                                     scale=DH ** -0.5).then_inc(sq_done, 1)
                if t.c >= 4:
                    act.wait_ge(pv_done, t.n - 3)
                nc.scalar.activation(kv[t.slot][:, :, 0, :], kv_ps[:].rearrange("p (h d) -> p h d", d=DH), ACT.Copy).then_inc(kv_hi, 1)

            def step(s, quad):
                if exists(s + 1):
                    squares_and_hi(s + 1)
                if exists(s):
                    weights(s)
                if exists(s + 1):
                    keep_kt(s + 1)
                if s.c % NT == NT - 2 and s.c > 0:
                    act.wait_ge(wout_in, 32 * (quad + 1))
                    nc.scalar.activation(wout[:, quad * HQ:(quad + 1) * HQ, 0, :], wout_raw[:], ACT.Copy).then_inc(wout_hi, 1)

            steps(act, step)

        @block.vector
        def _(dve):
            def split_weights(t):
                b = t.c % 2
                if t.c >= 2:
                    dve.wait_ge(pv_done, t.n - 1)
                for c in range(2):
                    two = slice(c * 2 * NQ, (c + 1) * 2 * NQ)
                    dve.wait_ge(exp_done, t.n * 2 + (1 + c))
                    nc.vector.tensor_copy(probs_hi[b][:, two], probs[b][:, two]).then_inc(p_hi, 1)
                    dve.wait_ge(p_hi, t.n * 2 + (1 + c))
                    nc.vector.tensor_tensor(probs_lo[b][:, two], probs[b][:, two], probs_hi[b][:, two].bitcast(F32),
                                            ALU.subtract).then_inc(p_lo, 1)

            def split_kv(t):
                dve.wait_ge(kv_hi, t.n + 1)
                for side in (slice(0, HQ), slice(HQ, 2 * HQ)):
                    nc.vector.tensor_tensor(kv[t.slot][:, side, 1, :], kv_ps[:].rearrange("p (h d) -> p h d", d=DH)[:, side],
                                            kv[t.slot][:, side, 0, :].bitcast(F32), ALU.subtract).then_inc(kv_lo, 1)
                dve.wait_ge(sq_done, t.n + 1)
                if t.c >= 4:
                    dve.wait_ge(rms_done, t.n - 3)
                nc.vector.reduce_sum(k_ss[t.slot][:], k_sq[t.c % 2][:], AX_X).then_inc(ss_done, 1)
                dve.wait_ge(ss_done, t.n + 1)
                nc.vector.tensor_scalar_max(k_ms[t.slot][:], k_ss[t.slot][:], RMS_FLOOR ** 2).then_inc(ms_done, 1)

            def step(s, quad):
                if exists(s + -1):
                    split_weights(s + -1)
                if exists(s + 1):
                    split_kv(s + 1)
                if s.c % NT == NT - 1 and s.c > 0:
                    dve.wait_ge(wout_hi, quad + 1)
                    nc.vector.tensor_tensor(wout[:, quad * HQ:(quad + 1) * HQ, 1, :], wout_raw[:],
                                            wout[:, quad * HQ:(quad + 1) * HQ, 0, :].bitcast(F32), ALU.subtract).then_inc(wout_lo, 1)
                if exists(s + -2) and (s.c - 2) % NT == NT - 1:
                    dve.wait_ge(pv_done, s.c - 1)
                    for c in range(2):
                        two = slice(c * 2 * NQ, (c + 1) * 2 * NQ)
                        nc.vector.tensor_copy(attn_out[:, (s.c - 2) // NT, two], o_ps[:, two]).then_inc(out_kept, 1)

            steps(dve, step)

        @block.gpsimd
        def _(pool):
            def sum_weights(t):
                pool.wait_ge(exp_done, t.n * 2 + 2)
                if t.c >= 1:
                    pool.wait_ge(sum_done, t.n)
                total = weight_sum[:, quad_of(t), :]
                nc.gpsimd.tensor_tensor(total, total, probs[t.c % 2][:], ALU.add).then_inc(sum_done, 1)

            def root(t):
                pool.wait_ge(ms_done, t.n + 1)
                if t.c >= 4:
                    pool.wait_ge(exp_done, t.n * 2 - 6)
                nc.gpsimd.tensor_tensor(k_rms[t.slot][:], k_ms[t.slot][:], neg_half[:, 0:HQ], ALU.pow).then_inc(rms_done, 1)
                nc.gpsimd.tensor_copy(bias_now[t.slot][:], score_bias[:, bass.ds((t + -quad_of(t) * NT).n, 1)]).then_inc(bias_done, 1)

            def step(s, quad):
                if exists(s + -1):
                    sum_weights(s + -1)
                if exists(s + 1):
                    root(s + 1)

            steps(pool, step)


def attention_output(nc, sem, a, x_res, ident, attn_out, weight_sum, wout, bout, bout_in, fw, ew):
    RING = 4
    CHUNKS = H * NQ // 512
    with ExitStack() as ctx:
        parts = ctx.enter_context(nc.sbuf_tensor("out_parts", [P, NQUAD, 2, HQ * NQ], F32R))
        sum_hi = ctx.enter_context(nc.sbuf_tensor("sum_hi", [P, 2, HQ * NQ], F32R))
        sum_lo = ctx.enter_context(nc.sbuf_tensor("sum_lo", [P, 2, HQ * NQ], F32R))
        chooser = ctx.enter_context(nc.sbuf_tensor("chooser", [P, CHUNKS, CHUNKS], F32R))
        chooser_f = ctx.enter_context(nc.sbuf_tensor("chooser_f", [P, CHUNKS, CHUNKS], F32))
        sums = ctx.enter_context(nc.sbuf_tensor("sums", [CHUNKS, 512], F32))
        inverse = ctx.enter_context(nc.sbuf_tensor("inverse", [P, 4, CHUNKS], F32))
        sum_ps = ctx.enter_context(nc.psum_tensor("sum_ps", [P, 512], F32))
        column_ps = ctx.enter_context(nc.psum_tensor("column_ps", [P, 4, CHUNKS], F32))
        y_ps = [ctx.enter_context(nc.psum_tensor(f"y_ps{b}", [P, QT, D], F32)) for b in range(RING)]
        chooser_started, chooser_done = sem("chooser_started"), sem("chooser_done")
        sums_hi, sums_lo, sums_used, sums_kept, columns_done, inverse_done = (
            sem("sums_hi"), sem("sums_lo"), sem("sums_used"), sem("sums_kept"), sem("columns_done"), sem("inverse_done"))
        out_hi, out_lo = sem("out_hi"), sem("out_lo")
        y_done, bout_added, y_added = sem("y_done"), sem("bout_added"), sem("y_added")

        block = ctx.enter_context(nc.Block())

        @block.sync
        def _(sp):
            for name, tile in fw.w.items():
                sp.dma_start(tile[:], a["L0_attn_" + name].rearrange("(k p) n -> p k n", p=P)).then_inc(fw.w_in, 16)
            with nc.allow_non_contiguous_dma(reason="a vector onto partitions"):
                for name, tile in fw.columns.items():
                    sp.dma_start(tile[:], a["L0_attn_" + name].rearrange("(k p) -> p k", p=P)).then_inc(fw.bias_in, 16)
            for name, tile in fw.spread.items():
                sp.dma_start(tile[:], a["L0_attn_" + name].partition_broadcast(P)).then_inc(fw.bias_in, 16)
            sp.wait_ge(fw.blocks_zeroed, 1)
            for h in range(H // KD):
                sp.dma_start(fw.proj_bd[DHP * h:DHP * (h + 1), h, :], a["L0_attn_proj"]).then_inc(fw.proj_in, 16)
            for e in range(2):
                sp.dma_start(ew.w1_raw[e][:], a["ffn_W1"][e].rearrange("(k p) f -> p k f", p=P)).then_inc(ew.w1_in[e], 16)
                sp.dma_start(ew.w2_raw[e][:], a["ffn_W2"][e].rearrange("(t p) n -> p t n", p=P)).then_inc(ew.w2_in[e], 16)
            sp.dma_start(ew.b1[:], a["ffn_b1"]).then_inc(ew.b1_in, 16)

        @block.gpsimd
        def _(pool):
            nc.gpsimd.memset(fw.proj_bd[:], 0.0).then_inc(fw.blocks_zeroed, 1)
            nc.gpsimd.memset(fw.diag_bd[:], 0.5 * DHP ** -0.5).then_inc(fw.blocks_started, 1)
            nc.gpsimd.memset(fw.pair_mask[:], 1.0).then_inc(fw.blocks_started, 1)
            for quad in range(NQUAD):
                pool.wait_ge(out_hi, quad + 1)
                nc.gpsimd.tensor_tensor(parts[:, quad, 1, :], attn_out[:, quad, :], parts[:, quad, 0, :].bitcast(F32),
                                        ALU.subtract).then_inc(out_lo, 1)
            pool.wait_ge(fw.blocks_started, 2)
            for n, (tile, pattern, rows) in enumerate(((fw.diag_bd, [[-DHP, H // KD]], DHP), (fw.pair_mask, [[-M, 2], [0, VW]], M))):
                nc.gpsimd.affine_select(out=tile[:], in_=tile[:], compare_op=ALU.is_ge, fill=0.0, base=0,
                                        pattern=pattern, channel_multiplier=1).then_inc(fw.blocks_half, 1)
                pool.wait_ge(fw.blocks_half, 1 + n)
                nc.gpsimd.affine_select(out=tile[:], in_=tile[:], compare_op=ALU.is_ge, fill=0.0, base=rows - 1,
                                        pattern=[[-s, c] for s, c in pattern], channel_multiplier=-1).then_inc(fw.blocks_done, 1)

        @block.scalar
        def _(act):
            def sums_hi_part(quad):
                if quad >= 2:
                    act.wait_ge(sums_used, quad - 1)
                nc.scalar.activation(sum_hi[:, quad % 2, :], weight_sum[:, quad, :], ACT.Copy).then_inc(sums_hi, 1)

            def output_hi(quad):
                nc.scalar.activation(parts[:, quad, 0, :], attn_out[:, quad, :], ACT.Copy).then_inc(out_hi, 1)

            sums_hi_part(0)
            sums_hi_part(1)
            output_hi(0)
            output_hi(1)
            sums_hi_part(2)
            output_hi(2)
            sums_hi_part(3)
            output_hi(3)

        @block.tensor
        def _(pe):
            pe.wait_ge(chooser_done, 1)
            for n in range(CHUNKS):
                quad, at = n // 2, n % 2 * 512
                if n % 2 == 0:
                    pe.wait_ge(sums_lo, quad + 1)
                for s, part in enumerate((sum_hi, sum_lo)):
                    last = nc.tensor.matmul(sum_ps[0:CHUNKS, :], chooser[:, n, :], part[:, quad % 2, at:at + 512],
                                            start=n == 0 and s == 0, stop=n == CHUNKS - 1 and s == 1)
                if n % 2:
                    last.then_inc(sums_used, 1)
            pe.wait_ge(sums_kept, 1)
            for c in range(4):
                last = nc.tensor.transpose(column_ps[:, c, :], sums[:, c * P:(c + 1) * P], ident[0:CHUNKS, 0:CHUNKS])
            last.then_inc(columns_done, 1)
            for h in range(H):
                quad = h // HQ
                if h % HQ == 0:
                    pe.wait_ge(out_lo, quad + 1)
                if h >= RING:
                    pe.wait_ge(y_added, QT * (h - RING + 1))
                for j in range(QT):
                    at = (h % HQ) * NQ + j * P
                    last = part_products(nc, y_ps[h % RING][:, j, :], lambda k, s: parts[:, quad, s, at:at + P],
                                         lambda k, s: wout[:, h, s, :], 1)
                last.then_inc(y_done, 1)

        @block.vector
        def _(dve):
            nc.vector.memset(chooser_f[:], 0.0).then_inc(chooser_started, 1)
            dve.wait_ge(chooser_started, 1)
            nc.vector.memset(chooser_f[:].rearrange("p n m -> p (n m)")[:, 0::CHUNKS + 1], 1.0).then_inc(chooser_started, 1)
            dve.wait_ge(chooser_started, 2)
            nc.vector.tensor_copy(chooser[:], chooser_f[:]).then_inc(chooser_done, 1)
            dve.wait_ge(bout_in, 16)
            nc.vector.tensor_tensor(x_res[:], x_res[:], bout[:].unsqueeze(1).to_broadcast([P, QT, D]), ALU.add).then_inc(bout_added, 1)
            for quad in range(NQUAD):
                dve.wait_ge(sums_hi, quad + 1)
                nc.vector.tensor_tensor(sum_lo[:, quad % 2, :], weight_sum[:, quad, :], sum_hi[:, quad % 2, :].bitcast(F32),
                                        ALU.subtract).then_inc(sums_lo, 1)
            dve.wait_ge(sums_used, NQUAD)
            nc.vector.tensor_copy(sums[:], sum_ps[0:CHUNKS, :]).then_inc(sums_kept, 1)
            dve.wait_ge(columns_done, 1)
            nc.vector.reciprocal(inverse[:], column_ps[:]).then_inc(inverse_done, 1)
            dve.wait_ge(inverse_done, 1)
            dve.wait_ge(bout_added, 1)
            for h in range(H):
                dve.wait_ge(y_done, h + 1)
                for j in range(QT):
                    n = h * QT + j
                    if h:
                        dve.wait_ge(y_added, n - QT + 1)
                    nc.vector.scalar_tensor_tensor(x_res[:, j, :], y_ps[h % RING][:, j, :], inverse[:, h % 2 * QT + j, h // 2:h // 2 + 1],
                                                   x_res[:, j, :], ALU.mult, ALU.add).then_inc(y_added, 1)


def row_norm(nc, dve, own, eps_done, root_done, src, dst, stats, mean_var, var_eps, rstd):
    for j in range(QT):
        last = nc.vector.bn_stats(stats[:, j, :], src[:, j, :])
    last.then_inc(own, 1)
    dve.wait_ge(own, 1)
    for j in range(QT):
        last = nc.vector.bn_aggr(mean_var[:, j, :], stats[:, j, :])
    last.then_inc(own, 1)
    dve.wait_ge(own, 2)
    nc.vector.tensor_scalar_add(var_eps[:], mean_var[:, :, 1], LN_EPS).then_inc(eps_done, 1)
    dve.wait_ge(root_done, 1)
    for j in range(QT):
        last = nc.vector.tensor_scalar(dst[:, j, :], src[:, j, :], mean_var[:, j, 0:1], rstd[:, j:j + 1],
                                       ALU.subtract, ALU.mult)
    return last


def performer(nc, sem, x_res, ident, neg_half, fw, ew):
    HH = H // KD
    with ExitStack() as ctx:
        def sb(name, shape, dt=F32):
            return ctx.enter_context(nc.sbuf_tensor("f_" + name, shape, dt))

        w, columns, spread = fw.w, fw.columns, fw.spread
        stats, mean_var, var_eps, rstd = sb("stats", [P, QT, 6]), sb("mean_var", [P, QT, 2]), sb("var_eps", [P, QT]), sb("rstd", [P, QT])
        z, zt = sb("z", [P, QT, D]), sb("zt", [P, KD, NQ])
        proj_bd, diag_bd, pair_mask = fw.proj_bd, fw.diag_bd, fw.pair_mask
        qk_t = sb("qk_t", [P, 2, KD, 2, NQ], F32R)
        proj_p = sb("proj_p", [P, 2, HH * M], F32R)
        qk_sq = sb("qk_sq", [P, 2, KD, NQ])
        v_one = sb("v_one", [P, QT, H, VW])
        top = sb("top", [P, 2, QT * KD, HH])
        top_key = sb("top_key", [P, 2, H])
        less = sb("less", [P, 2, QT * KD, HH])
        feats = sb("feats", [P, 2, QT, KD * HH * M])
        kv_ctx = sb("kv_ctx", [PAIR, NPAIR, 2 * VW])
        qp_t = sb("qp_t", [PAIR, NPAIR * NQ])
        inverse = sb("inverse", [P, QT, H])
        o, o_t, h_t = sb("o", [P, QT, H, DHP]), sb("o_t", [P, KD, NQ]), sb("h_t", [P, KD, NQ])
        y = sb("y", [P, QT, D])
        ps = ctx.enter_context(nc.psum_tensor("f_ps", [P, 8, 512], F32))

        own, eps_done, root_done, z_done, zt_done, zt_kept = (
            sem("f_own"), sem("f_eps_done"), sem("f_root_done"), sem("f_z_done"), sem("f_zt_done"), sem("f_zt_kept"))
        qk_done, v_done, qk_kept, qk_lo, v_kept, proj_scaled = (
            sem("f_qk_done"), sem("f_v_done"), sem("f_qk_kept"), sem("f_qk_lo"), sem("f_v_kept"), sem("f_proj_scaled"))
        exponents_done, key_top, key_top_all = sem("f_exponents_done"), sem("f_key_top"), sem("f_key_top_all")
        less_done, exp_done, feats_done = sem("f_less_done"), sem("f_exp_done"), sem("f_feats_done")
        context_done, qp_done, context_kept, qp_kept = (
            sem("f_context_done"), sem("f_qp_done"), sem("f_context_kept"), sem("f_qp_kept"))
        o_ready, o_kept, ot_done, ot_kept = sem("f_o_ready"), sem("f_o_kept"), sem("f_ot_done"), sem("f_ot_kept")
        ht_done, ht_kept, fc_done = sem("f_ht_done"), sem("f_ht_kept"), sem("f_fc_done")

        block = ctx.enter_context(nc.Block())

        @block.gpsimd
        def _(pool):
            pool.wait_ge(eps_done, 1)
            nc.gpsimd.tensor_tensor(rstd[:], var_eps[:], neg_half[:, 0:QT], ALU.pow).then_inc(root_done, 1)
            pool.wait_ge(key_top, 1)
            nc.gpsimd.partition_all_reduce(top_key[:, 1, :], top_key[:, 0, :], P, bass.bass_isa.ReduceOp.max).then_inc(key_top_all, 1)
            pool.wait_ge(ew.w1_hi, 1)
            nc.gpsimd.tensor_tensor(ew.w1_first[:, :, 1, :], ew.w1_raw[0][:], ew.w1_first[:, :, 0, :].bitcast(F32),
                                    ALU.subtract).then_inc(ew.w1_lo, 1)

        @block.tensor
        def _(pe):
            pe.wait_ge(z_done, 1)
            for k in range(KD):
                for j in range(QT):
                    last = nc.tensor.transpose(ps[:, k, j * P:(j + 1) * P], z[:, j, k * P:(k + 1) * P], ident[:])
            last.then_inc(zt_done, 1)
            pe.wait_ge(fw.w_in, 16 * len(w))
            pe.wait_ge(zt_kept, 1)
            def transposed(n, name):
                for half in range(KD):
                    for k in range(KD):
                        last = nc.tensor.matmul(ps[:, 4 + 2 * n + half, 0:NQ], w[name][:, k, half * P:(half + 1) * P],
                                                zt[:, k, :], start=k == 0, stop=k == KD - 1)
                    last.then_inc(qk_done, 1)

            transposed(0, "Wq")
            for j in range(QT):
                for k in range(KD):
                    last = nc.tensor.matmul(ps[:, 2 + j, 0:D], zt[:, k, j * P:(j + 1) * P], w["Wv"][:, k, :],
                                            start=k == 0, stop=k == KD - 1)
            last.then_inc(v_done, 1)
            transposed(1, "Wk")
            pe.wait_ge(proj_scaled, 1)
            pe.wait_ge(fw.blocks_done, 2)
            pe.wait_ge(v_kept, 1)
            for n in range(2):
                pe.wait_ge(qk_lo, (n + 1) * KD)
                for j in range(QT):
                    for half in range(KD):
                        bank = ps[:, 4 * n + 2 * j + half]
                        part_products(nc, bank[:, 0:HH * M], lambda k, s: qk_t[:, n, half, s, j * P:(j + 1) * P],
                                      lambda k, s: proj_p[:, s, :], 1)
                        last = nc.tensor.matmul(bank[:, HH * M:HH * M + HH], qk_sq[:, n, half, j * P:(j + 1) * P],
                                                diag_bd[:], start=True, stop=True)
                last.then_inc(exponents_done, 1)
            pe.wait_ge(feats_done, 1)
            for g in range(NPAIR):
                for j in range(QT):
                    at = g * NQ + j * P
                    last = nc.tensor.transpose(ps[0:PAIR, at // 512, at % 512:at % 512 + P],
                                               feats[:, 0, j, g * PAIR:(g + 1) * PAIR], ident[:])
            last.then_inc(qp_done, 1)
            pe.wait_ge(feats_done, 2)
            for g in range(NPAIR):
                for j in range(QT):
                    last = nc.tensor.matmul(ps[0:PAIR, 4, g * 2 * VW:(g + 1) * 2 * VW], feats[:, 1, j, g * PAIR:(g + 1) * PAIR],
                                            v_one[:, j, 2 * g:2 * g + 2, :].rearrange("p h d -> p (h d)"),
                                            start=j == 0, stop=j == QT - 1)
            last.then_inc(context_done, 1)
            pe.wait_ge(context_kept, 1)
            pe.wait_ge(qp_kept, 1)
            for j in range(QT):
                for g in range(NPAIR):
                    last = nc.tensor.matmul(ps[:, 6 + j, g * 2 * VW:(g + 1) * 2 * VW], qp_t[:, g * NQ + j * P:g * NQ + (j + 1) * P],
                                            kv_ctx[:, g, :], start=True, stop=True)
            last.then_inc(o_ready, 1)
            pe.wait_ge(o_kept, 1)
            for k in range(KD):
                for j in range(QT):
                    last = nc.tensor.transpose(ps[:, k, j * P:(j + 1) * P],
                                               o[:, j].rearrange("p h d -> p (h d)")[:, k * P:(k + 1) * P], ident[:])
            last.then_inc(ot_done, 1)
            pe.wait_ge(ot_kept, 1)
            for half in range(KD):
                for k in range(KD):
                    last = nc.tensor.matmul(ps[:, 2 + half, 0:NQ], w["Wo"][:, k, half * P:(half + 1) * P], o_t[:, k, :],
                                            start=k == 0, stop=k == KD - 1)
            last.then_inc(ht_done, 1)
            pe.wait_ge(ht_kept, 1)
            for j in range(QT):
                for k in range(KD):
                    last = nc.tensor.matmul(ps[:, 4 + j, 0:D], h_t[:, k, j * P:(j + 1) * P], w["Wfc"][:, k, :],
                                            start=k == 0, stop=k == KD - 1)
            last.then_inc(fc_done, 1)

        @block.scalar
        def _(act):
            act.wait_ge(ew.w1_in[0], 16)
            nc.scalar.activation(ew.w1_first[:, :, 0, :], ew.w1_raw[0][:], ACT.Copy).then_inc(ew.w1_hi, 1)
            act.wait_ge(ew.w2_in[0], 16)
            nc.scalar.activation(ew.w2_first[:, :, 0, :], ew.w2_raw[0][:], ACT.Copy).then_inc(ew.w2_hi, 1)
            act.wait_ge(fw.bias_in, 16 * 5)
            for n, name in enumerate(("bq", "bk")):
                for half in range(KD):
                    act.wait_ge(qk_done, n * KD + half + 1)
                    nc.scalar.activation(qk_t[:, n, half, 0, :], ps[:, 4 + 2 * n + half, 0:NQ], ACT.Identity,
                                         bias=columns[name][:, half:half + 1])
                    nc.scalar.activation(qk_sq[:, n, half, :], ps[:, 4 + 2 * n + half, 0:NQ], ACT.Square,
                                         bias=columns[name][:, half:half + 1]).then_inc(qk_kept, 1)
            for n in range(2):
                side = feats[:, n].rearrange("p j m -> p (j m)")
                act.wait_ge(less_done, n + 1)
                nc.scalar.activation(side, side, ACT.Exp).then_inc(exp_done, 1)
            act.wait_ge(qp_done, 1)
            nc.scalar.activation(qp_t[:], ps[0:PAIR, 0:4].rearrange("p b n -> p (b n)"), ACT.Copy).then_inc(qp_kept, 1)
            act.wait_ge(ht_done, 1)
            for half in range(KD):
                last = nc.scalar.activation(h_t[:, half, :], ps[:, 2 + half, 0:NQ], ACT.Identity,
                                            bias=columns["bo"][:, half:half + 1])
            last.then_inc(ht_kept, 1)

        @block.vector
        def _(dve):
            row_norm(nc, dve, own, eps_done, root_done, x_res, z, stats, mean_var, var_eps, rstd).then_inc(z_done, 1)
            count = [NORM_LINKS]

            def link(ins):
                count[0] += 1
                ins.then_inc(own, 1)
                dve.wait_ge(own, count[0])

            dve.wait_ge(zt_done, 1)
            nc.vector.tensor_copy(zt[:], ps[:, 0:KD, 0:NQ]).then_inc(zt_kept, 1)
            dve.wait_ge(fw.proj_in, 16 * HH)
            flat = proj_bd[:].rearrange("p h m -> p (h m)")
            link(nc.vector.tensor_scalar_mul(flat, flat, DHP ** -0.25))
            link(nc.vector.tensor_copy(proj_p[:, 0, :], flat))
            nc.vector.tensor_tensor(proj_p[:, 1, :], flat, proj_p[:, 0, :].bitcast(F32), ALU.subtract).then_inc(proj_scaled, 1)
            link(nc.vector.memset(v_one[:], 1.0))
            dve.wait_ge(fw.bias_in, 16 * 5)

            def lo_parts(n, name):
                for half in range(KD):
                    dve.wait_ge(qk_kept, n * KD + half + 1)
                    nc.vector.scalar_tensor_tensor(qk_t[:, n, half, 1, :], ps[:, 4 + 2 * n + half, 0:NQ], columns[name][:, half:half + 1],
                                                   qk_t[:, n, half, 0, :].bitcast(F32), ALU.add, ALU.subtract).then_inc(qk_lo, 1)

            lo_parts(0, "bq")
            dve.wait_ge(v_done, 1)
            for j in range(QT):
                last = nc.vector.tensor_tensor(v_one[:, j, :, 0:DHP], ps[:, 2 + j, 0:D].rearrange("p (h d) -> p h d", d=DHP),
                                               spread["bv"][:].rearrange("p (h d) -> p h d", d=DHP), ALU.add)
            last.then_inc(v_kept, 1)
            lo_parts(1, "bk")

            def exponents(n):
                return ps[:, 4 * n:4 * n + 4, 0:HH * M].rearrange("p b (h m) -> p b h m", m=M)

            def highest(n):
                dve.wait_ge(exponents_done, n + 1)
                return nc.vector.reduce_max(top[:, n], exponents(n), AX_X)

            def subtract(n, most):
                link(nc.vector.tensor_tensor(less[:, n], ps[:, 4 * n:4 * n + 4, HH * M:HH * M + HH], most, ALU.add))
                nc.vector.tensor_tensor(feats[:, n].rearrange("p j (k h m) -> p (j k) h m", k=KD, m=M), exponents(n),
                                        less[:, n].unsqueeze(3).to_broadcast([P, QT * KD, HH, M]), ALU.subtract).then_inc(less_done, 1)

            def finish(n):
                dve.wait_ge(exp_done, n + 1)
                nc.vector.tensor_scalar(feats[:, n], feats[:, n], FEAT_EPS, M ** -0.5, ALU.add, ALU.mult).then_inc(feats_done, 1)

            link(highest(0))
            subtract(0, top[:, 0])
            link(highest(1))
            nc.vector.tensor_tensor(top_key[:, 0, :], top[:, 1, 0:KD].rearrange("p k h -> p (k h)"),
                                    top[:, 1, KD:2 * KD].rearrange("p k h -> p (k h)"), ALU.max).then_inc(key_top, 1)
            finish(0)
            dve.wait_ge(key_top_all, 1)
            for j in range(QT):
                link(nc.vector.tensor_copy(top[:, 1, j * KD:(j + 1) * KD], top_key[:, 1, :].rearrange("p (k h) -> p k h", k=KD)))
            subtract(1, top[:, 1])
            finish(1)
            dve.wait_ge(ew.w2_hi, 1)
            nc.vector.tensor_tensor(ew.w2_first[:, :, 1, :], ew.w2_raw[0][:], ew.w2_first[:, :, 0, :].bitcast(F32),
                                    ALU.subtract).then_inc(ew.w2_lo, 1)
            dve.wait_ge(fw.blocks_done, 2)
            dve.wait_ge(context_done, 1)
            nc.vector.tensor_tensor(kv_ctx[:], ps[0:PAIR, 4, 0:NPAIR * 2 * VW].rearrange("p (g n) -> p g n", g=NPAIR),
                                    pair_mask[:].rearrange("p c n -> p (c n)").unsqueeze(1).to_broadcast([PAIR, NPAIR, 2 * VW]),
                                    ALU.mult).then_inc(context_kept, 1)
            dve.wait_ge(o_ready, 1)
            sums = ps[:, 6:8, 0:H * VW].rearrange("p j (h d) -> p j h d", d=VW)
            link(nc.vector.reciprocal(inverse[:], sums[:, :, :, DHP]))
            for j in range(QT):
                last = nc.vector.tensor_tensor(o[:, j], sums[:, j, :, 0:DHP], inverse[:, j].unsqueeze(2).to_broadcast([P, H, DHP]), ALU.mult)
            last.then_inc(o_kept, 1)
            dve.wait_ge(ot_done, 1)
            nc.vector.tensor_copy(o_t[:], ps[:, 0:KD, 0:NQ]).then_inc(ot_kept, 1)
            dve.wait_ge(fc_done, 1)
            link(nc.vector.tensor_tensor(y[:], ps[:, 4:6, 0:D], spread["bfc"][:].unsqueeze(1).to_broadcast([P, QT, D]), ALU.add))
            for j in range(QT):
                last = nc.vector.scalar_tensor_tensor(x_res[:, j, :], y[:, j, :], 0.0, x_res[:, j, :], ALU.max, ALU.add)
            link(last)


def experts(nc, sem, a, x_res, ident, neg_half, ew):
    E1 = E + 1
    BANKS = FT * NQ // 512
    FB = FT // BANKS
    FH = FT // 2
    with ExitStack() as ctx:
        def sb(name, shape, dt=F32):
            return ctx.enter_context(nc.sbuf_tensor("e_" + name, shape, dt))

        def pair(name, shape, dt=F32):
            return [sb(f"{name}{b}", shape, dt) for b in range(2)]

        w1_raw, w2_raw = ew.w1_raw, ew.w2_raw
        b1 = pair("b1_now", [P, FT])
        w1 = [ew.w1_first, sb("w1_second", [P, KD, 2, F], F32R)]
        w2 = [ew.w2_first, sb("w2_second", [P, FT, 2, D], F32R)]
        b2 = sb("b2", [E1, D])
        wg = sb("wg", [P, KD, E])
        stats, mean_var, var_eps, rstd = sb("stats", [P, QT, 6]), sb("mean_var", [P, QT, 2]), sb("var_eps", [P, QT]), sb("rstd", [P, QT])
        z, zt = sb("z", [P, QT, D]), sb("zt", [P, KD, NQ])
        zp = sb("zp", [P, KD, 2, NQ], F32R)
        logit_top, neg_top = sb("logit_top", [P, QT, 8]), sb("neg_top", [P, QT])
        gate_exp, gate_sum, gate_inv = sb("gate_exp", [P, QT, E]), sb("gate_sum", [P, QT]), sb("gate_inv", [P, QT])
        gate = sb("gate", [P, QT, E])
        best, best_at = sb("best", [P, QT, 8]), sb("best_at", [P, QT, 8], U32)
        best_f, two = sb("best_f", [P, QT, 2]), sb("two", [P, QT, 4])
        number, number_f = sb("number", [P, E], mybir.dt.int32), sb("number_f", [P, E])
        picked = sb("picked", [P, QT, 2, E])
        share = sb("share", [P, QT, E1])
        share_t = sb("share_t", [E1, NQ])
        act_f = sb("act_f", [P, FT, NQ])
        act_p = sb("act_p", [P, 2, FT, NQ], F32R)
        h_ps = ctx.enter_context(nc.psum_tensor("e_h_ps", [P, FT, NQ], F32))
        y_ps = [ctx.enter_context(nc.psum_tensor(f"e_y_ps{b}", [P, QT, D], F32)) for b in range(2)]
        gate_ps = ctx.enter_context(nc.psum_tensor("e_gate_ps", [P, 512], F32))
        bias_ps = ctx.enter_context(nc.psum_tensor("e_bias_ps", [P, QT, D], F32))

        w1_in, w2_in, w1_hi, w1_lo, w2_hi, w2_lo = ew.w1_in, ew.w2_in, ew.w1_hi, ew.w1_lo, ew.w2_hi, ew.w2_lo
        b1_kept, b2_in, wg_in = sem("e_b1_kept"), sem("e_b2_in"), sem("e_wg_in")
        numbered = sem("e_numbered")
        own, eps_done, root_done, z_done, zt_done, zt_kept = (
            sem("e_own"), sem("e_eps_done"), sem("e_root_done"), sem("e_z_done"), sem("e_zt_done"), sem("e_zt_kept"))
        zp_hi, zp_done, logits_done, neg_done, gate_exp_done = (
            sem("e_zp_hi"), sem("e_zp_done"), sem("e_logits_done"), sem("e_neg_done"), sem("e_gate_exp_done"))
        share_done, share_t_done, share_t_kept, bias_done = (
            sem("e_share_done"), sem("e_share_t_done"), sem("e_share_t_kept"), sem("e_bias_done"))
        up_done, silu_done, act_hi, act_lo, down_done, added = (
            sem("e_up_done"), sem("e_silu_done"), sem("e_act_hi"), sem("e_act_lo"), sem("e_down_done"), sem("e_added"))

        block = ctx.enter_context(nc.Block())

        @block.sync
        def _(sp):
            sp.dma_start(wg[:], a["L0_ffn_Wg"].rearrange("(k p) e -> p k e", p=P)).then_inc(wg_in, 16)
            sp.dma_start(b2[:], a["ffn_b2"]).then_inc(b2_in, 16)

            def load(t):
                e = bass.ds(t.n, 1)
                sp.wait_ge(w1_lo, t.n - 1)
                sp.dma_start(w1_raw[t.slot][:], a["ffn_W1"][e].rearrange("e (k p) f -> p (e k) f", p=P)).then_inc(w1_in[t.slot], 16)
                sp.wait_ge(w2_lo, t.n - 1)
                sp.dma_start(w2_raw[t.slot][:], a["ffn_W2"][e].rearrange("e (t p) n -> p (e t) n", p=P)).then_inc(w2_in[t.slot], 16)

            run(sp, load, 2, E1, 2)

        @block.gpsimd
        def _(pool):
            nc.gpsimd.iota(number[:], [[1, E]], base=0, channel_multiplier=0).then_inc(numbered, 1)
            pool.wait_ge(eps_done, 1)
            nc.gpsimd.tensor_tensor(rstd[:], var_eps[:], neg_half[:, 0:QT], ALU.pow).then_inc(root_done, 1)

            def lo1(t):
                pool.wait_ge(w1_hi, t.n + 1)
                nc.gpsimd.tensor_tensor(w1[t.slot][:, :, 1, :], w1_raw[t.slot][:], w1[t.slot][:, :, 0, :].bitcast(F32),
                                        ALU.subtract).then_inc(w1_lo, 1)
                biases(t)

            def biases(t):
                nc.gpsimd.tensor_copy(b1[t.slot][:], ew.b1[:, bass.ds(t.n, 1), :].rearrange("p e f -> p (e f)")).then_inc(b1_kept, 1)

            pool.wait_ge(ew.b1_in, 16)
            biases(Turn(0, 2))
            run(pool, lo1, 1, E1, 2)

        @block.tensor
        def _(pe):
            pe.wait_ge(z_done, 1)
            for k in range(KD):
                for j in range(QT):
                    last = nc.tensor.transpose(y_ps[0][:, k, j * P:(j + 1) * P], z[:, j, k * P:(k + 1) * P], ident[:])
            last.then_inc(zt_done, 1)
            pe.wait_ge(zt_kept, 1)
            pe.wait_ge(wg_in, 16)
            for j in range(QT):
                for k in range(KD):
                    last = nc.tensor.matmul(gate_ps[:, j * E:(j + 1) * E], zt[:, k, j * P:(j + 1) * P], wg[:, k, :],
                                            start=k == 0, stop=k == KD - 1)
            last.then_inc(logits_done, 1)
            pe.wait_ge(zp_done, 1)

            def up(t):
                pe.wait_ge(w1_lo, t.n + 1)
                for b in range(BANKS):
                    if t.c >= 1:
                        pe.wait_ge(silu_done, t.n * BANKS + (b + 1 - BANKS))
                    for f in range(b * FB, (b + 1) * FB):
                        last = part_products(nc, h_ps[:, f, :], lambda k, s: w1[t.slot][:, k, s, f * P:(f + 1) * P],
                                             lambda k, s: zp[:, k, s, :])
                    last.then_inc(up_done, 1)

            def down(t):
                b = t.slot
                pe.wait_ge(w2_lo, t.n + 1)
                if t.c >= 2:
                    pe.wait_ge(added, t.n - 1)
                for half in range(2):
                    pe.wait_ge(act_lo, t.n * 2 + (1 + half))
                    terms = [(f, s, m) for f in range(half * FH, (half + 1) * FH) for s, m in ((0, 0), (0, 1), (1, 0))]
                    for j in range(QT):
                        for n, (f, s, m) in enumerate(terms):
                            last = nc.tensor.matmul(y_ps[b][:, j, :], act_p[:, s, f, j * P:(j + 1) * P], w2[b][:, f, m, :],
                                                    start=half == 0 and j == 0 and n == 0,
                                                    stop=half == 1 and n == len(terms) - 1, skip_group_check=True)
                    last.then_inc(down_done, 1)

            def turn(t):
                up(t)
                down(t + -1)

            up(Turn(0, 2))
            pe.wait_ge(share_done, 1)
            for j in range(QT):
                last = nc.tensor.transpose(bias_ps[0:E1, j, 0:P], share[:, j, :], ident[:])
            last.then_inc(share_t_done, 1)
            up(Turn(1, 2))
            pe.wait_ge(share_t_kept, 1)
            pe.wait_ge(b2_in, 16)
            for j in range(QT):
                last = nc.tensor.matmul(bias_ps[:, j, :], share_t[:, j * P:(j + 1) * P], b2[:], start=True, stop=True)
            last.then_inc(bias_done, 1)
            down(Turn(0, 2))
            run(pe, turn, 2, E1, 2)
            down(Turn(E1 - 1, 2))

        @block.scalar
        def _(act):
            def hi1(t):
                act.wait_ge(w1_in[t.slot], (t.lap + 1) * 16)
                if t.c >= 2:
                    act.wait_ge(up_done, (t.n - 1) * BANKS)
                nc.scalar.activation(w1[t.slot][:, :, 0, :], w1_raw[t.slot][:], ACT.Copy).then_inc(w1_hi, 1)

            def hi2(t):
                act.wait_ge(w2_in[t.slot], (t.lap + 1) * 16)
                if t.c >= 2:
                    act.wait_ge(down_done, (t.n - 1) * 2)
                nc.scalar.activation(w2[t.slot][:, :, 0, :], w2_raw[t.slot][:], ACT.Copy).then_inc(w2_hi, 1)

            def silu(t):
                act.wait_ge(b1_kept, t.n + 1)
                for b in range(BANKS):
                    act.wait_ge(up_done, t.n * BANKS + (b + 1))
                    if t.c >= 1 and b % (BANKS // 2) == 0:
                        act.wait_ge(act_lo, t.n * 2 + (b // (BANKS // 2) - 1))
                    for f in range(b * FB, (b + 1) * FB):
                        last = nc.scalar.activation(act_f[:, f, :], h_ps[:, f, :], ACT.Silu, bias=b1[t.slot][:, f:f + 1])
                    last.then_inc(silu_done, 1)

            def turn(t):
                hi1(t + 1)
                silu(t)
                hi2(t + 1)

            hi1(Turn(1, 2))
            act.wait_ge(zt_kept, 1)
            nc.scalar.activation(zp[:, :, 0, :], zt[:], ACT.Copy).then_inc(zp_hi, 1)
            act.wait_ge(neg_done, 1)
            for j in range(QT):
                last = nc.scalar.activation(gate_exp[:, j, :], gate_ps[:, j * E:(j + 1) * E], ACT.Exp,
                                            bias=neg_top[:, j:j + 1], accum_out=gate_sum[:, j:j + 1])
            last.then_inc(gate_exp_done, 1)
            silu(Turn(0, 2))
            hi2(Turn(1, 2))
            run(act, turn, 1, E1 - 1, 2)
            silu(Turn(E1 - 1, 2))

        @block.vector
        def _(dve):
            row_norm(nc, dve, own, eps_done, root_done, x_res, z, stats, mean_var, var_eps, rstd).then_inc(z_done, 1)
            count = [NORM_LINKS]

            def link(ins):
                count[0] += 1
                ins.then_inc(own, 1)
                dve.wait_ge(own, count[0])

            def lo2(t):
                dve.wait_ge(w2_hi, t.n + 1)
                nc.vector.tensor_tensor(w2[t.slot][:, :, 1, :], w2_raw[t.slot][:], w2[t.slot][:, :, 0, :].bitcast(F32), ALU.subtract).then_inc(w2_lo, 1)

            def split_act(t):
                for half in range(2):
                    tiles = slice(half * FH, (half + 1) * FH)
                    dve.wait_ge(silu_done, t.n * BANKS + (half + 1) * (BANKS // 2))
                    if t.c >= 1:
                        dve.wait_ge(down_done, t.n * 2 + (half - 1))
                    nc.vector.tensor_copy(act_p[:, 0, tiles], act_f[:, tiles]).then_inc(act_hi, 1)
                    dve.wait_ge(act_hi, t.n * 2 + (1 + half))
                    nc.vector.tensor_tensor(act_p[:, 1, tiles], act_f[:, tiles], act_p[:, 0, tiles].bitcast(F32), ALU.subtract).then_inc(act_lo, 1)

            def add(t):
                dve.wait_ge(down_done, t.n * 2 + 2)
                if t.c >= 1:
                    dve.wait_ge(added, t.n)
                for j in range(QT):
                    last = nc.vector.scalar_tensor_tensor(x_res[:, j, :], y_ps[t.slot][:, j, :], share[:, j, bass.ds(t.n, 1)],
                                                          x_res[:, j, :], ALU.mult, ALU.add)
                last.then_inc(added, 1)

            def turn(t):
                split_act(t)
                add(t + -1)
                lo2(t + 1)

            dve.wait_ge(zt_done, 1)
            nc.vector.tensor_copy(zt[:], y_ps[0][:]).then_inc(zt_kept, 1)
            dve.wait_ge(zt_kept, 1)
            dve.wait_ge(zp_hi, 1)
            nc.vector.tensor_tensor(zp[:, :, 1, :], zt[:], zp[:, :, 0, :].bitcast(F32), ALU.subtract).then_inc(zp_done, 1)
            dve.wait_ge(logits_done, 1)
            for j in range(QT):
                link(nc.vector.max(logit_top[:, j, :], gate_ps[:, j * E:(j + 1) * E]))
            nc.vector.tensor_scalar_mul(neg_top[:], logit_top[:, :, 0], -1.0).then_inc(neg_done, 1)
            dve.wait_ge(numbered, 1)
            link(nc.vector.tensor_copy(number_f[:], number[:]))
            dve.wait_ge(gate_exp_done, 1)
            link(nc.vector.reciprocal(gate_inv[:], gate_sum[:]))
            for j in range(QT):
                link(nc.vector.tensor_scalar(gate[:, j, :], gate_exp[:, j, :], gate_inv[:, j:j + 1], None, ALU.mult))
                link(nc.vector.max(best[:, j, :], gate[:, j, :]))
                link(nc.vector.max_index(best_at[:, j, :], best[:, j, :], gate[:, j, :]))
            link(nc.vector.tensor_copy(best_f[:], best_at[:, :, 0:2]))
            link(nc.vector.tensor_tensor(two[:, :, 0], best[:, :, 0], best[:, :, 1], ALU.add))
            link(nc.vector.tensor_scalar_add(two[:, :, 0], two[:, :, 0], TOP_EPS))
            link(nc.vector.reciprocal(two[:, :, 1], two[:, :, 0]))
            link(nc.vector.memset(share[:], SHARED))
            for j in range(QT):
                link(nc.vector.tensor_scalar(two[:, j, 2:4], best[:, j, 0:2], two[:, j, 1:2], None, ALU.mult))
                for c in range(2):
                    link(nc.vector.tensor_scalar(picked[:, j, c, :], number_f[:], best_f[:, j, c:c + 1],
                                                 two[:, j, 2 + c:3 + c], ALU.is_equal, ALU.mult))
                last = nc.vector.tensor_tensor(share[:, j, 0:E], picked[:, j, 0, :], picked[:, j, 1, :], ALU.add)
            last.then_inc(share_done, 1)
            dve.wait_ge(share_t_done, 1)
            nc.vector.tensor_copy(share_t[:].rearrange("e (j n) -> e j n", j=QT), bias_ps[0:E1, :, 0:P]).then_inc(share_t_kept, 1)
            split_act(Turn(0, 2))
            lo2(Turn(1, 2))
            dve.wait_ge(bias_done, 1)
            link(nc.vector.tensor_tensor(x_res[:], x_res[:], bias_ps[:], ALU.add))
            run(dve, turn, 1, E1 - 1, 2)
            split_act(Turn(E1 - 1, 2))
            add(Turn(E1 - 2, 2))
            add(Turn(E1 - 1, 2))


def store_result(nc, sem, out, x_res):
    with ExitStack() as ctx:
        stored = sem("stored")
        block = ctx.enter_context(nc.Block())

        @block.sync
        def _(sp):
            sp.dma_start(out.rearrange("o (j p) d -> p (o j) d", p=P), x_res[:]).then_inc(stored, 16)
            sp.wait_ge(stored, 16)


def kernel(**inputs):
    import numpy as np
    import concourse.bacc as bacc
    from concourse.bass_utils import run_bass_kernel_spmd

    arrays = laid_out(np, inputs)
    nc = bacc.Bacc("TRN2", target_bir_lowering=False, num_devices=1)
    aps = {name: nc.dram_tensor("in_" + name, x.shape, mybir.dt.from_np(x.dtype), kind="ExternalInput").ap()
           for name, x in arrays.items()}
    out = nc.dram_tensor("out", (1, NQ, D), F32, kind="ExternalOutput").ap()
    perceiver_kernel(nc, aps, out)
    result = run_bass_kernel_spmd(nc, [{"in_" + name: x for name, x in arrays.items()}], core_ids=[0])
    return result.results[0]["out"]


def laid_out(np, inputs):
    arrays = {name: np.ascontiguousarray(x) for name, x in inputs.items()}
    arrays["mask_BxS2_bf1"] = np.ascontiguousarray(arrays["mask_BxS2_bf1"].reshape(CT, P).T)
    for name in ("Wq", "Wk", "Wv", "Wo", "Wfc", "proj"):
        arrays["L0_attn_" + name] = np.ascontiguousarray(arrays["L0_attn_" + name].T)
    for name in ("W1", "b1", "W2", "b2"):
        own, shared = arrays.pop("L0_ffn_" + name), arrays.pop(f"L0_ffn_{name[0]}s{name[1]}")
        arrays["ffn_" + name] = np.concatenate([own, shared[None]])
    arrays["ffn_b1"] = np.ascontiguousarray(arrays["ffn_b1"].reshape(E + 1, FT, P).transpose(2, 0, 1))
    return arrays
```
